# Optimizing a Trainium2 kernel written in Bass

```python
import numpy as np
import jax
import jax.numpy as jnp

def _softmax(x, axis=-1):
    return jax.nn.softmax(x, axis=axis)

def _gelu(x):
    return jax.nn.gelu(x, approximate=True)

def _silu(x):
    return jax.nn.silu(x)

def _sigmoid(x):
    return jax.nn.sigmoid(x)

def _layernorm(x, axis=-1, eps=1e-05):
    m = jnp.mean(x, axis=axis, keepdims=True)
    v = jnp.var(x, axis=axis, keepdims=True)
    return (x - m) / jnp.sqrt(v + eps)

def _scatter_add(tgt, idx, src, axis=0):
    return tgt.at[idx].add(src)

def _segment_sum(src, seg, n):
    return jax.ops.segment_sum(src, seg, n)
kernel_name = 'mk_recurrent_d4_jaxref_r8_87f695'

def setup_inputs(seed: int=0):
    np.random.seed(seed)
    _w = jnp.asarray

    def _L0_attn_setup():
        import jax, jax.numpy as jnp
        import numpy as np
        D_MODEL = 128
        NHEAD = 16
        HEAD_DIM = D_MODEL // NHEAD
        ROTARY_DIM = HEAD_DIM
        D_INNER = 2 * D_MODEL
        HEADDIM = 64
        H_SSM = D_INNER // HEADDIM
        D_STATE = 128
        D_CONV = 4
        CHUNK = 32
        CONV_DIM = D_INNER + 2 * D_STATE
        D_IN_PROJ = 2 * D_INNER + 2 * D_STATE + H_SSM
        EPS = 1e-05

        def rmsnorm(x, w):
            var = jnp.mean(x * x, axis=-1, keepdims=True)
            return x * jax.lax.rsqrt(var + EPS) * w

        def apply_rope(q):
            T = q.shape[1]
            half = ROTARY_DIM // 2
            inv_freq = 1.0 / 10000.0 ** (jnp.arange(0, ROTARY_DIM, 2, dtype=jnp.float32) / ROTARY_DIM)
            freqs = jnp.arange(T, dtype=jnp.float32)[:, None] * inv_freq[None, :]
            cos = jnp.cos(freqs)[None, :, None, :]
            sin = jnp.sin(freqs)[None, :, None, :]
            q1 = q[..., :half]
            q2 = q[..., half:ROTARY_DIM]
            rest = q[..., ROTARY_DIM:]
            return jnp.concatenate([q1 * cos - q2 * sin, q2 * cos + q1 * sin, rest], axis=-1)

        def segsum(x):
            T = x.shape[-1]
            xc = jnp.cumsum(x, axis=-1)
            ss = xc[..., :, None] - xc[..., None, :]
            mask = jnp.tril(jnp.ones((T, T), dtype=bool))
            return jnp.where(mask, ss, -jnp.inf)

        def ssd(x, dt, A, Bm, Cm):
            b, l, h, p = x.shape
            n = Bm.shape[-1]
            c = l // CHUNK
            xdt = (x * dt[..., None]).reshape(b, c, CHUNK, h, p)
            Adt = (dt * A).reshape(b, c, CHUNK, h).transpose(0, 3, 1, 2)
            Br = Bm.reshape(b, c, CHUNK, n)
            Cr = Cm.reshape(b, c, CHUNK, n)
            Acs = jnp.cumsum(Adt, axis=-1)
            Lmat = jnp.exp(segsum(Adt))
            Y_diag = jnp.einsum('bcln,bcsn,bhcls,bcshp->bclhp', Cr, Br, Lmat, xdt)
            decay_states = jnp.exp(Acs[..., -1:] - Acs)
            states = jnp.einsum('bcln,bhcl,bclhp->bchpn', Br, decay_states, xdt)
            A_chunk = jnp.pad(Acs[..., -1], ((0, 0), (0, 0), (1, 0)))
            decay_chunk = jnp.exp(segsum(A_chunk))
            states = jnp.concatenate([jnp.zeros_like(states[:, :1]), states], axis=1)
            new_states = jnp.einsum('bhzc,bchpn->bzhpn', decay_chunk, states)
            states_prev = new_states[:, :-1]
            Y_off = jnp.einsum('bcln,bchpn,bhcl->bclhp', Cr, states_prev, jnp.exp(Acs))
            return (Y_diag + Y_off).reshape(b, l, h, p)
        key = jax.random.key(seed)
        ks = jax.random.split(key, 8)
        B, T = (2, 256)
        return {'x': jax.random.normal(ks[0], (B, T, D_MODEL), dtype=jnp.float32), 'W_in': jax.random.normal(ks[1], (3 * D_MODEL, D_MODEL), dtype=jnp.float32) * 0.02, 'W_zxbcdt': jax.random.normal(ks[2], (D_IN_PROJ, D_MODEL), dtype=jnp.float32) * 0.02, 'conv_w': jax.random.normal(ks[3], (CONV_DIM, D_CONV), dtype=jnp.float32) * 0.2, 'conv_b': jnp.zeros((CONV_DIM,), dtype=jnp.float32), 'dt_bias': jax.random.normal(ks[4], (H_SSM,), dtype=jnp.float32) * 0.5, 'A_log': jax.random.normal(ks[5], (H_SSM,), dtype=jnp.float32) * 0.5, 'D_param': jax.random.normal(ks[6], (H_SSM,), dtype=jnp.float32), 'norm_pre_w': jnp.ones((D_MODEL,), dtype=jnp.float32), 'norm_gated_w': jnp.ones((D_INNER,), dtype=jnp.float32), 'W_out': jax.random.normal(ks[7], (D_MODEL, D_INNER), dtype=jnp.float32) * 0.02}
    _L0_attn_in = _L0_attn_setup()

    def _L0_ffn_setup():
        import jax, jax.numpy as jnp
        import numpy as np
        BLOCK = 16
        _GRID = jnp.array([0.0, 0.5, 1.0, 1.5, 2.0, 3.0, 4.0, 6.0], dtype=jnp.float32)
        _MID = jnp.array([0.25, 0.75, 1.25, 1.75, 2.5, 3.5, 5.0], dtype=jnp.float32)

        def fp4_quant_dequant(x):
            shape = x.shape
            xb = x.reshape(shape[:-1] + (shape[-1] // BLOCK, BLOCK))
            scale = jnp.max(jnp.abs(xb), axis=-1, keepdims=True) / 6.0
            scale = jnp.maximum(scale, jnp.float32(1e-12))
            xn = xb / scale
            idx = jnp.searchsorted(_MID, jnp.abs(xn))
            q = _GRID[idx] * jnp.sign(xn) * scale
            return q.reshape(shape)

        def fp4_linear(x, w):
            xq = fp4_quant_dequant(x)
            wq = fp4_quant_dequant(w)
            return jnp.einsum('bsk,nk->bsn', xq, wq)
        key = jax.random.key(seed)
        k1, k2, k3, k4 = jax.random.split(key, 4)
        H, I = (128, 352)
        x = jax.random.normal(k1, (4, 512, H), dtype=jnp.float32)
        w_gate = jax.random.normal(k2, (I, H), dtype=jnp.float32) * 0.02
        w_up = jax.random.normal(k3, (I, H), dtype=jnp.float32) * 0.02
        w_down = jax.random.normal(k4, (H, I), dtype=jnp.float32) * 0.02
        return {'x': x, 'w_gate': w_gate, 'w_up': w_up, 'w_down': w_down}
    _L0_ffn_in = _L0_ffn_setup()

    def _L1_attn_setup():
        import jax, jax.numpy as jnp
        import numpy as np
        EMBED = 128
        HEADS = 16
        PER_DIM = EMBED // HEADS
        C, T = (64, 128)

        def entmax15(x, axis=-1):
            x = x / 2.0
            x = x - jnp.max(x, axis=axis, keepdims=True)
            xs = -jnp.sort(-x, axis=axis)
            n = x.shape[axis]
            k = jnp.arange(1, n + 1, dtype=x.dtype)
            cum = jnp.cumsum(xs, axis=axis)
            cumsq = jnp.cumsum(xs * xs, axis=axis)
            mean = cum / k
            ss = cumsq - cum * mean
            delta = jnp.clip((1.0 - ss) / k, 0.0)
            tau = mean - jnp.sqrt(delta)
            k_star = jnp.sum((tau <= xs).astype(jnp.int32), axis=axis, keepdims=True) - 1
            tau_star = jnp.take_along_axis(tau, k_star, axis=axis)
            return jnp.square(jnp.clip(x - tau_star, 0.0))
        key = jax.random.key(seed)
        ks = jax.random.split(key, 7)
        s = 1.0 / np.sqrt(PER_DIM)
        return {'y_de': jax.random.normal(ks[0], (C, T, EMBED), dtype=jnp.float32), 'Wq': jax.random.normal(ks[1], (PER_DIM, PER_DIM), dtype=jnp.float32) * s, 'bq': jax.random.normal(ks[2], (PER_DIM,), dtype=jnp.float32) * s, 'Wk': jax.random.normal(ks[3], (PER_DIM, PER_DIM), dtype=jnp.float32) * s, 'bk': jax.random.normal(ks[4], (PER_DIM,), dtype=jnp.float32) * s, 'Wv': jax.random.normal(ks[5], (PER_DIM, PER_DIM), dtype=jnp.float32) * s, 'bv': jax.random.normal(ks[6], (PER_DIM,), dtype=jnp.float32) * s}
    _L1_attn_in = _L1_attn_setup()

    def _L1_ffn_setup():
        import jax, jax.numpy as jnp
        import numpy as np
        B, S, H, F, E, K = (2, 128, 128, 256, 8, 2)
        key = jax.random.key(seed)
        ks = jax.random.split(key, 5)
        scale_h = 1.0 / np.sqrt(H)
        scale_f = 1.0 / np.sqrt(F)
        return {'inputs': jax.random.normal(ks[0], (B, S, H), dtype=jnp.float32), 'router_w': jax.random.normal(ks[1], (H, E), dtype=jnp.float32) * scale_h, 'w1': jax.random.normal(ks[2], (E, H, F), dtype=jnp.float32) * scale_h, 'w3': jax.random.normal(ks[3], (E, H, F), dtype=jnp.float32) * scale_h, 'w2': jax.random.normal(ks[4], (E, F, H), dtype=jnp.float32) * scale_f}
    _L1_ffn_in = _L1_ffn_setup()

    def _L2_attn_setup():
        import jax, jax.numpy as jnp
        import numpy as np
        B, L, DM, DI, H = (4, 256, 128, 256, 16)
        HD = DI // H
        KS = 4
        ROPE_BASE = 10000.0
        GATING_C = 8.0
        EPS_NORM = 1e-06
        EPS_DT = 0.0001
        GN_GROUPS = 16
        GN_EPS = 1e-05

        def _rms_norm(x, w):
            v = jnp.mean(x * x, axis=-1, keepdims=True)
            return x * jax.lax.rsqrt(v + EPS_NORM) * w

        def _conv_silu(x, w, b):
            k = w.shape[1]
            xp = jnp.pad(x, ((0, 0), (k - 1, 0), (0, 0)))
            y = b
            for j in range(k):
                y = y + xp[:, j:j + x.shape[1], :] * w[:, j]
            return y * jax.nn.sigmoid(y)

        def _forward(x, rms_w, in_proj_w, in_proj_b, conv_w, conv_b, gate_w, gate_b, log_dt_scale, Q_w, readout_w, out_w, gn_w, gn_b, D_param):
            b, l, _ = x.shape
            di = conv_w.shape[0]
            h = log_dt_scale.shape[0]
            hd = di // h
            residual = x
            xn = _rms_norm(x, rms_w)
            proj = xn @ in_proj_w + in_proj_b
            z = proj[..., :di]
            x_gate = proj[..., di:2 * di]
            K = proj[..., 2 * di:3 * di].reshape(b, l, h, hd)
            V = proj[..., 3 * di:].reshape(b, l, h, 2)
            x_conv = _conv_silu(x_gate, conv_w, conv_b)
            gates = (x_conv @ gate_w + gate_b).reshape(b, l, 7, h)
            alpha_raw, omega_raw = (gates[..., 0, :], gates[..., 1, :])
            sel_B, sel_C = (gates[..., 2, :], gates[..., 3, :])
            sel_dt, beta_raw, r_raw = (gates[..., 4, :], gates[..., 5, :], gates[..., 6, :])
            freqs = 1.0 / ROPE_BASE ** (jnp.arange(h, dtype=jnp.float32) / h)
            dt = jax.nn.softplus(sel_dt) * jnp.exp(log_dt_scale) + EPS_DT
            alpha = jax.nn.softplus(alpha_raw)
            omega = freqs * (1.0 + jnp.tanh(omega_raw))
            ah, wh = (0.5 * dt * alpha, 0.5 * dt * omega)
            det = (1.0 + ah) ** 2 + wh ** 2
            c = (1.0 - ah ** 2 - wh ** 2) / det
            s = 2.0 * wh / det
            mag = jnp.sqrt(c * c + s * s)
            theta = jnp.arctan2(s, c)
            r = jax.nn.sigmoid(r_raw)
            mag2 = jnp.exp(GATING_C * r * jnp.log(jnp.clip(mag, 1e-08, 1.0)))
            cbar, sbar = (mag2 * jnp.cos(theta), mag2 * jnp.sin(theta))
            vp_scale = jax.nn.sigmoid(sel_B) * jnp.sqrt(jnp.clip(1.0 - mag2 ** 2, 0.0, 1.0) + 1e-06)
            beta = jax.nn.sigmoid(beta_raw)
            sel_C_gate = jax.nn.sigmoid(sel_C)
            Q = (x_conv @ Q_w).reshape(b, l, h, hd)
            K = K / (jnp.linalg.norm(K, axis=-1, keepdims=True) + 1e-06)
            Q = Q / (jnp.linalg.norm(Q, axis=-1, keepdims=True) + 1e-06)
            Vg = V * vp_scale[..., None]

            def step(S, inp):
                ct, st, kt, vt, bt = inp
                S0, S1 = (S[:, :, 0], S[:, :, 1])
                Sd = jnp.stack([ct[..., None] * S0 + st[..., None] * S1, -st[..., None] * S0 + ct[..., None] * S1], axis=2)
                pred = jnp.einsum('bhsd,bhd->bhs', Sd, kt)
                Sn = Sd + bt[:, :, None, None] * (vt - pred)[..., None] * kt[:, :, None, :]
                return (Sn, Sn)
            xs = (jnp.moveaxis(cbar, 1, 0), jnp.moveaxis(sbar, 1, 0), jnp.moveaxis(K, 1, 0), jnp.moveaxis(Vg, 1, 0), jnp.moveaxis(beta, 1, 0))
            S0 = jnp.zeros((b, h, 2, hd), dtype=x.dtype)
            _, Ys = jax.lax.scan(step, S0, xs)
            Y = jnp.moveaxis(Ys, 0, 1)
            retrieved = jnp.einsum('blhsd,blhd->blhs', Y, Q) * sel_C_gate[..., None]
            y = retrieved.reshape(b, l, h * 2) @ readout_w
            yf = y.astype(jnp.float32).reshape(b, l, GN_GROUPS, di // GN_GROUPS)
            mean = jnp.mean(yf, axis=(1, 3), keepdims=True)
            var = jnp.mean((yf - mean) ** 2, axis=(1, 3), keepdims=True)
            yn = ((yf - mean) * jax.lax.rsqrt(var + GN_EPS)).reshape(b, l, di)
            y = (yn * gn_w + gn_b).astype(x.dtype)
            y = y * (z * jax.nn.sigmoid(z))
            y = y + D_param * x_conv
            out = y @ out_w
            return residual + out
        key = jax.random.key(seed)
        ks = jax.random.split(key, 16)
        in_sz = 3 * DI + 2 * H
        gate_b = jnp.concatenate([jnp.zeros(2 * H), jnp.full((H,), 1.0), jnp.full((H,), 1.0), jnp.full((H,), -4.0), jnp.zeros(H), jnp.full((H,), -2.0)])
        return {'x': jax.random.normal(ks[0], (B, L, DM), jnp.float32), 'rms_w': jnp.ones((DM,), jnp.float32), 'in_proj_w': jax.random.normal(ks[1], (DM, in_sz), jnp.float32) / np.sqrt(DM), 'in_proj_b': jnp.zeros((in_sz,), jnp.float32), 'conv_w': jax.random.normal(ks[2], (DI, KS), jnp.float32) / np.sqrt(KS), 'conv_b': jnp.zeros((DI,), jnp.float32), 'gate_w': jax.random.normal(ks[3], (DI, 7 * H), jnp.float32) / np.sqrt(DI), 'gate_b': gate_b.astype(jnp.float32), 'log_dt_scale': 0.1 * jax.random.normal(ks[4], (H,), jnp.float32), 'Q_w': jnp.eye(DI, dtype=jnp.float32), 'readout_w': jax.random.normal(ks[5], (2 * H, DI), jnp.float32) / np.sqrt(2 * H), 'out_w': jax.random.normal(ks[6], (DI, DM), jnp.float32) / np.sqrt(DI), 'gn_w': jnp.ones((DI,), jnp.float32) + 0.1 * jax.random.normal(ks[7], (DI,), jnp.float32), 'gn_b': 0.1 * jax.random.normal(ks[8], (DI,), jnp.float32), 'D_param': 0.1 * jax.random.normal(ks[9], (DI,), jnp.float32)}
    _L2_attn_in = _L2_attn_setup()

    def _L2_ffn_setup():
        import jax, jax.numpy as jnp
        import numpy as np
        BS, SLEN, DIM = (1, 256, 128)
        NUM_EXPERTS, TOP_K = (8, 2)
        HID = 176

        def _masked_grouped_mm(x, w, onehot):
            g = jnp.einsum('tk,gnk->tgn', x, w, preferred_element_type=jnp.float32)
            return jnp.einsum('tgn,tg->tn', g, onehot)

        def moe_forward(x, gate_w, expert_bias, w_up, w_down, shared_w_up, shared_w_down):
            bs, slen, dim = x.shape
            xf = x.reshape(-1, dim)
            scores = jax.nn.sigmoid((xf @ gate_w.T).astype(jnp.float32))
            biased = scores + expert_bias
            _, sel = jax.lax.top_k(biased, TOP_K)
            top_scores = jnp.take_along_axis(scores, sel, axis=-1)
            flat_sel = sel.reshape(-1)
            counts = jnp.bincount(flat_sel, length=NUM_EXPERTS)
            order = jnp.argsort(flat_sel, stable=True)
            scores_sorted = top_scores.reshape(-1)[order]
            token_ids = order // TOP_K
            routed_in = (xf[token_ids] * scores_sorted[:, None]).astype(x.dtype)
            seg = jnp.repeat(jnp.arange(NUM_EXPERTS), counts, total_repeat_length=flat_sel.shape[0])
            onehot = jax.nn.one_hot(seg, NUM_EXPERTS, dtype=jnp.float32)
            h = _masked_grouped_mm(routed_in.astype(jnp.bfloat16), w_up.astype(jnp.bfloat16), onehot)
            h = jnp.square(jax.nn.relu(h.astype(jnp.bfloat16)))
            routed_out = _masked_grouped_mm(h.astype(jnp.bfloat16), w_down.astype(jnp.bfloat16), onehot)
            routed_out = routed_out.astype(jnp.bfloat16).astype(x.dtype)
            hs = jnp.square(jax.nn.relu(xf @ shared_w_up.T))
            shared_out = hs @ shared_w_down.T
            combined = jnp.zeros((flat_sel.shape[0], dim), routed_out.dtype).at[order].set(routed_out)
            out = combined.reshape(-1, TOP_K, dim).sum(axis=1) + shared_out
            return out.reshape(bs, slen, dim)
        key = jax.random.key(seed)
        k = jax.random.split(key, 6)
        s = 0.02
        return {'x': jax.random.normal(k[0], (BS, SLEN, DIM), jnp.float32), 'gate_w': jax.random.normal(k[1], (NUM_EXPERTS, DIM), jnp.float32) * s, 'expert_bias': jnp.zeros((NUM_EXPERTS,), jnp.float32), 'w_up': jax.random.normal(k[2], (NUM_EXPERTS, HID, DIM), jnp.float32) * s, 'w_down': jax.random.normal(k[3], (NUM_EXPERTS, DIM, HID), jnp.float32) * s, 'shared_w_up': jax.random.normal(k[4], (HID, DIM), jnp.float32) * s, 'shared_w_down': jax.random.normal(k[5], (DIM, HID), jnp.float32) * s}
    _L2_ffn_in = _L2_ffn_setup()

    def _L3_attn_setup():
        import jax, jax.numpy as jnp
        import numpy as np
        B, N, D, NH, MAXLEN = (2, 256, 128, 16, 256)
        HD = D // NH

        def srel_skew(x):
            b, h, n, _ = x.shape
            v = jnp.pad(x, ((0, 0), (0, 0), (0, 0), (1, 0)))
            return v.reshape(b, h, n + 1, n)[:, :, :n, :]

        def split_head(x):
            b, n, _ = x.shape
            return x.reshape(b, n, NH, HD).transpose(0, 2, 1, 3)
        key = jax.random.key(seed)
        ks = jax.random.split(key, 7)
        scale = 0.02
        return {'x': jax.random.normal(ks[0], (B, N, D), dtype=jnp.float32), 'Wq': jax.random.normal(ks[1], (D, D), dtype=jnp.float32) * scale, 'Wk': jax.random.normal(ks[2], (D, D), dtype=jnp.float32) * scale, 'Wv': jax.random.normal(ks[3], (D, D), dtype=jnp.float32) * scale, 'Wp': jax.random.normal(ks[4], (D, D), dtype=jnp.float32) * scale, 'bp': jnp.zeros((D,), dtype=jnp.float32), 'rel_embed': jax.random.normal(ks[5], (MAXLEN, D), dtype=jnp.float32) * scale}
    _L3_attn_in = _L3_attn_setup()

    def _L3_ffn_setup():
        import jax, jax.numpy as jnp
        import numpy as np
        DIM = 128
        HIDDEN = 384
        SCALE = 1.0 / 127.0

        def _dequant(w_int, dtype):
            return w_int.astype(dtype) * jnp.asarray(SCALE, dtype)
        key = jax.random.key(seed)
        k_x, k_g, k_u, k_d = jax.random.split(key, 4)
        x = jax.random.normal(k_x, (4, 256, DIM), dtype=jnp.float32)
        w_gate = jax.random.randint(k_g, (HIDDEN, DIM), -127, 128, dtype=jnp.int32)
        w_up = jax.random.randint(k_u, (HIDDEN, DIM), -127, 128, dtype=jnp.int32)
        w_down = jax.random.randint(k_d, (DIM, HIDDEN), -127, 128, dtype=jnp.int32)
        return {'x': x, 'w_gate': w_gate, 'w_up': w_up, 'w_down': w_down}
    _L3_ffn_in = _L3_ffn_setup()
    _d = {'L0_attn_x': _L0_attn_in['x'], 'L0_attn_W_in': _L0_attn_in['W_in'], 'L0_attn_W_zxbcdt': _L0_attn_in['W_zxbcdt'], 'L0_attn_conv_w': _L0_attn_in['conv_w'], 'L0_attn_conv_b': _L0_attn_in['conv_b'], 'L0_attn_dt_bias': _L0_attn_in['dt_bias'], 'L0_attn_A_log': _L0_attn_in['A_log'], 'L0_attn_D_param': _L0_attn_in['D_param'], 'L0_attn_norm_pre_w': _L0_attn_in['norm_pre_w'], 'L0_attn_norm_gated_w': _L0_attn_in['norm_gated_w'], 'L0_attn_W_out': _L0_attn_in['W_out'], 'L0_ffn_w_gate': _L0_ffn_in['w_gate'], 'L0_ffn_w_up': _L0_ffn_in['w_up'], 'L0_ffn_w_down': _L0_ffn_in['w_down'], 'L1_attn_Wq': _L1_attn_in['Wq'], 'L1_attn_bq': _L1_attn_in['bq'], 'L1_attn_Wk': _L1_attn_in['Wk'], 'L1_attn_bk': _L1_attn_in['bk'], 'L1_attn_Wv': _L1_attn_in['Wv'], 'L1_attn_bv': _L1_attn_in['bv'], 'L1_ffn_router_w': _L1_ffn_in['router_w'], 'L1_ffn_w1': _L1_ffn_in['w1'], 'L1_ffn_w3': _L1_ffn_in['w3'], 'L1_ffn_w2': _L1_ffn_in['w2'], 'L2_attn_rms_w': _L2_attn_in['rms_w'], 'L2_attn_in_proj_w': _L2_attn_in['in_proj_w'], 'L2_attn_in_proj_b': _L2_attn_in['in_proj_b'], 'L2_attn_conv_w': _L2_attn_in['conv_w'], 'L2_attn_conv_b': _L2_attn_in['conv_b'], 'L2_attn_gate_w': _L2_attn_in['gate_w'], 'L2_attn_gate_b': _L2_attn_in['gate_b'], 'L2_attn_log_dt_scale': _L2_attn_in['log_dt_scale'], 'L2_attn_Q_w': _L2_attn_in['Q_w'], 'L2_attn_readout_w': _L2_attn_in['readout_w'], 'L2_attn_out_w': _L2_attn_in['out_w'], 'L2_attn_gn_w': _L2_attn_in['gn_w'], 'L2_attn_gn_b': _L2_attn_in['gn_b'], 'L2_attn_D_param': _L2_attn_in['D_param'], 'L2_ffn_gate_w': _L2_ffn_in['gate_w'], 'L2_ffn_expert_bias': _L2_ffn_in['expert_bias'], 'L2_ffn_w_up': _L2_ffn_in['w_up'], 'L2_ffn_w_down': _L2_ffn_in['w_down'], 'L2_ffn_shared_w_up': _L2_ffn_in['shared_w_up'], 'L2_ffn_shared_w_down': _L2_ffn_in['shared_w_down'], 'L3_attn_Wq': _L3_attn_in['Wq'], 'L3_attn_Wk': _L3_attn_in['Wk'], 'L3_attn_Wv': _L3_attn_in['Wv'], 'L3_attn_Wp': _L3_attn_in['Wp'], 'L3_attn_bp': _L3_attn_in['bp'], 'L3_attn_rel_embed': _L3_attn_in['rel_embed'], 'L3_ffn_w_gate': _L3_ffn_in['w_gate'], 'L3_ffn_w_up': _L3_ffn_in['w_up'], 'L3_ffn_w_down': _L3_ffn_in['w_down']}
    _x0 = _d['L0_attn_x']
    _d['L0_attn_x'] = jax.random.normal(jax.random.fold_in(jax.random.key(seed), 1), (4, 1024, 128), dtype=_x0.dtype)
    del _x0
    return _d

def reference(L0_attn_x, L0_attn_W_in, L0_attn_W_zxbcdt, L0_attn_conv_w, L0_attn_conv_b, L0_attn_dt_bias, L0_attn_A_log, L0_attn_D_param, L0_attn_norm_pre_w, L0_attn_norm_gated_w, L0_attn_W_out, L0_ffn_w_gate, L0_ffn_w_up, L0_ffn_w_down, L1_attn_Wq, L1_attn_bq, L1_attn_Wk, L1_attn_bk, L1_attn_Wv, L1_attn_bv, L1_ffn_router_w, L1_ffn_w1, L1_ffn_w3, L1_ffn_w2, L2_attn_rms_w, L2_attn_in_proj_w, L2_attn_in_proj_b, L2_attn_conv_w, L2_attn_conv_b, L2_attn_gate_w, L2_attn_gate_b, L2_attn_log_dt_scale, L2_attn_Q_w, L2_attn_readout_w, L2_attn_out_w, L2_attn_gn_w, L2_attn_gn_b, L2_attn_D_param, L2_ffn_gate_w, L2_ffn_expert_bias, L2_ffn_w_up, L2_ffn_w_down, L2_ffn_shared_w_up, L2_ffn_shared_w_down, L3_attn_Wq, L3_attn_Wk, L3_attn_Wv, L3_attn_Wp, L3_attn_bp, L3_attn_rel_embed, L3_ffn_w_gate, L3_ffn_w_up, L3_ffn_w_down):

    def _L0_attn_ref(x, W_in, W_zxbcdt, conv_w, conv_b, dt_bias, A_log, D_param, norm_pre_w, norm_gated_w, W_out):
        import jax, jax.numpy as jnp
        import numpy as np
        D_MODEL = 128
        NHEAD = 16
        HEAD_DIM = D_MODEL // NHEAD
        ROTARY_DIM = HEAD_DIM
        D_INNER = 2 * D_MODEL
        HEADDIM = 64
        H_SSM = D_INNER // HEADDIM
        D_STATE = 128
        D_CONV = 4
        CHUNK = 32
        CONV_DIM = D_INNER + 2 * D_STATE
        D_IN_PROJ = 2 * D_INNER + 2 * D_STATE + H_SSM
        EPS = 1e-05

        def rmsnorm(x, w):
            var = jnp.mean(x * x, axis=-1, keepdims=True)
            return x * jax.lax.rsqrt(var + EPS) * w

        def apply_rope(q):
            T = q.shape[1]
            half = ROTARY_DIM // 2
            inv_freq = 1.0 / 10000.0 ** (jnp.arange(0, ROTARY_DIM, 2, dtype=jnp.float32) / ROTARY_DIM)
            freqs = jnp.arange(T, dtype=jnp.float32)[:, None] * inv_freq[None, :]
            cos = jnp.cos(freqs)[None, :, None, :]
            sin = jnp.sin(freqs)[None, :, None, :]
            q1 = q[..., :half]
            q2 = q[..., half:ROTARY_DIM]
            rest = q[..., ROTARY_DIM:]
            return jnp.concatenate([q1 * cos - q2 * sin, q2 * cos + q1 * sin, rest], axis=-1)

        def segsum(x):
            T = x.shape[-1]
            xc = jnp.cumsum(x, axis=-1)
            ss = xc[..., :, None] - xc[..., None, :]
            mask = jnp.tril(jnp.ones((T, T), dtype=bool))
            return jnp.where(mask, ss, -jnp.inf)

        def ssd(x, dt, A, Bm, Cm):
            b, l, h, p = x.shape
            n = Bm.shape[-1]
            c = l // CHUNK
            xdt = (x * dt[..., None]).reshape(b, c, CHUNK, h, p)
            Adt = (dt * A).reshape(b, c, CHUNK, h).transpose(0, 3, 1, 2)
            Br = Bm.reshape(b, c, CHUNK, n)
            Cr = Cm.reshape(b, c, CHUNK, n)
            Acs = jnp.cumsum(Adt, axis=-1)
            Lmat = jnp.exp(segsum(Adt))
            Y_diag = jnp.einsum('bcln,bcsn,bhcls,bcshp->bclhp', Cr, Br, Lmat, xdt)
            decay_states = jnp.exp(Acs[..., -1:] - Acs)
            states = jnp.einsum('bcln,bhcl,bclhp->bchpn', Br, decay_states, xdt)
            A_chunk = jnp.pad(Acs[..., -1], ((0, 0), (0, 0), (1, 0)))
            decay_chunk = jnp.exp(segsum(A_chunk))
            states = jnp.concatenate([jnp.zeros_like(states[:, :1]), states], axis=1)
            new_states = jnp.einsum('bhzc,bchpn->bzhpn', decay_chunk, states)
            states_prev = new_states[:, :-1]
            Y_off = jnp.einsum('bcln,bchpn,bhcl->bclhp', Cr, states_prev, jnp.exp(Acs))
            return (Y_diag + Y_off).reshape(b, l, h, p)
        N, T, _ = x.shape
        qkv = (x @ W_in.T).reshape(N, T, 3, NHEAD, HEAD_DIM)
        q = apply_rope(qkv[:, :, 0]).reshape(N, T, D_MODEL)
        residual = q
        h = rmsnorm(q, norm_pre_w)
        zxbcdt = h @ W_zxbcdt.T
        z = zxbcdt[..., :D_INNER]
        xBC = zxbcdt[..., D_INNER:D_INNER + CONV_DIM]
        dt = jax.nn.softplus(zxbcdt[..., -H_SSM:] + dt_bias)
        xp = jnp.pad(xBC, ((0, 0), (D_CONV - 1, 0), (0, 0)))
        conv_out = conv_b
        for k in range(D_CONV):
            conv_out = conv_out + xp[:, k:k + T, :] * conv_w[:, k]
        xBC = jax.nn.silu(conv_out)
        x_ssm = xBC[..., :D_INNER].reshape(N, T, H_SSM, HEADDIM)
        Bm = xBC[..., D_INNER:D_INNER + D_STATE]
        Cm = xBC[..., D_INNER + D_STATE:]
        A = -jnp.exp(A_log)
        y = ssd(x_ssm, dt, A, Bm, Cm) + D_param[None, None, :, None] * x_ssm
        y = y.reshape(N, T, D_INNER)
        y = rmsnorm(y * jax.nn.silu(z), norm_gated_w)
        out = y @ W_out.T
        return out + residual

    def _L0_ffn_ref(x, w_gate, w_up, w_down):
        import jax, jax.numpy as jnp
        import numpy as np
        BLOCK = 16
        _GRID = jnp.array([0.0, 0.5, 1.0, 1.5, 2.0, 3.0, 4.0, 6.0], dtype=jnp.float32)
        _MID = jnp.array([0.25, 0.75, 1.25, 1.75, 2.5, 3.5, 5.0], dtype=jnp.float32)

        def fp4_quant_dequant(x):
            shape = x.shape
            xb = x.reshape(shape[:-1] + (shape[-1] // BLOCK, BLOCK))
            scale = jnp.max(jnp.abs(xb), axis=-1, keepdims=True) / 6.0
            scale = jnp.maximum(scale, jnp.float32(1e-12))
            xn = xb / scale
            idx = jnp.searchsorted(_MID, jnp.abs(xn))
            q = _GRID[idx] * jnp.sign(xn) * scale
            return q.reshape(shape)

        def fp4_linear(x, w):
            xq = fp4_quant_dequant(x)
            wq = fp4_quant_dequant(w)
            return jnp.einsum('bsk,nk->bsn', xq, wq)
        gate = fp4_linear(x, w_gate)
        y = fp4_linear(x, w_up)
        h = jax.nn.silu(gate) * y
        return fp4_linear(h, w_down)

    def _L1_attn_ref(y_de, Wq, bq, Wk, bk, Wv, bv):
        import jax, jax.numpy as jnp
        import numpy as np
        EMBED = 128
        HEADS = 16
        PER_DIM = EMBED // HEADS
        C, T = (64, 128)

        def entmax15(x, axis=-1):
            x = x / 2.0
            x = x - jnp.max(x, axis=axis, keepdims=True)
            xs = -jnp.sort(-x, axis=axis)
            n = x.shape[axis]
            k = jnp.arange(1, n + 1, dtype=x.dtype)
            cum = jnp.cumsum(xs, axis=axis)
            cumsq = jnp.cumsum(xs * xs, axis=axis)
            mean = cum / k
            ss = cumsq - cum * mean
            delta = jnp.clip((1.0 - ss) / k, 0.0)
            tau = mean - jnp.sqrt(delta)
            k_star = jnp.sum((tau <= xs).astype(jnp.int32), axis=axis, keepdims=True) - 1
            tau_star = jnp.take_along_axis(tau, k_star, axis=axis)
            return jnp.square(jnp.clip(x - tau_star, 0.0))
        c, t, e = y_de.shape
        mask = jnp.tril(jnp.ones((t, e), dtype=y_de.dtype), k=-1)
        x = (y_de * mask).reshape(c, t, HEADS, PER_DIM)
        q = x @ Wq.T + bq
        k_ = x @ Wk.T + bk
        v = x @ Wv.T + bv
        scale = 1.0 / e ** 0.5
        scores = jnp.einsum('cthd,ctgd->cthg', q, k_) * scale
        attn = entmax15(scores, axis=-1)
        out = jnp.einsum('cthg,ctgd->cthd', attn, v)
        return out.reshape(c, t, e)

    def _L1_ffn_ref(inputs, router_w, w1, w3, w2):
        import jax, jax.numpy as jnp
        import numpy as np
        B, S, H, F, E, K = (2, 128, 128, 256, 8, 2)
        b, s, h = inputs.shape
        x = inputs.reshape(-1, h)
        logits = x @ router_w
        top_vals, top_idx = jax.lax.top_k(logits, K)
        importance = jax.nn.softmax(top_vals.astype(jnp.float32), axis=-1).astype(x.dtype)
        one_hot = top_idx[..., None] == jnp.arange(E)[None, None, :]
        combine = jnp.sum(jnp.where(one_hot, importance[..., None], 0.0), axis=1)
        gate = jax.nn.silu(jnp.einsum('th,ehf->etf', x, w1))
        up = jnp.einsum('th,ehf->etf', x, w3)
        expert_out = jnp.einsum('etf,efh->eth', gate * up, w2)
        out = jnp.einsum('te,eth->th', combine, expert_out)
        return out.reshape(b, s, h)

    def _L2_attn_ref(x, rms_w, in_proj_w, in_proj_b, conv_w, conv_b, gate_w, gate_b, log_dt_scale, Q_w, readout_w, out_w, gn_w, gn_b, D_param):
        import jax, jax.numpy as jnp
        import numpy as np
        B, L, DM, DI, H = (4, 256, 128, 256, 16)
        HD = DI // H
        KS = 4
        ROPE_BASE = 10000.0
        GATING_C = 8.0
        EPS_NORM = 1e-06
        EPS_DT = 0.0001
        GN_GROUPS = 16
        GN_EPS = 1e-05

        def _rms_norm(x, w):
            v = jnp.mean(x * x, axis=-1, keepdims=True)
            return x * jax.lax.rsqrt(v + EPS_NORM) * w

        def _conv_silu(x, w, b):
            k = w.shape[1]
            xp = jnp.pad(x, ((0, 0), (k - 1, 0), (0, 0)))
            y = b
            for j in range(k):
                y = y + xp[:, j:j + x.shape[1], :] * w[:, j]
            return y * jax.nn.sigmoid(y)

        def _forward(x, rms_w, in_proj_w, in_proj_b, conv_w, conv_b, gate_w, gate_b, log_dt_scale, Q_w, readout_w, out_w, gn_w, gn_b, D_param):
            b, l, _ = x.shape
            di = conv_w.shape[0]
            h = log_dt_scale.shape[0]
            hd = di // h
            residual = x
            xn = _rms_norm(x, rms_w)
            proj = xn @ in_proj_w + in_proj_b
            z = proj[..., :di]
            x_gate = proj[..., di:2 * di]
            K = proj[..., 2 * di:3 * di].reshape(b, l, h, hd)
            V = proj[..., 3 * di:].reshape(b, l, h, 2)
            x_conv = _conv_silu(x_gate, conv_w, conv_b)
            gates = (x_conv @ gate_w + gate_b).reshape(b, l, 7, h)
            alpha_raw, omega_raw = (gates[..., 0, :], gates[..., 1, :])
            sel_B, sel_C = (gates[..., 2, :], gates[..., 3, :])
            sel_dt, beta_raw, r_raw = (gates[..., 4, :], gates[..., 5, :], gates[..., 6, :])
            freqs = 1.0 / ROPE_BASE ** (jnp.arange(h, dtype=jnp.float32) / h)
            dt = jax.nn.softplus(sel_dt) * jnp.exp(log_dt_scale) + EPS_DT
            alpha = jax.nn.softplus(alpha_raw)
            omega = freqs * (1.0 + jnp.tanh(omega_raw))
            ah, wh = (0.5 * dt * alpha, 0.5 * dt * omega)
            det = (1.0 + ah) ** 2 + wh ** 2
            c = (1.0 - ah ** 2 - wh ** 2) / det
            s = 2.0 * wh / det
            mag = jnp.sqrt(c * c + s * s)
            theta = jnp.arctan2(s, c)
            r = jax.nn.sigmoid(r_raw)
            mag2 = jnp.exp(GATING_C * r * jnp.log(jnp.clip(mag, 1e-08, 1.0)))
            cbar, sbar = (mag2 * jnp.cos(theta), mag2 * jnp.sin(theta))
            vp_scale = jax.nn.sigmoid(sel_B) * jnp.sqrt(jnp.clip(1.0 - mag2 ** 2, 0.0, 1.0) + 1e-06)
            beta = jax.nn.sigmoid(beta_raw)
            sel_C_gate = jax.nn.sigmoid(sel_C)
            Q = (x_conv @ Q_w).reshape(b, l, h, hd)
            K = K / (jnp.linalg.norm(K, axis=-1, keepdims=True) + 1e-06)
            Q = Q / (jnp.linalg.norm(Q, axis=-1, keepdims=True) + 1e-06)
            Vg = V * vp_scale[..., None]

            def step(S, inp):
                ct, st, kt, vt, bt = inp
                S0, S1 = (S[:, :, 0], S[:, :, 1])
                Sd = jnp.stack([ct[..., None] * S0 + st[..., None] * S1, -st[..., None] * S0 + ct[..., None] * S1], axis=2)
                pred = jnp.einsum('bhsd,bhd->bhs', Sd, kt)
                Sn = Sd + bt[:, :, None, None] * (vt - pred)[..., None] * kt[:, :, None, :]
                return (Sn, Sn)
            xs = (jnp.moveaxis(cbar, 1, 0), jnp.moveaxis(sbar, 1, 0), jnp.moveaxis(K, 1, 0), jnp.moveaxis(Vg, 1, 0), jnp.moveaxis(beta, 1, 0))
            S0 = jnp.zeros((b, h, 2, hd), dtype=x.dtype)
            _, Ys = jax.lax.scan(step, S0, xs)
            Y = jnp.moveaxis(Ys, 0, 1)
            retrieved = jnp.einsum('blhsd,blhd->blhs', Y, Q) * sel_C_gate[..., None]
            y = retrieved.reshape(b, l, h * 2) @ readout_w
            yf = y.astype(jnp.float32).reshape(b, l, GN_GROUPS, di // GN_GROUPS)
            mean = jnp.mean(yf, axis=(1, 3), keepdims=True)
            var = jnp.mean((yf - mean) ** 2, axis=(1, 3), keepdims=True)
            yn = ((yf - mean) * jax.lax.rsqrt(var + GN_EPS)).reshape(b, l, di)
            y = (yn * gn_w + gn_b).astype(x.dtype)
            y = y * (z * jax.nn.sigmoid(z))
            y = y + D_param * x_conv
            out = y @ out_w
            return residual + out
        return _forward(x, rms_w, in_proj_w, in_proj_b, conv_w, conv_b, gate_w, gate_b, log_dt_scale, Q_w, readout_w, out_w, gn_w, gn_b, D_param)

    def _L2_ffn_ref(x, gate_w, expert_bias, w_up, w_down, shared_w_up, shared_w_down):
        import jax, jax.numpy as jnp
        import numpy as np
        BS, SLEN, DIM = (1, 256, 128)
        NUM_EXPERTS, TOP_K = (8, 2)
        HID = 176

        def _masked_grouped_mm(x, w, onehot):
            g = jnp.einsum('tk,gnk->tgn', x, w, preferred_element_type=jnp.float32)
            return jnp.einsum('tgn,tg->tn', g, onehot)

        def moe_forward(x, gate_w, expert_bias, w_up, w_down, shared_w_up, shared_w_down):
            bs, slen, dim = x.shape
            xf = x.reshape(-1, dim)
            scores = jax.nn.sigmoid((xf @ gate_w.T).astype(jnp.float32))
            biased = scores + expert_bias
            _, sel = jax.lax.top_k(biased, TOP_K)
            top_scores = jnp.take_along_axis(scores, sel, axis=-1)
            flat_sel = sel.reshape(-1)
            counts = jnp.bincount(flat_sel, length=NUM_EXPERTS)
            order = jnp.argsort(flat_sel, stable=True)
            scores_sorted = top_scores.reshape(-1)[order]
            token_ids = order // TOP_K
            routed_in = (xf[token_ids] * scores_sorted[:, None]).astype(x.dtype)
            seg = jnp.repeat(jnp.arange(NUM_EXPERTS), counts, total_repeat_length=flat_sel.shape[0])
            onehot = jax.nn.one_hot(seg, NUM_EXPERTS, dtype=jnp.float32)
            h = _masked_grouped_mm(routed_in.astype(jnp.bfloat16), w_up.astype(jnp.bfloat16), onehot)
            h = jnp.square(jax.nn.relu(h.astype(jnp.bfloat16)))
            routed_out = _masked_grouped_mm(h.astype(jnp.bfloat16), w_down.astype(jnp.bfloat16), onehot)
            routed_out = routed_out.astype(jnp.bfloat16).astype(x.dtype)
            hs = jnp.square(jax.nn.relu(xf @ shared_w_up.T))
            shared_out = hs @ shared_w_down.T
            combined = jnp.zeros((flat_sel.shape[0], dim), routed_out.dtype).at[order].set(routed_out)
            out = combined.reshape(-1, TOP_K, dim).sum(axis=1) + shared_out
            return out.reshape(bs, slen, dim)
        return moe_forward(x, gate_w, expert_bias, w_up, w_down, shared_w_up, shared_w_down)

    def _L3_attn_ref(x, Wq, Wk, Wv, Wp, bp, rel_embed):
        import jax, jax.numpy as jnp
        import numpy as np
        B, N, D, NH, MAXLEN = (2, 256, 128, 16, 256)
        HD = D // NH

        def srel_skew(x):
            b, h, n, _ = x.shape
            v = jnp.pad(x, ((0, 0), (0, 0), (0, 0), (1, 0)))
            return v.reshape(b, h, n + 1, n)[:, :, :n, :]

        def split_head(x):
            b, n, _ = x.shape
            return x.reshape(b, n, NH, HD).transpose(0, 2, 1, 3)
        b, n, d = x.shape
        qx = split_head(x @ Wq.T)
        kx = split_head(x @ Wk.T)
        vx = split_head(x @ Wv.T)
        ns = jnp.arange(n) + (MAXLEN - n)
        ex = rel_embed[ns].reshape(n, NH, HD).transpose(1, 0, 2)
        srel = srel_skew(jnp.einsum('bhnd,hmd->bhnm', qx, ex))
        inv_dim = 1.0 / np.sqrt(d / NH)
        qk = (jnp.einsum('bhnd,bhmd->bhnm', qx, kx) + srel) * inv_dim
        mask = 1000000000.0 * jnp.triu(jnp.ones((n, n), dtype=x.dtype), 1)
        atten = jax.nn.softmax(qk - mask, axis=-1)
        out = jnp.einsum('bhnm,bhmd->bhnd', atten, vx).transpose(0, 2, 1, 3).reshape(b, n, d)
        return out @ Wp.T + bp

    def _L3_ffn_ref(x, w_gate, w_up, w_down):
        import jax, jax.numpy as jnp
        import numpy as np
        DIM = 128
        HIDDEN = 384
        SCALE = 1.0 / 127.0

        def _dequant(w_int, dtype):
            return w_int.astype(dtype) * jnp.asarray(SCALE, dtype)
        wg = _dequant(w_gate, x.dtype)
        wu = _dequant(w_up, x.dtype)
        wd = _dequant(w_down, x.dtype)
        gate = jnp.einsum('bsd,hd->bsh', x, wg)
        up = jnp.einsum('bsd,hd->bsh', x, wu)
        h = jax.nn.silu(gate) * up
        return jnp.einsum('bsh,dh->bsd', h, wd)
    x = L0_attn_x
    xn = _layernorm(x, axis=-1)
    s = _L0_attn_ref(xn, L0_attn_W_in, L0_attn_W_zxbcdt, L0_attn_conv_w, L0_attn_conv_b, L0_attn_dt_bias, L0_attn_A_log, L0_attn_D_param, L0_attn_norm_pre_w, L0_attn_norm_gated_w, L0_attn_W_out)
    g = _silu(_L0_ffn_ref(xn, L0_ffn_w_gate, L0_ffn_w_up, L0_ffn_w_down))
    x = x + s * g
    xn = _layernorm(x, axis=-1)
    s = _L1_attn_ref(xn, L1_attn_Wq, L1_attn_bq, L1_attn_Wk, L1_attn_bk, L1_attn_Wv, L1_attn_bv)
    g = _silu(_L1_ffn_ref(xn, L1_ffn_router_w, L1_ffn_w1, L1_ffn_w3, L1_ffn_w2))
    x = x + s * g
    xn = _layernorm(x, axis=-1)
    s = _L2_attn_ref(xn, L2_attn_rms_w, L2_attn_in_proj_w, L2_attn_in_proj_b, L2_attn_conv_w, L2_attn_conv_b, L2_attn_gate_w, L2_attn_gate_b, L2_attn_log_dt_scale, L2_attn_Q_w, L2_attn_readout_w, L2_attn_out_w, L2_attn_gn_w, L2_attn_gn_b, L2_attn_D_param)
    g = _silu(_L2_ffn_ref(xn, L2_ffn_gate_w, L2_ffn_expert_bias, L2_ffn_w_up, L2_ffn_w_down, L2_ffn_shared_w_up, L2_ffn_shared_w_down))
    x = x + s * g
    xn = _layernorm(x, axis=-1)
    s = _L3_attn_ref(xn, L3_attn_Wq, L3_attn_Wk, L3_attn_Wv, L3_attn_Wp, L3_attn_bp, L3_attn_rel_embed)
    g = _silu(_L3_ffn_ref(xn, L3_ffn_w_gate, L3_ffn_w_up, L3_ffn_w_down))
    x = x + s * g
    return x

_drawn_inputs = setup_inputs


def setup_inputs(seed=0):
    import zlib

    import numpy as np

    out = dict(_drawn_inputs(seed))
    spreads = {'L0_attn_conv_b': (0.0, 0.1),
     'L0_attn_norm_pre_w': (1.0, 0.2),
     'L0_attn_norm_gated_w': (1.0, 0.2),
     'L2_attn_rms_w': (1.0, 0.2),
     'L2_attn_in_proj_b': (0.0, 0.1),
     'L2_attn_conv_b': (0.0, 0.1),
     'L2_ffn_expert_bias': (0.0, 0.1),
     'L3_attn_bp': (0.0, 0.1)}
    factors = {}
    for name, (base, spread) in spreads.items():
        noise = np.random.default_rng([zlib.crc32(name.encode()), seed]).standard_normal(out[name].shape)
        drawn = base * np.exp(spread * noise) if base else spread * noise
        out[name] = jnp.asarray(drawn.astype(out[name].dtype))
    for name, factor in factors.items():
        out[name] = (out[name] * factor).astype(out[name].dtype)
    return out
```

```python
from contextlib import ExitStack, contextmanager

import concourse.bass as bass
import numpy as np
from concourse import mybir

F32 = mybir.dt.float32
BF16 = mybir.dt.bfloat16
I32 = mybir.dt.int32
ALU = mybir.AluOpType
ACT = mybir.ActivationFunctionType
AX = mybir.AxisListType.X
P = 128
D = 128
B, T = 4, 1024
TB = 512
NT = TB // P
LN_EPS = 1e-5


class Mark:

    def __init__(self, src):
        self.src, self.n, self.loop = src, src.n, src.loop


class Counted:

    def __init__(self, nc, name, step=1):
        self.sem = nc.alloc_semaphore(name)
        nc.sync.sem_inc(self.sem, step)
        self.name, self.step, self.n, self.loop, self.per, self.base = name, step, step, None, 0, 0

    def value(self, n, loop):
        if loop is None:
            return n
        assert loop is self.loop, "a mark from a loop's body is used outside of it"
        return loop * self.per + n

    def raise_by(self, ins):
        ins.then_inc(self.sem, self.step)
        self.n += self.step


class Engine(Counted):

    def __init__(self, nc, eng, name):
        super().__init__(nc, name)
        self.eng, self.seen, self.apart, self.spare = eng, {}, False, None
        self.each_apart = False

    def wait(self, *sources):
        for s in sources:
            m = s if isinstance(s, Mark) else Mark(s)
            key = (m.src.name, m.loop is None)
            if self.seen.get(key, -1) >= m.n:
                continue
            self.seen[key] = m.n
            self.eng.wait_ge(m.src.sem, m.src.value(m.n, m.loop))
            if self.each_apart and self.loop is not None:
                self.eng.sem_inc(self.spare.sem, 1)

    def __call__(self, op, *args, after=(), own=True, apart=False, **kw):
        self.wait(*after)
        if own:
            self.wait(self)
        if self.loop is not None and (apart or self.apart):
            self.eng.sem_inc(self.spare.sem, 1)
        self.raise_by(op(*args, **kw))
        return Mark(self)

    def dma(self, queue, out, in_, after=()):
        self.wait(*after)
        queue.raise_by(self.eng.dma_start(out, in_))
        return Mark(queue)


class Machine:

    def __init__(self, nc, per_iteration):
        self.nc, self.per_iteration, self.learned = nc, per_iteration, {}
        self.V = Engine(nc, nc.vector, "vector_done")
        self.A = Engine(nc, nc.scalar, "scalar_done")
        self.G = Engine(nc, nc.gpsimd, "gpsimd_done")
        self.E = Engine(nc, nc.tensor, "tensor_done")
        self.S = Engine(nc, nc.sync, "sync_done")
        self.engines = (self.V, self.A, self.G, self.E, self.S)
        self.queues = {}
        spare = Counted(nc, "spare")
        for e in self.engines:
            e.spare = spare
        self.G.apart = self.S.each_apart = True
        self.n_names = 0

    def queue(self, name):
        if name not in self.queues:
            self.queues[name] = Counted(self.nc, "dma_" + name, 16)
        return self.queues[name]

    @contextmanager
    def loop(self, name, n, inner=None):
        every = list(self.engines) + list(self.queues.values())
        per = self.per_iteration.get(name, {})
        with ExitStack() as st:
            i = at = st.enter_context(self.nc.Fori(0, n))
            if inner:
                j = st.enter_context(self.nc.Fori(0, inner))
                i, at, n = i * inner + j, (i, j), n * inner
            for c in every:
                assert c.loop is None
                c.loop, c.per, c.base = i, per.get(c.name, 0), c.n
            for e in self.engines:
                e.seen = {}
            yield at
            assert all(q in every for q in self.queues.values()), "make queues ahead of a loop"
            self.learned[name] = {c.name: c.n - c.base for c in every}
        for c in every:
            c.n, c.loop = c.base + n * (c.n - c.base), None
        for e in self.engines:
            e.seen = {}

    def barrier(self):
        for e in self.engines:
            e.wait(*self.engines, *self.queues.values())

    @contextmanager
    def scope(self):
        with ExitStack() as st:
            def sb(shape, dt=F32):
                self.n_names += 1
                return st.enter_context(self.nc.sbuf_tensor(f"t{self.n_names}", list(shape), dt))
            yield sb
            self.barrier()


def rep(ap, axis, n):
    v = ap.unsqueeze(axis)
    shape = list(v.shape)
    shape[axis] = n
    return v.broadcast_to(shape)


def bank(ps, k, n=TB):
    return ps[:, k, 0:n]


class Common:

    def __init__(self, m, dram):
        nc = m.nc
        self.m, self.dram = m, dram
        self.ps = nc.alloc_psum_tensor("banks", [P, 8, TB], F32)
        self.xT = nc.alloc_sbuf_tensor("xT", [P, B * T], F32)
        self.ident = nc.alloc_sbuf_tensor("ident", [P, P], F32)
        self.mean_d = nc.alloc_sbuf_tensor("mean_d", [P, P], F32)
        self.eps = {v: nc.alloc_sbuf_tensor(f"eps{k}", [P, 1], F32) for k, v in enumerate((1e-5, 1e-6))}
        self.one = nc.alloc_sbuf_tensor("one", [P, 1], F32)
        self.q_w = m.queue("weights")
        m.queue("out")
        for k in "abcd":
            m.queue(k)

    def load_start(self):
        m, nc = self.m, self.m.nc
        m.S.dma(self.q_w, self.xT[:], self.dram["xT"])
        m.S.dma(self.q_w, self.ident[:], self.dram["c_ident"])
        m.V(nc.vector.memset, self.mean_d[:], 1.0 / D, own=False)
        m.V(nc.vector.memset, self.one[:], 1.0, own=False)
        for v, t in self.eps.items():
            m.V(nc.vector.memset, t[:], v, own=False)
        m.barrier()

    def layernorm(self, x, xn, tmp, bk):
        m, nc = self.m, self.m.nc
        V, A, E = m.V, m.A, m.E
        E(nc.tensor.matmul, bank(self.ps, bk), self.mean_d[:], x, start=True, stop=True, after=(V, A))
        V(nc.vector.tensor_tensor, xn, x, bank(self.ps, bk), ALU.subtract, after=(E, A))
        self.inverse_rms(xn, tmp, bk, LN_EPS)
        V(nc.vector.tensor_tensor, xn, xn, tmp, ALU.mult)

    def inverse_rms(self, x, out, bk, eps):
        m, nc = self.m, self.m.nc
        V, A, E = m.V, m.A, m.E
        A(nc.scalar.activation, out, x, ACT.Square, after=(V, E))
        E(nc.tensor.matmul, bank(self.ps, bk), self.mean_d[:], out, start=True, stop=True, after=(A, V))
        A(nc.scalar.activation, out, bank(self.ps, bk), ACT.Sqrt, bias=self.eps[eps][:], after=(E, V))
        V(nc.vector.reciprocal, out, out, after=(A,))

    def transpose(self, out, in_, after=()):
        k = in_.shape[0]
        return self.m.E(self.m.nc.tensor.transpose, out, in_, self.ident[0:k, 0:k], after=after)

    def update(self, x, s, g_ps, tmp):
        m, nc = self.m, self.m.nc
        m.A(nc.scalar.activation, tmp, g_ps, ACT.Silu, after=(m.E, m.V))
        m.V(nc.vector.tensor_tensor, tmp, tmp, s, ALU.mult, after=(m.A,))
        m.V(nc.vector.tensor_tensor, x, x, tmp, ALU.add)


H0, HP = 4, 64
DI0 = H0 * HP
FF0 = 352
QB = 16


def fp4(c, src, out, w, after):
    m, nc = c.m, c.m.nc
    V, A, G = m.V, m.A, m.G
    n = src.shape[0]
    nb = src.shape[1] // QB
    s3 = src.rearrange("p (b k) -> p b k", k=QB)
    o3 = out.rearrange("p (b k) -> p b k", k=QB)
    scale, inv = w["scale"][0:n, 0:nb], w["inv"][0:n, 0:nb]
    mag, fine, coarse, sign = (w[k][0:n, 0:nb * QB] for k in ("mag", "fine", "coarse", "sign"))
    mag3 = mag.rearrange("p (b k) -> p b k", k=QB)
    A(nc.scalar.activation, sign, src, ACT.Sign, after=(*after, V))
    V(nc.vector.tensor_reduce, scale, s3, AX, ALU.max, apply_absolute_value=True, after=after)
    V(nc.vector.tensor_scalar, scale, scale, 1.0 / 6.0, 1e-12, ALU.mult, ALU.max)
    V(nc.vector.reciprocal, inv, scale)
    V(nc.vector.tensor_tensor, mag3, s3, rep(inv, 2, QB), ALU.mult, after=(G,))
    V(nc.vector.scalar_tensor_tensor, mag, mag, -1.0, mag, ALU.mult, ALU.max)
    V(nc.vector.tensor_scalar, coarse, mag, 5.0, 2.0, ALU.is_gt, ALU.mult)
    V(nc.vector.tensor_scalar, fine, mag, 0.25, None, ALU.is_gt, own=False)
    for mid in (2.5, 3.5):
        V(nc.vector.scalar_tensor_tensor, coarse, mag, mid, coarse, ALU.is_gt, ALU.add)
    for mid in (0.75, 1.25, 1.75):
        V(nc.vector.scalar_tensor_tensor, fine, mag, mid, fine, ALU.is_gt, ALU.add)
    V(nc.vector.scalar_tensor_tensor, fine, coarse, 2.0, fine, ALU.mult, ALU.add)
    V(nc.vector.tensor_scalar, scale, scale, 0.5, None, ALU.mult, own=False)
    V(nc.vector.tensor_tensor, fine, fine, sign, ALU.mult, after=(A,))
    return V(nc.vector.tensor_tensor, o3, fine.rearrange("p (b k) -> p b k", k=QB), rep(scale, 2, QB), ALU.mult)


def layer0(c):
    m, nc, ps, d = c.m, c.m.nc, c.ps, c.dram
    V, A, G, E, S = m.V, m.A, m.G, m.E, m.S
    mm, act, tt, ts, stt = (nc.tensor.matmul, nc.scalar.activation, nc.vector.tensor_tensor,
                            nc.vector.tensor_scalar, nc.vector.scalar_tensor_tensor)
    with m.scope() as sb:
        wq, wqr = sb([P, D]), sb([P, D])
        wz, wxbc = sb([P, DI0]), sb([P, 4, 2 * DI0])
        wdt, wout = sb([P, H0]), sb([P, 2, D])
        cos, sin = sb([P, T]), sb([P, T])
        upper = sb([P, P])
        conv_b, npre, ngat, dcol = sb([P, 4]), sb([P, 1]), sb([P, 2]), sb([P, 2])
        dtb, neg_a = sb([P, H0]), sb([P, H0])
        wg, wu, wd = sb([P, FF0]), sb([P, FF0]), sb([P, 3, D])
        mean_di = sb([P, P])
        with m.scope() as tmp:
            raw, taps = tmp([P, 2 * DI0]), tmp([P, 4, 2 * DI0])
            wrow, wquant, wdrow, wdq = tmp([P, 2, 3, D]), tmp([P, D]), tmp([P, FF0]), tmp([P, FF0])
            w = {k: tmp([P, FF0]) for k in ("mag", "fine", "coarse", "sign")}
            w.update(scale=tmp([P, FF0 // QB]), inv=tmp([P, FF0 // QB]))
            for out, name in ((wq, "wq"), (wqr, "wqr"), (wz, "wz"), (wdt, "wdt"), (cos, "c_cos"), (sin, "c_sin"),
                              (upper, "c_upper"), (raw, "wxbc"), (wdrow, "fd0")):
                S.dma(c.q_w, out[:], d[name])
            S.dma(c.q_w, wout[:], d["wout0"].rearrange("(k p) n -> p k n", p=P))
            S.dma(c.q_w, conv_b[:], d["convb0"])
            S.dma(c.q_w, npre[:], d["npre"])
            S.dma(c.q_w, ngat[:], d["ngat"])
            for k in range(4):
                S.dma(c.q_w, taps[:, k, :], d["convw0"][k:k + 1, :].partition_broadcast(P))
            S.dma(c.q_w, dcol[:], d["D0"])
            S.dma(c.q_w, dtb[:], d["dtb"].unsqueeze(0).partition_broadcast(P))
            S.dma(c.q_w, neg_a[:], d["alog"].unsqueeze(0).partition_broadcast(P))
            for g, name in enumerate(("fg0", "fu0")):
                for k in range(3):
                    n = min(P, FF0 - k * P)
                    S.dma(c.q_w, wrow[0:n, g, k, :], d[name][k * P:k * P + n, :])
            V(nc.vector.memset, mean_di[:], 1.0 / DI0)
            for k in range(4):
                V(tt, wxbc[:, k, :], raw[:], taps[:, k, :], ALU.mult, after=(c.q_w,), own=False)
            A(act, neg_a[:], neg_a[:], ACT.Exp, after=(c.q_w,))
            V(ts, neg_a[:], neg_a[:], -1.0, None, ALU.mult, after=(A,))
            for g, out in enumerate((wg, wu)):
                for k in range(3):
                    n = min(P, FF0 - k * P)
                    fp4(c, wrow[0:n, g, k, :], wquant[0:n, :], w, (c.q_w, E))
                    c.transpose(ps[:, 0, 0:n], wquant[0:n, :], after=(V,))
                    V(nc.vector.tensor_copy, out[:, k * P:k * P + n], ps[:, 0, 0:n], after=(E,))
            fp4(c, wdrow[:], wdq[:], w, (c.q_w,))
            for k in range(3):
                n = min(P, FF0 - k * P)
                c.transpose(ps[0:n, 0, 0:P], wdq[:, k * P:k * P + n], after=(V,))
                V(nc.vector.tensor_copy, wd[0:n, k, :], ps[0:n, 0, 0:P], after=(E,))

        xn, q, hp = sb([P, TB]), sb([P, TB]), sb([P, 3 + TB])
        ta, tb = sb([P, TB]), sb([P, TB])
        zs, xbc, y = sb([P, 2, TB]), sb([P, 4, TB]), sb([P, 2, TB])
        dt, adt, t16 = sb([P, NT, H0]), sb([P, NT, H0]), sb([P, NT, H0])
        xdt, xdd, btok = sb([P, H0, HP]), sb([P, H0, HP]), sb([P, P])
        acs, dd = sb([P, H0]), sb([P, H0])
        ua, low, ce, mt = sb([P, H0, P]), sb([P, H0, P]), sb([P, H0, P]), sb([P, H0, P])
        ec, gm = sb([P, H0, P]), sb([P, P])
        state = sb([P, H0, HP])
        ones = sb([P, P])
        V(nc.vector.memset, ones[:], 1.0)
        w = {k: sb([P, FF0]) for k in ("mag", "fine", "coarse", "sign")}
        w.update(scale=sb([P, FF0 // QB]), inv=sb([P, FF0 // QB]))
        xt, xq, xqT = sb([P, D]), sb([P, D]), sb([P, P])
        hid, hq, hqT = sb([P, FF0]), sb([P, FF0]), sb([P, 3, TB])

        with m.loop("layer0", B) as b:
            for half in range(T // TB):
                xb = c.xT[:, bass.ds(b * T + half * TB, TB)]
                c.layernorm(xb, xn[:], ta[:], 0)
                E(mm, bank(ps, 0), wq[:], xn[:], start=True, stop=True, after=(V, A))
                E(mm, bank(ps, 1), wqr[:], xn[:], start=True, stop=True)
                at = slice(half * TB, half * TB + TB)
                V(tt, q[:], bank(ps, 0), cos[:, at], ALU.mult, after=(E,))
                V(tt, ta[:], bank(ps, 1), sin[:, at], ALU.mult)
                V(tt, q[:], q[:], ta[:], ALU.add)
                if half == 0:
                    V(nc.vector.memset, hp[:, 0:3], 0.0, after=(E,))
                else:
                    V(nc.vector.tensor_copy, hp[:, 0:3], hp[:, TB:TB + 3], after=(E,))
                c.inverse_rms(q[:], ta[:], 0, 1e-5)
                V(stt, hp[:, 3:], q[:], npre[:], ta[:], ALU.mult, ALU.mult)
                for k in range(2):
                    E(mm, bank(ps, k), wz[:, k * P:(k + 1) * P], hp[:, 3:], start=True, stop=True, after=(V, A))
                for k in range(4):
                    for j in range(4):
                        E(mm, bank(ps, 2 + k), wxbc[:, j, k * P:(k + 1) * P], hp[:, j:j + TB],
                          start=(j == 0), stop=(j == 3), own=False)
                for t in range(NT):
                    E(mm, ps[:, 6, H0 * t:H0 * t + H0], hp[:, 3 + t * P:3 + (t + 1) * P], wdt[:],
                      start=True, stop=True, own=False)
                for k in range(2):
                    A(act, zs[:, k, :], bank(ps, k), ACT.Silu, after=(E, V), own=False)
                for k in range(4):
                    A(act, xbc[:, k, :], bank(ps, 2 + k), ACT.Silu, bias=conv_b[:, k:k + 1], own=False)
                V(tt, dt[:], ps[:, 6, 0:NT * H0].rearrange("p (t h) -> p t h", h=H0), rep(dtb[:], 1, NT),
                  ALU.add, after=(E,))
                V(stt, t16[:], dt[:], -1.0, dt[:], ALU.mult, ALU.max)
                A(act, t16[:], t16[:], ACT.Exp, scale=-1.0, after=(V,))
                A(act, t16[:], t16[:], ACT.Ln, bias=c.one[:])
                V(stt, dt[:], dt[:], 0.0, t16[:], ALU.max, ALU.add, after=(A,))
                V(tt, adt[:], dt[:], rep(neg_a[:], 1, NT), ALU.mult)
                for t in range(NT):
                    ct = slice(t * P, (t + 1) * P)
                    first = half == 0 and t == 0
                    for k in range(3):
                        c.transpose(ps[:, 0, k * P:(k + 1) * P], xbc[:, k, ct], after=(A, V))
                    V(tt, xdt[:], ps[:, 0, 0:DI0].rearrange("p (h q) -> p h q", h=H0), rep(dt[:, t, :], 2, HP),
                      ALU.mult, after=(E,))
                    V(nc.vector.tensor_copy, btok[:], ps[:, 0, DI0:DI0 + P], own=False)
                    V(tt, ua[:], rep(upper[:], 1, H0), rep(adt[:, t, :], 2, P), ALU.mult, own=False)
                    E(mm, ps[:, 1, 0:H0], upper[:], adt[:, t, :], start=True, stop=True, after=(V,))
                    E(mm, bank(ps, 2), ones[:], ua[:].rearrange("p h t -> p (h t)"), start=True, stop=True, own=False)
                    E(mm, ps[:, 3, 0:P], xbc[:, 2, ct], xbc[:, 3, ct], start=True, stop=True, own=False)
                    rows = bank(ps, 2).rearrange("p (h t) -> p h t", h=H0)
                    V(nc.vector.tensor_copy, acs[:], ps[:, 1, 0:H0], after=(E,))
                    V(tt, gm[:], ps[:, 3, 0:P], upper[:], ALU.mult, own=False)
                    for h in range(H0):
                        V(ts, low[:, h, :], rows[:, h, :], acs[:, h:h + 1], 0.0, ALU.subtract, ALU.min, own=(h == 0))
                    V(tt, dd[:], rows[:, :, P - 1], acs[:], ALU.subtract, own=False)
                    A(act, ec[:], rows, ACT.Exp, after=(E, V))
                    A(act, low[:], low[:], ACT.Exp, own=False)
                    A(act, dd[:], dd[:], ACT.Exp, own=False)
                    V(tt, mt[:], low[:], rep(gm[:], 1, H0), ALU.mult, after=(A,))
                    V(tt, ce[:], ec[:], rep(xbc[:, 3, ct], 1, H0), ALU.mult, own=False)
                    V(tt, xdd[:], xdt[:], rep(dd[:], 2, HP), ALU.mult, own=False)
                    for h in range(H0):
                        o = ps[(h % 2) * HP:(h % 2 + 1) * HP, 4, (h // 2) * P:(h // 2 + 1) * P]
                        E(mm, o, xdt[:, h, :], mt[:, h, :], start=True, stop=first, after=(V,))
                        if not first:
                            E(mm, o, state[:, h, :], ce[:, h, :], start=False, stop=True, own=False)
                    E(mm, ps[:, 5, 0:DI0], btok[:], xdd[:].rearrange("p h q -> p (h q)"), start=True, stop=True)
                    for k in range(2):
                        V(stt, y[:, k, ct], xbc[:, k, ct], dcol[:, k:k + 1], ps[:, 4, k * P:(k + 1) * P],
                          ALU.mult, ALU.add, after=(E,), own=False)
                    new = ps[:, 5, 0:DI0].rearrange("p (h q) -> p h q", h=H0)
                    if first:
                        V(nc.vector.tensor_copy, state[:], new)
                    else:
                        V(tt, state[:], state[:], rep(ec[:, :, P - 1], 2, HP), ALU.mult)
                        V(tt, state[:], state[:], new, ALU.add)
                V(tt, y[:], y[:], zs[:], ALU.mult)
                for k in range(2):
                    A(act, zs[:, k, :], y[:, k, :], ACT.Square, after=(V,))
                    E(mm, bank(ps, 0), mean_di[:], zs[:, k, :], start=(k == 0), stop=(k == 1), after=(A,))
                A(act, ta[:], bank(ps, 0), ACT.Sqrt, bias=c.eps[1e-5][:], after=(E,))
                V(nc.vector.reciprocal, ta[:], ta[:], after=(A,))
                for k in range(2):
                    V(stt, y[:, k, :], y[:, k, :], ngat[:, k:k + 1], ta[:], ALU.mult, ALU.mult)
                    E(mm, bank(ps, 1), wout[:, k, :], y[:, k, :], start=(k == 0), stop=(k == 1), after=(V,))
                V(tt, q[:], q[:], bank(ps, 1), ALU.add, after=(E,))
                for t in range(NT):
                    ct = slice(t * P, (t + 1) * P)
                    c.transpose(ps[:, 2, 0:P], xn[:, ct], after=(V,))
                    A(nc.scalar.copy, xt[:], ps[:, 2, 0:P], after=(E, V))
                    fp4(c, xt[:], xq[:], w, (A,))
                    c.transpose(ps[:, 2, 0:P], xq[:], after=(V,))
                    A(nc.scalar.copy, xqT[:], ps[:, 2, 0:P], after=(E,))
                    E(mm, ps[:, 3, 0:FF0], xqT[:], wg[:], start=True, stop=True, after=(A,))
                    E(mm, ps[:, 4, 0:FF0], xqT[:], wu[:], start=True, stop=True)
                    A(act, hid[:], ps[:, 3, 0:FF0], ACT.Silu, after=(E, V))
                    V(tt, hid[:], hid[:], ps[:, 4, 0:FF0], ALU.mult, after=(A,))
                    fp4(c, hid[:], hq[:], w, (A,))
                    for k in range(3):
                        n = min(P, FF0 - k * P)
                        c.transpose(ps[0:n, 5, k * P:(k + 1) * P], hq[:, k * P:k * P + n], after=(V, A))
                    turned = bank(ps, 5, 3 * P).rearrange("p (k t) -> p k t", k=3)
                    A(nc.scalar.copy, hqT[:, 0:2, ct], turned[:, 0:2, :], after=(E,))
                    A(nc.scalar.copy, hqT[0:n, 2, ct], turned[0:n, 2, :])
                for k in range(3):
                    n = min(P, FF0 - k * P)
                    E(mm, bank(ps, 6), wd[0:n, k, :], hqT[0:n, k, :], start=(k == 0), stop=(k == 2), after=(A,))
                c.update(xb, q[:], bank(ps, 6), tb[:])


NH = 16
HD = D // NH
E1, F1 = 8, 256
ATTN_SCALE1 = D ** -0.5 / 2.0


def woven(*parts):
    live = list(parts)
    while live:
        for part in list(live):
            for _ in range(part[1]):
                if next(part[0], True):
                    live.remove(part)
                    break


def route(c, logits, w, keep, softmax):
    m, nc = c.m, c.m.nc
    V, A = m.V, m.A
    tt = nc.vector.tensor_tensor
    n = logits.shape[2]
    lj, le = rep(logits, 2, n), rep(logits, 3, n)
    V(tt, w["beats"], lj, le, ALU.is_equal, own=True)
    V(tt, w["beats"], w["beats"], rep(w["lower"], 1, NT), ALU.mult)
    V(tt, w["more"], lj, le, ALU.is_gt, own=False)
    V(tt, w["beats"], w["beats"], w["more"], ALU.add)
    V(nc.vector.tensor_reduce, w["rank"], w["beats"], AX, ALU.add)
    if softmax:
        V(nc.vector.tensor_reduce, w["top"], logits, AX, ALU.max, own=False)
        V(tt, w["score"], logits, rep(w["top"], 2, n), ALU.subtract)
        e = A(nc.scalar.activation, w["score"], w["score"], ACT.Exp, after=(Mark(V),), own=False)
        V(nc.vector.scalar_tensor_tensor, w["comb"], w["rank"], float(keep), w["score"], ALU.is_lt, ALU.mult, after=(e,))
        V(nc.vector.tensor_reduce, w["top"], w["comb"], AX, ALU.add)
        V(nc.vector.reciprocal, w["top"], w["top"])
        return V(tt, w["comb"], w["comb"], rep(w["top"], 2, n), ALU.mult)
    return V(nc.vector.scalar_tensor_tensor, w["comb"], w["rank"], float(keep), w["score"], ALU.is_lt, ALU.mult)


def route_buffers(sb, n):
    w = {k: sb([P, NT, n])[:] for k in ("rank", "score", "comb")}
    w.update(top=sb([P, NT])[:], beats=sb([P, NT, n, n])[:], more=sb([P, NT, n, n])[:], lower=sb([P, n, n])[:])
    return w


def sort_descending(c, a, b, n):
    V, tt = c.m.V, c.m.nc.vector.tensor_tensor
    size = 2
    while size <= n:
        step = size
        while step >= 2:
            va, vb = (x.rearrange("p (r k) -> p r k", k=step) for x in (a, b))
            h = step // 2
            if step == size:
                hi = slice(step - 1, h - 1 if h > 0 else None, -1)
            else:
                hi = slice(h, step)
            V(tt, vb[:, :, 0:h], va[:, :, 0:h], va[:, :, hi], ALU.max)
            V(tt, vb[:, :, hi], va[:, :, 0:h], va[:, :, hi], ALU.min, own=False)
            a, b = b, a
            step //= 2
        size *= 2
    return a, b


def layer1(c):
    m, nc, ps, d = c.m, c.m.nc, c.ps, c.dram
    V, A, G, E, S = m.V, m.A, m.G, m.E, m.S
    mm, act, tt, ts, stt = (nc.tensor.matmul, nc.scalar.activation, nc.vector.tensor_tensor,
                            nc.vector.tensor_scalar, nc.vector.scalar_tensor_tensor)
    reduce, copy = nc.vector.tensor_reduce, nc.vector.tensor_copy
    with m.scope() as sb:
        wqkv, bias, ones = sb([P, 3 * D]), sb([1, 3 * D]), sb([1, P])
        wr, w1, w3, w2 = sb([P, E1]), sb([P, E1, F1]), sb([P, E1, F1]), sb([P, F1 // P, E1, D])
        blocks, before = sb([P, P]), sb([P, P])
        order, restart, inv_k = sb([P, NH]), sb([P, NT * NH * NH]), sb([P, NH])
        pick = sb([E1, E1, P])
        rb = route_buffers(sb, E1)
        for out, name in ((wqkv, "wqkv1"), (bias, "bqkv1"), (blocks, "c_blocks"), (before, "c_before"),
                          (order, "c_order"), (inv_k, "c_inv_k"), (restart, "c_restart"), (pick, "c_pick"), (wr, "wr1")):
            S.dma(c.q_w, out[:], d[name])
        S.dma(c.q_w, rb["lower"], d["c_lower"])
        S.dma(c.q_w, w1[:], d["w1"].rearrange("e h f -> h e f"))
        S.dma(c.q_w, w3[:], d["w3"].rearrange("e h f -> h e f"))
        for k in range(F1 // P):
            S.dma(c.q_w, w2[:, k], d["w2"][:, k * P:(k + 1) * P, :].rearrange("e f h -> f e h"))
        V(nc.vector.memset, ones[:], 1.0)
        for k in range(3):
            V(tt, wqkv[:, k * D:(k + 1) * D], wqkv[:, k * D:(k + 1) * D], blocks[:], ALU.mult, after=(c.q_w,))

        xn, xm, tmp = sb([P, TB]), sb([P, P]), sb([P, TB])
        qkv = sb([P, NT, 3 * D])
        prod = [sb([P, NH * NH * HD]) for _ in range(2)]
        sc, sa, sbuf2 = (sb([P, NT, NH, NH]) for _ in range(3))
        cum, cumsq, tau = (sb([P, NT, NH, NH]) for _ in range(3))
        one = sb([P, NT * NH])
        s_tok, s_T = sb([P, NT, D]), sb([P, TB])
        lg, combT = sb([P, NT, E1]), sb([E1, TB])
        xs, hid = sb([P, 2, TB]), sb([P, 2, TB])
        rows = NT * NH

        def attention(half):
            ready = []
            for t in range(NT):
                x = xn[:, t * P:(t + 1) * P]
                if half == 0 and t == 0:
                    r = V(tt, xm[:], x, before[:], ALU.mult)
                    x = xm[:]
                else:
                    r = Mark(V)
                E(mm, bank(ps, 0, 3 * D), x, wqkv[:], start=True, stop=False, after=(r, Mark(A)))
                e = E(mm, bank(ps, 0, 3 * D), ones[:], bias[:], start=False, stop=True, own=False)
                A(act, qkv[:, t, 0:D], bank(ps, 0, D), ACT.Copy, scale=ATTN_SCALE1, after=(e, Mark(V), Mark(G)), own=False)
                a = A(nc.scalar.copy, qkv[:, t, D:], ps[:, 0, D:3 * D], own=False)
                q = qkv[:, t, 0:D].rearrange("p (h d) -> p h d", h=NH)
                k = qkv[:, t, D:2 * D].rearrange("p (h d) -> p h d", h=NH)
                pr = prod[t % 2][:].rearrange("p (h g d) -> p h g d", h=NH, g=NH)
                g = G(nc.gpsimd.tensor_tensor, pr, rep(q, 2, NH), rep(k, 1, NH), ALU.mult, after=(a, *ready[-2:-1]), own=False)
                ready.append(V(reduce, sc[:, t], pr, AX, ALU.add, after=(g,), own=False))
                yield
            flat = "p t h g -> p (t h g)"
            V(copy, sa[:], sc[:])
            top, other = sort_descending(c, sa[:].rearrange(flat), sbuf2[:].rearrange(flat), NH)
            yield
            r3 = "p (r k) -> p r k"
            top, other = top.rearrange(r3, k=NH), other.rearrange(r3, k=NH)
            z, cm, cs, tu = (x[:].rearrange("p t h g -> p (t h) g") for x in (sc, cum, cumsq, tau))
            V(copy, one[:], top[:, :, 0])
            V(tt, z, z, rep(one[:], 2, NH), ALU.subtract)
            r = V(tt, top, top, rep(one[:], 2, NH), ALU.subtract, own=False)
            a = A(act, other, top, ACT.Square, after=(r,), own=False)
            yield
            fl = "p r k -> p (r k)"
            V(nc.vector.tensor_tensor_scan, cm.rearrange(fl), restart[:], top.rearrange(fl), 0.0, ALU.mult, ALU.add)
            V(nc.vector.tensor_tensor_scan, cs.rearrange(fl), restart[:], other.rearrange(fl), 0.0, ALU.mult, ALU.add,
              after=(a,), own=False)
            yield
            ik = rep(inv_k[:], 1, rows)
            V(tt, tu, cm, ik, ALU.mult)
            V(tt, cm, cm, tu, ALU.mult)
            V(tt, cs, cs, cm, ALU.subtract)
            yield
            V(ts, cs, cs, -1.0, 1.0, ALU.mult, ALU.add)
            V(tt, cs, cs, ik, ALU.mult)
            r = V(ts, cs, cs, 0.0, None, ALU.max)
            a = A(act, cs, cs, ACT.Sqrt, after=(r,), own=False)
            yield
            V(tt, tu, tu, cs, ALU.subtract, after=(a,))
            V(tt, cm, tu, top, ALU.is_le)
            V(reduce, one[:], cm, AX, ALU.add)
            yield
            V(tt, cm, rep(order[:], 1, rows), rep(one[:], 2, NH), ALU.is_equal)
            V(tt, cm, cm, tu, ALU.mult)
            V(reduce, one[:], cm, AX, ALU.add)
            yield
            V(tt, z, z, rep(one[:], 2, NH), ALU.subtract)
            r = V(ts, z, z, 0.0, None, ALU.max)
            a = A(act, z, z, ACT.Square, after=(r,), own=False)
            yield
            ready = []
            for t in range(NT):
                v = qkv[:, t, 2 * D:].rearrange("p (g d) -> p d g", g=NH)
                pr = prod[t % 2][:].rearrange("p (h d g) -> p h d g", h=NH, d=HD)
                g = G(nc.gpsimd.tensor_tensor, pr, rep(sc[:, t], 2, HD), rep(v, 1, NH), ALU.mult,
                      after=(a, *ready[-2:-1]), own=False)
                ready.append(V(reduce, s_tok[:, t].rearrange("p (h d) -> p h d", h=NH), pr, AX, ALU.add,
                               after=(g,), own=False))
                c.transpose(ps[:, 0, t * P:(t + 1) * P], s_tok[:, t], after=(ready[-1], Mark(A)))
                yield
            A(nc.scalar.copy, s_T[:], bank(ps, 0), after=(Mark(E), Mark(V)), own=False)
            yield

        def moe():
            for t in range(NT):
                e = E(mm, ps[:, 1, t * E1:(t + 1) * E1], xn[:, t * P:(t + 1) * P], wr[:], start=True, stop=True, own=False)
            V(copy, lg[:], ps[:, 1, 0:NT * E1].rearrange("p (t e) -> p t e", t=NT), after=(e,))
            r = route(c, lg[:], rb, 2, True)
            yield
            for t in range(NT):
                e = c.transpose(ps[0:E1, 1, t * P:(t + 1) * P], rb["comb"][:, t], after=(r,))
            spread = A(nc.scalar.copy, combT[:], ps[0:E1, 1, :], after=(e,), own=False)
            yield
            hidden, downs = [], []
            for s in range(2 * E1 + 1):
                if s < 2 * E1:
                    e, k = s // 2, s % 2
                    b1, b3 = 2 + 2 * (s % 2), 3 + 2 * (s % 2)
                    if k == 0:
                        mk = E(mm, bank(ps, 1), pick[:, e, :], combT[:], start=True, stop=True,
                               after=(spread,), own=False)
                        spread = V(tt, xs[:, e % 2], xn[:], bank(ps, 1), ALU.mult, after=(mk,), own=False)
                    free = hidden[s - 2:s - 1]
                    g = E(mm, bank(ps, b1), w1[:, e, k * P:(k + 1) * P], xn[:], start=True, stop=True, after=free, own=False)
                    u = E(mm, bank(ps, b3), w3[:, e, k * P:(k + 1) * P], xs[:, e % 2], start=True, stop=True,
                          after=(spread,), own=False)
                    a = A(act, hid[:, s % 2], bank(ps, b1), ACT.Silu, after=(g, *downs[s - 2:s - 1]), own=False)
                    hidden.append(V(tt, hid[:, s % 2], hid[:, s % 2], bank(ps, b3), ALU.mult, after=(a, u), own=False))
                if s > 0:
                    e, k = (s - 1) // 2, (s - 1) % 2
                    downs.append(E(mm, bank(ps, 6), w2[:, k, e, :], hid[:, (s - 1) % 2], start=(s == 1),
                                   stop=(s == 2 * E1), after=(hidden[s - 1],), own=False))
                yield

        with m.loop("layer1", B) as b:
            for half in range(T // TB):
                xb = c.xT[:, bass.ds(b * T + half * TB, TB)]
                c.layernorm(xb, xn[:], tmp[:], 0)
                E.wait(V, A)
                woven((attention(half), 1), (moe(), 1))
                c.update(xb, s_T[:], bank(ps, 6), tmp[:])


DI2 = 256
DH2 = DI2 // NH
CH = P
E2, F2 = 8, 176
NTT = B * T // P


def delta_inputs(c, sb, keep):
    m, nc, ps, d = c.m, c.m.nc, c.ps, c.dram
    V, A, G, E, S = m.V, m.A, m.G, m.E, m.S
    mm, act, tt, ts, stt = (nc.tensor.matmul, nc.scalar.activation, nc.vector.tensor_tensor,
                            nc.vector.tensor_scalar, nc.vector.scalar_tensor_tensor)
    win, ones = sb([P, 800]), sb([1, P])
    b_z, b_x, b_kv, b_g = sb([P, 2]), sb([P, 2]), sb([1, 288]), sb([1, 7 * NH])
    rms_w, taps, conv_b = sb([P, 1]), sb([P, 2, 4]), sb([P, 2])
    gate_w, q_w = sb([P, 2, 7 * NH]), sb([P, 2, DI2])
    for out, name in ((win, "win2"), (b_z, "bz2"), (b_x, "bx2"), (b_kv, "bkv2"), (b_g, "bg2"), (rms_w, "rms2"),
                      (conv_b, "convb2")):
        S.dma(c.q_w, out[:], d[name])
    for out, name in ((taps, "convw2"), (gate_w, "gatew2"), (q_w, "qw2")):
        S.dma(c.q_w, out[:], d[name].rearrange("(k p) n -> p k n", p=P))
    V(nc.vector.memset, ones[:], 1.0)
    V.wait(c.q_w)
    E.wait(c.q_w, V)
    A.wait(c.q_w)
    h, ta = sb([P, TB]), sb([P, TB])
    xn = sb([P, TB])
    xg, zs, xc = sb([P, 2, 3 + TB]), sb([P, 2, TB]), sb([P, 2, TB])
    kq, sq = sb([P, NT, 2, DI2]), sb([P, NT, 2, DI2])
    norm = sb([P, NT, 2 * NH])
    with m.loop("layer2_inputs", B) as b:
        for half in range(T // TB):
            x0, t0 = b * T + half * TB, b * (T // P) + half * NT
            c.layernorm(c.xT[:, bass.ds(x0, TB)], xn[:], ta[:], 0)
            V(nc.vector.tensor_copy, keep["xn"][:, bass.ds(x0, TB)], xn[:])
            c.inverse_rms(xn[:], ta[:], 0, 1e-6)
            V(stt, h[:], xn[:], rms_w[:], ta[:], ALU.mult, ALU.mult)
            if half == 0:
                V(nc.vector.memset, xg[:, :, 0:3], 0.0)
            else:
                V(nc.vector.tensor_copy, xg[:, :, 0:3], xg[:, :, TB:TB + 3])
            for k in range(4):
                E(mm, bank(ps, k), win[:, k * P:(k + 1) * P], h[:], start=True, stop=True, after=(V, A), own=False)
            for k in range(2):
                A(act, zs[:, k], bank(ps, k), ACT.Silu, bias=b_z[:, k:k + 1], after=(E, m.queues["a"]), own=False)
            for k in range(2):
                A(act, xg[:, k, 3:], bank(ps, 2 + k), ACT.Identity, bias=b_x[:, k:k + 1], after=(V,), own=False)
            S.dma(m.queues["a"], keep["z"][:, :, bass.ds(x0, TB)], zs[:], after=(A,))
            for k in range(2):
                V(ts, xc[:, k], xg[:, k, 0:TB], taps[:, k, 0:1], conv_b[:, k:k + 1], ALU.mult, ALU.add,
                  after=(A, m.queues["b"]))
                for j in range(1, 4):
                    V(stt, xc[:, k], xg[:, k, j:j + TB], taps[:, k, j:j + 1], xc[:, k], ALU.mult, ALU.add)
            A(act, xc[:], xc[:], ACT.Silu, after=(V,))
            S.dma(m.queues["b"], keep["xconv"][:, :, bass.ds(x0, TB)], xc[:], after=(A,))
            for t in range(NT):
                ct = slice(t * P, (t + 1) * P)
                for out, rows, w_row, w_main in ((bank(ps, 4, 288), (h[:, ct],), b_kv, (win[:, 512:800],)),
                                                 (bank(ps, 5, 7 * NH), (xc[:, 0, ct], xc[:, 1, ct]), b_g,
                                                  (gate_w[:, 0], gate_w[:, 1])),
                                                 (bank(ps, 6, DI2), (xc[:, 0, ct], xc[:, 1, ct]), None,
                                                  (q_w[:, 0], q_w[:, 1]))):
                    for k, (r, w) in enumerate(zip(rows, w_main)):
                        E(mm, out, r, w, start=(k == 0), stop=(k == 1 and w_row is None), after=(A, V), own=False)
                    if w_row is not None:
                        E(mm, out, ones[:], w_row[:], start=False, stop=True, own=False)
                A(nc.scalar.copy, kq[:, t, 0], bank(ps, 4, DI2), after=(E, V), own=False)
                A(nc.scalar.copy, keep["v"][:, bass.ds(t0 + t, 1)], ps[:, 4:5, DI2:288], own=False)
                A(nc.scalar.copy, keep["gates"][:, bass.ds(t0 + t, 1)], ps[:, 5:6, 0:7 * NH], own=False)
                A(nc.scalar.copy, kq[:, t, 1], bank(ps, 6, DI2), own=False)
            A(act, sq[:], kq[:], ACT.Square)
            V(nc.vector.tensor_reduce, norm[:], sq[:].rearrange("p t k (h d) -> p t (k h) d", d=DH2), AX, ALU.add, after=(A,))
            A(act, norm[:], norm[:], ACT.Sqrt, after=(V,))
            V(ts, norm[:], norm[:], 1e-6, None, ALU.add, after=(A,))
            V(nc.vector.reciprocal, norm[:], norm[:])
            for k, name in enumerate(("k", "q")):
                V(tt, keep[name][:, bass.ds(t0, NT)].rearrange("p t (h d) -> p t h d", d=DH2),
                  kq[:, :, k].rearrange("p t (h d) -> p t h d", d=DH2), rep(norm[:, :, k * NH:(k + 1) * NH], 3, DH2),
                  ALU.mult, own=(k == 0))


def delta_gates(c, sb, keep):
    m, nc, d = c.m, c.m.nc, c.dram
    V, A, S = m.V, m.A, m.S
    act, tt, ts, stt = nc.scalar.activation, nc.vector.tensor_tensor, nc.vector.tensor_scalar, nc.vector.scalar_tensor_tensor
    t_scale, freqs = sb([P, NH]), sb([P, NH])
    S.dma(c.q_w, t_scale[:], d["ldt2"].unsqueeze(0).partition_broadcast(P))
    S.dma(c.q_w, freqs[:], d["c_freqs"])
    A(act, t_scale[:], t_scale[:], ACT.Exp, after=(c.q_w,))
    V.wait(c.q_w, A)
    alpha, omega, sel_b, sel_c, sel_dt, beta, r = (keep["gates"][:, :, j * NH:(j + 1) * NH] for j in range(7))
    decay, o_beta, cos, sin, v0, v1 = (keep["g"][:, j] for j in range(6))
    t1, t2, dt, det = (sb([P, NTT, NH])[:] for _ in range(4))

    def softplus(out, x):
        V(stt, t1, x, -1.0, x, ALU.mult, ALU.max)
        A(act, t1, t1, ACT.Exp, scale=-1.0, after=(V,))
        A(act, t1, t1, ACT.Ln, bias=c.one[:])
        V(stt, out, x, 0.0, t1, ALU.max, ALU.add, after=(A,))

    softplus(dt, sel_dt)
    V(tt, dt, dt, rep(t_scale[:], 1, NTT), ALU.mult)
    V(ts, dt, dt, 1e-4, 0.5, ALU.add, ALU.mult)
    softplus(t2, alpha)
    V(tt, alpha, t2, dt, ALU.mult)
    A(act, omega, omega, ACT.Tanh, after=(V,))
    A(act, sel_b, sel_b, ACT.Sigmoid)
    A(act, keep["sel_c"][:], sel_c, ACT.Sigmoid)
    A(act, o_beta, beta, ACT.Sigmoid)
    A(act, r, r, ACT.Sigmoid)
    V(ts, omega, omega, 1.0, None, ALU.add, after=(A,))
    V(tt, omega, omega, rep(freqs[:], 1, NTT), ALU.mult)
    V(tt, omega, omega, dt, ALU.mult)
    V(tt, t2, omega, omega, ALU.mult)
    V(ts, det, alpha, 1.0, None, ALU.add)
    V(tt, det, det, det, ALU.mult)
    V(tt, det, det, t2, ALU.add)
    V(nc.vector.reciprocal, det, det)
    V(tt, t1, alpha, alpha, ALU.mult)
    V(tt, t1, t1, t2, ALU.add)
    V(ts, t1, t1, -1.0, 1.0, ALU.mult, ALU.add)
    V(tt, cos, t1, det, ALU.mult)
    V(stt, sin, omega, 2.0, det, ALU.mult, ALU.mult)
    V(tt, t1, cos, cos, ALU.mult)
    V(tt, t2, sin, sin, ALU.mult)
    V(tt, t1, t1, t2, ALU.add)
    V(ts, det, t1, 0.0, None, ALU.is_equal)
    V(ts, t1, t1, 1e-32, None, ALU.max)
    A(act, t1, t1, ACT.Sqrt, after=(V,))
    V(nc.vector.reciprocal, t2, t1, after=(A,))
    V(tt, cos, cos, t2, ALU.mult)
    V(tt, cos, cos, det, ALU.add)
    V(tt, sin, sin, t2, ALU.mult)
    V(ts, t1, t1, 1e-8, 1.0, ALU.max, ALU.min)
    A(act, t1, t1, ACT.Ln, after=(V,))
    V(stt, t1, t1, 8.0, r, ALU.mult, ALU.mult, after=(A,))
    A(act, decay, t1, ACT.Exp, after=(V,))
    V(tt, t1, decay, decay, ALU.mult, after=(A,))
    V(ts, t1, t1, -1.0, 1.0, ALU.mult, ALU.add)
    V(ts, t1, t1, 0.0, 1.0, ALU.max, ALU.min)
    V(ts, t1, t1, 1e-6, None, ALU.add)
    A(act, t1, t1, ACT.Sqrt, after=(V,))
    V(tt, t1, t1, sel_b, ALU.mult, after=(A,))
    vv = keep["v"][:].rearrange("p t (h s) -> p t h s", s=2)
    V(tt, v0, vv[:, :, :, 0], t1, ALU.mult)
    V(tt, v1, vv[:, :, :, 1], t1, ALU.mult, own=False)


def delta_recurrence(c, sb, keep):
    m, nc, ps, d = c.m, c.m.nc, c.ps, c.dram
    V, A, G, E, S = m.V, m.A, m.G, m.E, m.S
    act, tt, ts, stt = nc.scalar.activation, nc.vector.tensor_tensor, nc.vector.tensor_scalar, nc.vector.scalar_tensor_tensor
    gtt, gts, gcopy = nc.gpsimd.tensor_tensor, nc.gpsimd.tensor_scalar, nc.gpsimd.tensor_copy
    kst, qst = sb([P, 2, B, NH, DH2]), sb([P, 2, B, NH, DH2])
    gst = sb([P, 6, 2, B, NH])
    kc, qc, nb = (sb([P, CH, DH2]) for _ in range(3))
    yc = sb([P, 1 + CH, DH2])
    g = sb([P, 6, CH])
    turn, turn2, ta, tb = (sb([P, 2, CH]) for _ in range(4))
    carry = sb([P, 2])
    w, wt, nbm, u, scaled = sb([P, CH]), sb([P, 2, CH]), sb([P, CH]), sb([P, CH]), sb([P, DH2])
    product = sb([P, DH2])
    ret = sb([P, CH])
    tok, cs_tok, rt, ro = sb([P, 2, B, NH]), sb([P, 2, B, NH]), sb([P, 2, B, NH]), sb([P, B, NH, 2])
    sel = sb([P, B, NH])
    V(nc.vector.memset, yc[:, 0, :], 0.0)
    V(nc.vector.memset, carry[:, 0:1], 1.0)
    V(nc.vector.memset, carry[:, 1:2], 0.0)
    H = P // 2
    nt = T // P
    m.barrier()
    with m.loop("layer2_recurrence", nt) as i:
        def tile_of(x):
            return x.rearrange("p (b t) n -> p b t n", b=B)[:, :, bass.ds(i, 1), :].squeeze(2)

        for s in range(2):
            for st, name in ((kst, "k"), (qst, "q")):
                G(gcopy, st[:, s].rearrange("p b h d -> p b (h d)"), tile_of(keep[name][:]), after=(E,), own=False)
            for j in range(6):
                A(nc.scalar.copy, gst[:, j, s], tile_of(keep["g"][:, j]), after=(E, V), own=False)
        V(nc.vector.tensor_copy, sel[:], tile_of(keep["sel_c"][:]))
        for j in range(6):
            c.transpose(ps[:, j // 4, (j % 4) * P:(j % 4 + 1) * P], gst[:, j].rearrange("p s b h -> p (s b h)"), after=(A, V, G))
        A(nc.scalar.copy, g[:, 0:4].rearrange("p j t -> p (j t)"), bank(ps, 0), after=(E, V, G))
        A(nc.scalar.copy, g[:, 4:6].rearrange("p j t -> p (j t)"), bank(ps, 1, 2 * P), own=False)
        for q, (st, out) in enumerate(((kst, kc), (qst, qc))):
            for d0 in range(0, DH2, 4):
                bk = 2 + (d0 // 4) % 4
                for dd in range(4):
                    c.transpose(ps[:, bk, dd * P:(dd + 1) * P], st[:, :, :, :, d0 + dd].rearrange("p s b h -> p (s b h)"),
                                after=(G, A))
                A(nc.scalar.copy, out[:, :, d0:d0 + 4].rearrange("p t d -> p d t"),
                  bank(ps, bk).rearrange("p (d t) -> p d t", d=4), after=(E, V), own=False)
        G(gcopy, turn[:], g[:, 2:4], after=(A,))
        a, b2 = turn, turn2
        sh = 1
        while sh < CH:
            G(gcopy, b2[:, :, 0:sh], a[:, :, 0:sh])
            G(gtt, ta[:, :, sh:], a[:, :, sh:], rep(a[:, 0, 0:CH - sh], 1, 2), ALU.mult, own=False)
            G(gtt, tb[:, :, sh:], a[:, ::-1, sh:], rep(a[:, 1, 0:CH - sh], 1, 2), ALU.mult, own=False)
            G(gtt, b2[:, 0, sh:], ta[:, 0, sh:], tb[:, 0, sh:], ALU.subtract)
            G(gtt, b2[:, 1, sh:], ta[:, 1, sh:], tb[:, 1, sh:], ALU.add, own=False)
            a, b2 = b2, a
            sh *= 2
        G(gts, ta[:], a[:], carry[:, 0:1], None, ALU.mult)
        G(gts, tb[:], a[:, ::-1], carry[:, 1:2], None, ALU.mult, own=False)
        G(gtt, a[:, 0], ta[:, 0], tb[:, 0], ALU.subtract)
        G(gtt, a[:, 1], ta[:, 1], tb[:, 1], ALU.add)
        G(gcopy, carry[:], a[:, :, CH - 1])
        cum = a
        for lo, ci, si in ((0, 0, 1), (H, 1, 0)):
            hp = slice(lo, lo + H)
            V(tt, wt[hp, 0], g[hp, 4], cum[hp, ci], ALU.mult, after=(G, A), own=False)
            V(tt, wt[hp, 1], g[hp, 5], cum[hp, si], ALU.mult, own=False)
            V(tt, w[hp], wt[hp, 0], wt[hp, 1], ALU.subtract if lo == 0 else ALU.add)
        V(tt, w[:], w[:], g[:, 1], ALU.mult)
        V(stt, nbm[:], g[:, 0], -1.0, g[:, 1], ALU.mult, ALU.mult)
        V(tt, nb[:], kc[:], rep(nbm[:], 2, DH2), ALU.mult)
        for t in range(CH):
            V(nc.vector.tensor_tensor_reduce, product[:], yc[:, t], nb[:, t], 1.0, w[:, t:t + 1],
              ALU.mult, ALU.add, u[:, t:t + 1])
            V(ts, scaled[:], yc[:, t], g[:, 0, t:t + 1], None, ALU.mult, own=False)
            V(stt, yc[:, t + 1], kc[:, t], u[:, t:t + 1], scaled[:], ALU.mult, ALU.add)
        V(nc.vector.tensor_copy, yc[:, 0], yc[:, CH])
        V(tt, nb[:], yc[:, 1:], qc[:], ALU.mult, own=False)
        V(nc.vector.tensor_reduce, ret[:], nb[:], AX, ALU.add)
        c.transpose(ps[:, 6, 0:P], ret[:], after=(V, A))
        for k in range(2):
            c.transpose(ps[:, 6, (1 + k) * P:(2 + k) * P], cum[:, k], after=(G,))
        A(nc.scalar.copy, tok[:].rearrange("p s b h -> p (s b h)"), ps[:, 6, 0:P], after=(E, V))
        for k in range(2):
            A(nc.scalar.copy, cs_tok[:, k].rearrange("p b h -> p (b h)"), ps[:, 6, (1 + k) * P:(1 + k) * P + H], own=False)
        re, im, co, si = tok[:, 0], tok[:, 1], cs_tok[:, 0], cs_tok[:, 1]
        for s, (x, y, op) in enumerate((((re, co), (im, si), ALU.add), ((im, co), (re, si), ALU.subtract))):
            V(tt, rt[:, 0], x[0], x[1], ALU.mult, after=(A,))
            V(tt, rt[:, 1], y[0], y[1], ALU.mult, own=False)
            V(tt, rt[:, 0], rt[:, 0], rt[:, 1], op)
            V(tt, ro[:, :, :, s], rt[:, 0], sel[:], ALU.mult, after=(E,))
        for b in range(B):
            c.transpose(ps[0:2 * NH, 7, b * P:(b + 1) * P], ro[:, b].rearrange("p h s -> p (h s)"), after=(V, A))
        A(nc.scalar.copy, keep["ret"][:].rearrange("p b t -> p b t")[:, :, bass.ds(i * P, P)],
          ps[0:2 * NH, 7].rearrange("p (b t) -> p b t", b=B), after=(E,), own=False)


def delta_outputs(c, sb, keep):
    m, nc, ps, d = c.m, c.m.nc, c.ps, c.dram
    V, A, G, E, S = m.V, m.A, m.G, m.E, m.S
    mm, act, tt, ts, stt = (nc.tensor.matmul, nc.scalar.activation, nc.vector.tensor_tensor,
                            nc.vector.tensor_scalar, nc.vector.scalar_tensor_tensor)
    copy = nc.vector.tensor_copy
    F = (P, F2 - P)
    read_w, group, out_w = sb([2 * NH, DI2]), sb([P, P]), sb([P, 2, D])
    gn_w, gn_b, dp = sb([P, 2]), sb([P, 2]), sb([P, 2])
    wr, ebias, pick = sb([P, E2]), sb([P, E2]), sb([E2, E2, P])
    up, down = sb([P, E2, F2], BF16), sb([P, 2, E2, D], BF16)
    sup, sdown = sb([P, F2]), sb([P, 2, D])
    rb = route_buffers(sb, E2)
    for out, name in ((read_w, "readw2"), (group, "c_group"), (gn_w, "gnw2"), (gn_b, "gnb2"), (dp, "dp2"), (wr, "wr2"),
                      (pick, "c_pick"), (sup, "sup2")):
        S.dma(c.q_w, out[:], d[name])
    S.dma(c.q_w, rb["lower"], d["c_lower"])
    S.dma(c.q_w, out_w[:], d["outw2"].rearrange("(k p) n -> p k n", p=P))
    S.dma(c.q_w, ebias[:], d["eb2"].unsqueeze(0).partition_broadcast(P))
    S.dma(c.q_w, sdown[0:F[0], 0], d["sdown2"][0:P, :])
    S.dma(c.q_w, sdown[0:F[1], 1], d["sdown2"][P:F2, :])
    with m.scope() as tmp:
        f_up, f_down = tmp([P, E2, F2]), tmp([P, 2, E2, D])
        S.dma(c.q_w, f_up[:], d["up2"])
        S.dma(c.q_w, f_down[0:F[0], 0], d["down2"][0:P])
        S.dma(c.q_w, f_down[0:F[1], 1], d["down2"][P:F2])
        V(copy, up[:], f_up[:], after=(c.q_w,))
        V(copy, down[0:F[0], 0], f_down[0:F[0], 0])
        V(copy, down[0:F[1], 1], f_down[0:F[1], 1])
    zx = sb([P, 2, 2, T])
    y = sb([P, 2, T])
    sq = sb([P, TB])
    sums, stat, ab = sb([P, 2, 2]), sb([P, 2, 2]), sb([P, 2, 2])
    xn, s_T, tmp_ = sb([P, TB]), sb([P, TB]), sb([P, TB])
    lg, combT = sb([P, NT, E2]), sb([E2, TB])
    xs, hid, rounded = sb([P, 2, TB], BF16), sb([P, 2, 2, TB], BF16), sb([P, TB], BF16)
    hs, acc = sb([P, 2, TB]), sb([P, TB])
    m.barrier()
    with m.loop("layer2_outputs", B) as b:
        S.dma(m.queues["a"], zx[:, 0], keep["z"][:, :, bass.ds(b * T, T)], after=(V,))
        S.dma(m.queues["b"], zx[:, 1], keep["xconv"][:, :, bass.ds(b * T, T)])
        for k in range(2):
            for half in range(2):
                bk = 2 * k + half
                E(mm, bank(ps, bk), read_w[:, k * P:(k + 1) * P],
                  keep["ret"][:, bass.ds(b, 1), half * TB:half * TB + TB].squeeze(1),
                  start=True, stop=True, after=(A, V), own=False, apart=True)
                A(act, y[:, k, half * TB:half * TB + TB], bank(ps, bk), ACT.Copy, accum_out=sums[:, k, half:half + 1],
                  after=(E, V), own=False)
        V(tt, stat[:, 0], sums[:, :, 0], sums[:, :, 1], ALU.add, after=(A,))
        E(mm, ps[:, 4, 0:2], group[:], stat[:, 0], start=True, stop=True, after=(V,))
        V(ts, ab[:, 1], ps[:, 4, 0:2], -1.0, None, ALU.mult, after=(E,))
        for k in range(2):
            for half in range(2):
                A(act, sq[:], y[:, k, half * TB:half * TB + TB], ACT.Square, bias=ab[:, 1, k:k + 1],
                  accum_out=sums[:, k, half:half + 1], after=(V,))
        V(tt, stat[:, 1], sums[:, :, 0], sums[:, :, 1], ALU.add, after=(A,))
        E(mm, ps[:, 4, 0:2], group[:], stat[:, 1], start=True, stop=True, after=(V,))
        A(act, stat[:, 0], ps[:, 4, 0:2], ACT.Sqrt, bias=c.eps[1e-5][:], after=(E,))
        V(nc.vector.reciprocal, stat[:, 0], stat[:, 0], after=(A,))
        V(tt, ab[:, 0], stat[:, 0], gn_w[:], ALU.mult)
        V(tt, stat[:, 1], ab[:, 1], ab[:, 0], ALU.mult)
        V(tt, stat[:, 1], stat[:, 1], gn_b[:], ALU.add)
        for k in range(2):
            V(ts, y[:, k], y[:, k], ab[:, 0, k:k + 1], stat[:, 1, k:k + 1], ALU.mult, ALU.add)
            V(tt, y[:, k], y[:, k], zx[:, 0, k], ALU.mult, after=(m.queues["a"],))
            V(stt, y[:, k], zx[:, 1, k], dp[:, k:k + 1], y[:, k], ALU.mult, ALU.add, after=(m.queues["b"],))
        for half in range(T // TB):
            hs_ = slice(half * TB, half * TB + TB)
            xb = c.xT[:, bass.ds(b * T + half * TB, TB)]
            V(copy, xn[:], keep["xn"][:, bass.ds(b * T + half * TB, TB)], after=(E,))
            for k in range(2):
                E(mm, bank(ps, 0), out_w[:, k], y[:, k, hs_], start=(k == 0), stop=(k == 1), after=(V, A), own=False)
            V(tt, s_T[:], xn[:], bank(ps, 0), ALU.add, after=(E,))
            for t in range(NT):
                E(mm, ps[:, 1, t * E2:(t + 1) * E2], xn[:, t * P:(t + 1) * P], wr[:], start=True, stop=True, own=False)
            A(act, rb["score"], ps[:, 1, 0:NT * E2].rearrange("p (t e) -> p t e", t=NT), ACT.Sigmoid, after=(E, V))
            V(tt, lg[:], rb["score"], rep(ebias[:], 1, NT), ALU.add, after=(A,))
            route(c, lg[:], rb, 2, False)
            for t in range(NT):
                c.transpose(ps[0:E2, 1, t * P:(t + 1) * P], rb["comb"][:, t], after=(V,))
            A(nc.scalar.copy, combT[:], ps[0:E2, 1, :], after=(E,))
            for k in range(2):
                E(mm, ps[0:F[k], 2 + k, :], sup[:, k * P:k * P + F[k]], xn[:], start=True, stop=True, after=(V, A), own=False)
                A(act, hs[0:F[k], k], ps[0:F[k], 2 + k, :], ACT.Relu, after=(E, V), own=False)
                V(tt, hs[0:F[k], k], hs[0:F[k], k], hs[0:F[k], k], ALU.mult, after=(A,), own=False)
                E(mm, bank(ps, 6), sdown[0:F[k], k], hs[0:F[k], k], start=(k == 0), stop=(k == 1), after=(V,), own=False)
            V(copy, acc[:], bank(ps, 6), after=(E,))
            for e in range(E2):
                E(mm, bank(ps, 1), pick[:, e, :], combT[:], start=True, stop=True, after=(A, V), own=False)
                V(tt, xs[:, e % 2], xn[:], bank(ps, 1), ALU.mult, after=(E,), own=False)
                for k in range(2):
                    E(mm, ps[0:F[k], 2 + k, :], up[:, e, k * P:k * P + F[k]], xs[:, e % 2], start=True, stop=True,
                      after=(V, A), own=False)
                    A(act, hid[0:F[k], e % 2, k], ps[0:F[k], 2 + k, :], ACT.Relu, after=(E, V), own=False)
                    V(tt, hid[0:F[k], e % 2, k], hid[0:F[k], e % 2, k], hid[0:F[k], e % 2, k], ALU.mult, after=(A,), own=False)
                for k in range(2):
                    E(mm, bank(ps, 4), down[0:F[k], k, e], hid[0:F[k], e % 2, k], start=(k == 0), stop=(k == 1), after=(V,), own=False)
                A(nc.scalar.copy, rounded[:], bank(ps, 4), after=(E, V), own=False)
                V(tt, acc[:], acc[:], rounded[:], ALU.add, after=(A,))
            c.update(xb, s_T[:], acc[:], tmp_[:])


def layer2(c):
    m, nc = c.m, c.m.nc
    with m.scope() as sb:
        keep = {"xn": sb([P, B * T]), "ret": sb([2 * NH, B, T]), 
                "z": nc.dram_tensor("z_scratch", (P, 2, B * T), F32, kind="Internal").ap(),
                "xconv": nc.dram_tensor("xconv_scratch", (P, 2, B * T), F32, kind="Internal").ap()}
        with m.scope() as tmp:
            keep.update(k=tmp([P, NTT, DI2]), q=tmp([P, NTT, DI2]), g=tmp([P, 6, NTT, NH]), sel_c=tmp([P, NTT, NH]))
            with m.scope() as tmp2:
                keep.update(v=tmp2([P, NTT, 2 * NH]), gates=tmp2([P, NTT, 7 * NH]))
                with m.scope() as inner:
                    delta_inputs(c, inner, keep)
                with m.scope() as inner:
                    delta_gates(c, inner, keep)
            with m.scope() as inner:
                delta_recurrence(c, inner, keep)
        with m.scope() as inner:
            delta_outputs(c, inner, keep)


PAD = 32
NG = NH * PAD // P
JG = P // PAD
REL = 256
QW = REL + P
NI = T // P
F3 = 384


def relative_attention(c, sb, keep):
    m, nc, ps, d = c.m, c.m.nc, c.ps, c.dram
    V, A, G, E, S = m.V, m.A, m.G, m.E, m.S
    mm, act, tt, ts, stt = (nc.tensor.matmul, nc.scalar.activation, nc.vector.tensor_tensor,
                            nc.vector.tensor_scalar, nc.vector.scalar_tensor_tensor)
    scale = HD ** -0.5
    n_units = JG * NI
    scratch = nc.dram_tensor("relative_scratch", (n_units, P, QW), F32, kind="Internal").ap()
    shifted = bass.AP(tensor=scratch.tensor, offset=P, ap=[[QW - 1, P], [P * QW, n_units], [1, REL]])
    wq, wk, wv, rel = sb([P, P]), sb([P, P]), sb([P, JG * HD]), sb([P, REL])
    row0 = sb([P, 1])
    within, neg = sb([P, P]), sb([P, P], BF16)
    ident_b = sb([P, P], BF16)
    x, q, k = sb([P, T]), sb([P, 1 + T]), sb([P, T])
    v = sb([P, NI, JG * HD])
    qr = [sb([P, QW]) for _ in range(2)]
    cs = sb([P, n_units, REL])
    far, two = sb([P, JG, NI - 4, P]), sb([P, JG, NI - 2, P])
    other = sb([P, P])
    s = [sb([P, T]) for _ in range(2)]
    pt = [sb([P, NI, P]) for _ in range(2)]
    mx, nmax, total, inv = (sb([P, n_units, 3]) for _ in range(4))
    att = sb([P, NI, JG * HD])
    S.dma(c.q_w, within[:], d["c_within"])
    V(nc.vector.tensor_scalar, neg[:], within[:], -1e9, None, ALU.mult, after=(c.q_w,))
    V(ts, other[:], c.ident[:], -1.0, 1.0, ALU.mult, ALU.add)
    V(nc.vector.memset, q[:, 0:1], 0.0)
    V(nc.vector.tensor_copy, ident_b[:], c.ident[:])
    m.barrier()
    q_in, q_out, q_back = m.queues["a"], (m.queues["b"], m.queues["d"]), m.queues["c"]
    with m.loop("layer3_attention", B, NG) as (b, g):
        for out, name in ((wq, "wq3"), (wk, "wk3"), (wv, "wv3"), (rel, "rel3")):
            S.dma(q_in, out[:], d[name][bass.ds(g, 1)].squeeze(0), after=(E, V, A))
        A(nc.scalar.copy, x[:], keep["xn"][:, bass.ds(b * T, T)], after=(E, V))
        V(nc.vector.tensor_copy, row0[:], rel[:, 0:1], after=(q_in,))
        V(ts, rel[:], rel[:], row0[:], None, ALU.subtract)
        V(ts, rel[:, 0:1], row0[:], -1.0, None, ALU.mult)
        for half in range(T // TB):
            h = slice(half * TB, half * TB + TB)
            E(mm, bank(ps, 2 * half), wq[:], x[:, h], start=True, stop=True, after=(A, V, q_in), own=False)
            E(mm, bank(ps, 2 * half + 1), wk[:], x[:, h], start=True, stop=True, own=False)
            A(act, q[:, 1 + half * TB:1 + half * TB + TB], bank(ps, 2 * half), ACT.Copy, scale=scale, after=(E, V), own=False)
            A(nc.scalar.copy, k[:, h], bank(ps, 2 * half + 1), own=False)
        for t in range(NI):
            e = E(mm, ps[:, 4, t * JG * HD:(t + 1) * JG * HD], x[:, t * P:(t + 1) * P], wv[:], start=True, stop=True, own=False)
        A(nc.scalar.copy, v[:].rearrange("p t n -> p (t n)"), bank(ps, 4, NI * JG * HD), after=(E,), own=False)
        units = [(j, i) for j in range(JG) for i in range(NI)]
        written = []
        for u, (j, i) in enumerate(units):
            r = slice(j * PAD, j * PAD + HD)
            buf, bk = qr[u % 2], 5 + u % 2
            e = E(mm, bank(ps, bk, REL), q[r, i * P:(i + 1) * P], rel[r, :], start=True, stop=True, after=(A, V), own=False)
            a = A(nc.scalar.copy, buf[:, 0:REL], bank(ps, bk, REL), after=(e, *written[-2:-1]), own=False)
            a = V(nc.vector.tensor_copy, buf[:, REL:QW], buf[:, 0:P], after=(a,), own=False)
            written.append(S.dma(q_out[u % 2], scratch[u], buf[:], after=(a, A, q_back)))
        S.dma(q_back, cs[:], shifted, after=(*q_out, V, G))

        own = cs[:, :, P:].rearrange("p (j i) z -> p j i z", j=JG)
        for j in range(JG):
            G(nc.gpsimd.tensor_tensor, two[:, j], own[:, j, 2:], rep(other[:], 1, NI - 2), ALU.mult, after=(q_back, V), own=False)
            tiles_ready = G(nc.gpsimd.tensor_tensor, far[:, j], own[:, j, 4:], rep(within[:], 1, NI - 4), ALU.mult, own=False)
        scored, expd, done, turned = [], [], [], []

        def scores(u):
            j, i = units[u]
            r = slice(j * PAD, j * PAD + HD)
            n = (i + 1) * P
            b0 = 2 * (u % 2)
            for lo in range(0, n, TB):
                hi = min(n, lo + TB)
                last = hi == n
                E(mm, ps[:, b0 + lo // TB, 0:hi - lo], q[r, 1 + i * P:1 + (i + 1) * P], k[r, lo:hi], start=True, stop=not last,
                  after=tuple(done[u - 2:u - 1]) + ((Mark(A), Mark(V)) if u < 2 else ()), own=False)
            e = E(mm, ps[:, b0 + i // 4, (i % 4) * P:(i % 4 + 1) * P], ident_b[:], neg[:], start=False, stop=True, own=False)
            scored.append(e)

        def add(u):
            j, i = units[u]
            b0 = 2 * (u % 2)
            out, rows = s[u % 2], ps[:, b0:b0 + 2, :].rearrange("p b n -> p (b n)")
            after = (scored[u], m.queues["c"], *turned[u - 2:u - 1])
            V.wait(*after, tiles_ready)
            parts = [(i - 1, i + 1, cs[:, u, :]) if i else (0, 1, cs[:, u, P:])]
            if i >= 2:
                parts.append((i - 2, i - 1, two[:, j, i - 2]))
            if i >= 3:
                parts.append((i - 3, i - 2, cs[:, u, 0:P]))
            if i >= 4:
                parts.append((i - 4, i - 3, far[:, j, i - 4]))
            for lo, hi, bias in parts:
                V(tt, out[:, lo * P:hi * P], rows[:, lo * P:hi * P], bias, ALU.add, own=False)
            if i > 4:
                V(nc.vector.tensor_copy, out[:, 0:(i - 4) * P], rows[:, 0:(i - 4) * P], own=False)
            done.append(Mark(V))
            V(nc.vector.tensor_reduce, mx[:, u, 0:1], out[:, 0:(i + 1) * P], AX, ALU.max)
            V(ts, nmax[:, u, 0:1], mx[:, u, 0:1], -1.0, None, ALU.mult)
            e = Mark(V)
            expd.append(A(act, out[:, 0:(i + 1) * P], out[:, 0:(i + 1) * P], ACT.Exp, bias=nmax[:, u, 0:1],
                          accum_out=total[:, u, 0:1], after=(e,), own=False))

        def attend(u):
            j, i = units[u]
            src, dst = s[u % 2], pt[u % 2]
            for lo in range(0, i + 1, 4):
                hi = min(i + 1, lo + 4)
                bk = 4 + (lo // 4)
                for t in range(lo, hi):
                    e = c.transpose(ps[:, bk, (t - lo) * P:(t - lo + 1) * P], src[:, t * P:(t + 1) * P],
                                    after=(expd[u], Mark(A), Mark(V)) if t == lo else ())
                A(nc.scalar.copy, dst[:, lo:hi].rearrange("p t n -> p (t n)"), bank(ps, bk, (hi - lo) * P), after=(e, Mark(E)), own=False)
            turned.append(e)
            a = Mark(A)
            o = ps[:, 6 + u % 2, 0:HD]
            for t in range(i + 1):
                e = E(mm, o, dst[:, t, :], v[:, t, j * HD:(j + 1) * HD], start=(t == 0), stop=(t == i), after=(a,), own=False)
            V(nc.vector.reciprocal, inv[:, u, 0:1], total[:, u, 0:1], after=(expd[u], e))
            V(ts, att[:, i, j * HD:(j + 1) * HD], o, inv[:, u, 0:1], None, ALU.mult)

        E.wait(A, V)
        for u in range(n_units + 2):
            if u < n_units:
                scores(u)
            if 1 <= u <= n_units:
                add(u - 1)
            if u >= 2:
                attend(u - 2)
        V(nc.vector.tensor_copy, keep["att"][:, bass.ds(b * NI, NI), bass.ds(g * JG * HD, JG * HD)], att[:])


def layer3(c):
    m, nc, ps, d = c.m, c.m.nc, c.ps, c.dram
    V, A, G, E, S = m.V, m.A, m.G, m.E, m.S
    mm, act, tt, ts = nc.tensor.matmul, nc.scalar.activation, nc.vector.tensor_tensor, nc.vector.tensor_scalar
    with m.scope() as sb:
        keep = {"xn": sb([P, B * T]), "att": sb([P, NTT, D])}
        with m.scope() as tmp:
            xn, ta = tmp([P, TB]), tmp([P, TB])
            with m.loop("layer3_norm", B * T // TB) as n:
                c.layernorm(c.xT[:, bass.ds(n * TB, TB)], xn[:], ta[:], 0)
                V(nc.vector.tensor_copy, keep["xn"][:, bass.ds(n * TB, TB)], xn[:])
        with m.scope() as tmp:
            relative_attention(c, tmp, keep)
        wp, bp = sb([P, D]), sb([P, 1])
        wg, wu, wd = sb([P, F3]), sb([P, F3]), sb([P, F3 // P, D])
        with m.scope() as tmp:
            ints = tmp([P, 3, F3], I32)
            S.dma(c.q_w, wp[:], d["wp3"])
            S.dma(c.q_w, bp[:], d["bp3"])
            S.dma(c.q_w, ints[:, 0], d["gate3"])
            S.dma(c.q_w, ints[:, 1], d["up3"])
            S.dma(c.q_w, ints[:, 2].rearrange("p (k n) -> p k n", k=3), d["down3"].rearrange("(k p) n -> p k n", p=P))
            for k, w in enumerate((wg[:], wu[:], wd[:].rearrange("p k n -> p (k n)"))):
                V(ts, w, ints[:, k], 1.0 / 127.0, None, ALU.mult, after=(c.q_w,))
        att, aT, sT, xn, hid, tmp_ = sb([P, NT, D]), sb([P, TB]), sb([P, TB]), sb([P, TB]), sb([P, 3, TB]), sb([P, TB])
        with m.loop("layer3_ffn", B * T // TB) as n:
            V(nc.vector.tensor_copy, att[:], keep["att"][:, bass.ds(n * NT, NT)], after=(E,))
            V(nc.vector.tensor_copy, xn[:], keep["xn"][:, bass.ds(n * TB, TB)])
            for t in range(NT):
                c.transpose(ps[:, 0, t * P:(t + 1) * P], att[:, t], after=(V, A))
            A(nc.scalar.copy, aT[:], bank(ps, 0), after=(E,))
            E(mm, bank(ps, 1), wp[:], aT[:], start=True, stop=True, after=(A,))
            A(act, sT[:], bank(ps, 1), ACT.Identity, bias=bp[:], after=(E, V))
            for k in range(3):
                b1, b2 = 2 + 2 * (k % 2), 3 + 2 * (k % 2)
                E(mm, bank(ps, b1), wg[:, k * P:(k + 1) * P], xn[:], start=True, stop=True, after=(V, A), own=False)
                E(mm, bank(ps, b2), wu[:, k * P:(k + 1) * P], xn[:], start=True, stop=True, own=False)
                A(act, hid[:, k], bank(ps, b1), ACT.Silu, after=(E, V), own=False)
                V(tt, hid[:, k], hid[:, k], bank(ps, b2), ALU.mult, after=(A,), own=False)
            for k in range(3):
                E(mm, bank(ps, 6), wd[:, k], hid[:, k], start=(k == 0), stop=(k == 2), after=(V,), own=False)
            c.update(c.xT[:, bass.ds(n * TB, TB)], sT[:], bank(ps, 6), tmp_[:])


LAYERS = (0, 1, 2, 3)


def program(nc, dram, out, per_iteration):
    m = Machine(nc, per_iteration)
    c = Common(m, dram)
    c.load_start()
    for k in LAYERS:
        (layer0, layer1, layer2, layer3)[k](c)
    m.barrier()
    m.S.dma(m.queues["out"], out, c.xT[:], after=(m.V,))
    m.S.wait(m.queues["out"])
    m.barrier()
    return m.learned


def constants():
    inv = (1.0 / 10000.0 ** (np.arange(0, 8, 2, dtype=np.float32) / 8)).astype(np.float32)
    f = np.arange(T, dtype=np.float32)[:, None] * inv[None, :]
    cos, sin = np.cos(f).T, np.sin(f).T
    i = np.arange(P)
    out = {
        "c_ident": np.eye(P),
        "c_upper": i[:, None] <= i[None, :],
        "c_cos": np.tile(cos, (32, 1)),
        "c_sin": np.tile(np.concatenate([-sin, sin]), (16, 1)),
        "c_blocks": i[:, None] // HD == i[None, :] // HD,
        "c_before": i[:, None] < i[None, :],
        "c_order": np.tile(np.arange(1, NH + 1), (P, 1)),
        "c_inv_k": np.tile(1.0 / np.arange(1, NH + 1), (P, 1)),
        "c_restart": np.tile(np.arange(NT * NH * NH) % NH != 0, (P, 1)),
        "c_pick": np.repeat(np.eye(E1)[:, :, None], P, 2),
        "c_freqs": np.tile(1.0 / 10000.0 ** (np.arange(NH, dtype=np.float32) / NH), (P, 1)),
        "c_group": (i[:, None] // DH2 == i[None, :] // DH2) / (DH2 * T),
        "c_within": i[None, :] > i[:, None],
        "c_lower": np.tile(np.arange(E1)[None, :] < np.arange(E1)[:, None], (P, 1, 1)),
    }
    return {k: np.ascontiguousarray(v, dtype=np.float32) for k, v in out.items()}


def laid_out(i):
    def columns(v):
        return v.reshape(-1, P).T

    def grouped(w, axis):
        w = np.moveaxis(w, axis, 0).reshape(NG, JG, HD, -1)
        out = np.zeros((NG, JG, PAD, w.shape[-1]), w.dtype)
        out[:, :, :HD] = w
        return out.reshape(NG, P, -1)

    partner = np.arange(D).reshape(16, 2, 4)[:, ::-1].reshape(-1)
    wq, zx = i["L0_attn_W_in"][:D], i["L0_attn_W_zxbcdt"]
    a = {
        "xT": i["L0_attn_x"].reshape(B * T, D).T,
        "wq": wq.T, "wqr": wq[partner].T,
        "wz": zx[:DI0].T, "wxbc": zx[DI0:DI0 + 2 * DI0].T, "wdt": zx[3 * DI0:].T,
        "convw0": i["L0_attn_conv_w"].T, "convb0": columns(i["L0_attn_conv_b"]), "dtb": i["L0_attn_dt_bias"],
        "alog": i["L0_attn_A_log"], "D0": columns(np.repeat(i["L0_attn_D_param"], HP)), "npre": columns(i["L0_attn_norm_pre_w"]),
        "ngat": columns(i["L0_attn_norm_gated_w"]), "wout0": i["L0_attn_W_out"].T,
        "fg0": i["L0_ffn_w_gate"], "fu0": i["L0_ffn_w_up"], "fd0": i["L0_ffn_w_down"],
    }
    a.update({
        "wqkv1": np.concatenate([np.tile(i["L1_attn_W" + k].T, (NH, NH)) for k in "qkv"], 1),
        "bqkv1": np.concatenate([np.tile(i["L1_attn_b" + k], NH) for k in "qkv"])[None, :],
        "wr1": i["L1_ffn_router_w"], "w1": i["L1_ffn_w1"], "w3": i["L1_ffn_w3"], "w2": i["L1_ffn_w2"],
    })
    a.update({
        "win2": i["L2_attn_in_proj_w"], "bz2": columns(i["L2_attn_in_proj_b"][:DI2]),
        "bx2": columns(i["L2_attn_in_proj_b"][DI2:2 * DI2]), "bkv2": i["L2_attn_in_proj_b"][None, 2 * DI2:],
        "bg2": i["L2_attn_gate_b"][None, :], "rms2": columns(i["L2_attn_rms_w"]), "convw2": i["L2_attn_conv_w"],
        "convb2": columns(i["L2_attn_conv_b"]), "gatew2": i["L2_attn_gate_w"], "qw2": i["L2_attn_Q_w"],
        "ldt2": i["L2_attn_log_dt_scale"], "readw2": i["L2_attn_readout_w"], "gnw2": columns(i["L2_attn_gn_w"]),
        "gnb2": columns(i["L2_attn_gn_b"]), "dp2": columns(i["L2_attn_D_param"]), "outw2": i["L2_attn_out_w"],
        "wr2": i["L2_ffn_gate_w"].T, "eb2": i["L2_ffn_expert_bias"],
        "up2": i["L2_ffn_w_up"].transpose(2, 0, 1), "down2": i["L2_ffn_w_down"].transpose(2, 0, 1),
        "sup2": i["L2_ffn_shared_w_up"].T, "sdown2": i["L2_ffn_shared_w_down"].T,
    })
    a.update({
        "wq3": grouped(i["L3_attn_Wq"], 0).transpose(0, 2, 1), "wk3": grouped(i["L3_attn_Wk"], 0).transpose(0, 2, 1),
        "wv3": i["L3_attn_Wv"].reshape(NG, JG * HD, D).transpose(0, 2, 1), "rel3": grouped(i["L3_attn_rel_embed"], 1),
        "wp3": i["L3_attn_Wp"].T, "bp3": columns(i["L3_attn_bp"]),
        "gate3": i["L3_ffn_w_gate"].T, "up3": i["L3_ffn_w_up"].T, "down3": i["L3_ffn_w_down"].T,
    })
    return {k: np.ascontiguousarray(v) for k, v in a.items()}


def kernel(**inputs):
    import concourse.bacc as bacc
    from concourse.bass_utils import run_bass_kernel_spmd as run

    arrays = {**laid_out({k: np.asarray(v) for k, v in inputs.items()}), **constants()}

    def build(per_iteration):
        nc = bacc.Bacc("TRN2", target_bir_lowering=False, num_devices=1)
        dram = {k: nc.dram_tensor("in_" + k, v.shape, mybir.dt.from_np(v.dtype), kind="ExternalInput").ap()
                for k, v in arrays.items()}
        out = nc.dram_tensor("out", (D, B * T), F32, kind="ExternalOutput").ap()
        return nc, program(nc, dram, out, per_iteration)

    _, per_iteration = build({})
    nc, _ = build(per_iteration)
    r = run(nc, [{"in_" + k: v for k, v in arrays.items()}], core_ids=[0])
    return np.ascontiguousarray(r.results[0]["out"].T).reshape(B, T, D)
```

```python
from contextlib import ExitStack, contextmanager

import concourse.bass as bass
import numpy as np
from concourse import mybir

F32 = mybir.dt.float32
BF16 = mybir.dt.bfloat16
I32 = mybir.dt.int32
ALU = mybir.AluOpType
ACT = mybir.ActivationFunctionType
AX = mybir.AxisListType.X
P = 128
D = 128
B, T = 4, 1024
TB = 512
NT = TB // P
LN_EPS = 1e-5


class Mark:

    def __init__(self, src):
        self.src, self.n, self.loop = src, src.n, src.loop


class Counted:

    def __init__(self, nc, name, step=1):
        self.sem = nc.alloc_semaphore(name)
        nc.sync.sem_inc(self.sem, step)
        self.name, self.step, self.n, self.loop, self.per, self.base = name, step, step, None, 0, 0

    def value(self, n, loop):
        if loop is None:
            return n
        assert loop is self.loop, "a mark from a loop's body is used outside of it"
        return loop * self.per + n

    def raise_by(self, ins):
        ins.then_inc(self.sem, self.step)
        self.n += self.step


class Engine(Counted):

    def __init__(self, nc, eng, name):
        super().__init__(nc, name)
        self.eng, self.seen, self.apart, self.spare = eng, {}, False, None
        self.each_apart, self.in_chain = False, True

    def wait(self, *sources):
        for s in sources:
            m = s if isinstance(s, Mark) else Mark(s)
            key = (m.src.name, m.loop is None)
            if self.seen.get(key, -1) >= m.n:
                continue
            self.seen[key] = m.n
            self.eng.wait_ge(m.src.sem, m.src.value(m.n, m.loop))
            if self.each_apart and self.loop is not None:
                self.eng.sem_inc(self.spare.sem, 1)

    def __call__(self, op, *args, after=(), own=None, apart=False, **kw):
        self.wait(*after)
        if own or (own is None and self.in_chain):
            self.wait(self)
        if self.loop is not None and (apart or self.apart):
            self.eng.sem_inc(self.spare.sem, 1)
        self.raise_by(op(*args, **kw))
        return Mark(self)

    def dma(self, queue, out, in_, after=()):
        self.wait(*after)
        queue.raise_by(self.eng.dma_start(out, in_))
        return Mark(queue)


class Machine:

    def __init__(self, nc, per_iteration):
        self.nc, self.per_iteration, self.learned = nc, per_iteration, {}
        self.V = Engine(nc, nc.vector, "vector_done")
        self.A = Engine(nc, nc.scalar, "scalar_done")
        self.G = Engine(nc, nc.gpsimd, "gpsimd_done")
        self.E = Engine(nc, nc.tensor, "tensor_done")
        self.S = Engine(nc, nc.sync, "sync_done")
        self.engines = (self.V, self.A, self.G, self.E, self.S)
        self.queues = {}
        spare = Counted(nc, "spare")
        for e in self.engines:
            e.spare = spare
        self.G.apart = self.S.each_apart = True
        self.E.in_chain = self.A.in_chain = False
        self.n_names = 0

    def queue(self, name):
        if name not in self.queues:
            self.queues[name] = Counted(self.nc, "dma_" + name, 16)
        return self.queues[name]

    @contextmanager
    def loop(self, name, n, inner=None):
        every = list(self.engines) + list(self.queues.values())
        per = self.per_iteration.get(name, {})
        with ExitStack() as st:
            i = at = st.enter_context(self.nc.Fori(0, n))
            if inner:
                j = st.enter_context(self.nc.Fori(0, inner))
                i, at, n = i * inner + j, (i, j), n * inner
            for c in every:
                assert c.loop is None
                c.loop, c.per, c.base = i, per.get(c.name, 0), c.n
            for e in self.engines:
                e.seen = {}
            yield at
            assert all(q in every for q in self.queues.values()), "make queues ahead of a loop"
            self.learned[name] = {c.name: c.n - c.base for c in every}
        for c in every:
            c.n, c.loop = c.base + n * (c.n - c.base), None
        for e in self.engines:
            e.seen = {}

    def barrier(self):
        for e in self.engines:
            e.wait(*self.engines, *self.queues.values())

    @contextmanager
    def scope(self):
        with ExitStack() as st:
            def sb(shape, dt=F32):
                self.n_names += 1
                return st.enter_context(self.nc.sbuf_tensor(f"t{self.n_names}", list(shape), dt))
            yield sb
            self.barrier()


def rep(ap, axis, n):
    v = ap.unsqueeze(axis)
    shape = list(v.shape)
    shape[axis] = n
    return v.broadcast_to(shape)


def bank(ps, k, n=TB):
    return ps[:, k, 0:n]


class Common:

    def __init__(self, m, dram):
        nc = m.nc
        self.m, self.dram = m, dram
        self.ps = nc.alloc_psum_tensor("banks", [P, 8, TB], F32)
        self.xT = nc.alloc_sbuf_tensor("xT", [P, B * T], F32)
        self.ident = nc.alloc_sbuf_tensor("ident", [P, P], F32)
        self.mean_d = nc.alloc_sbuf_tensor("mean_d", [P, P], F32)
        self.eps = {v: nc.alloc_sbuf_tensor(f"eps{k}", [P, 1], F32) for k, v in enumerate((1e-5, 1e-6))}
        self.one = nc.alloc_sbuf_tensor("one", [P, 1], F32)
        self.q_w = m.queue("weights")
        m.queue("out")
        for k in ("a", "b", "c", "d", *(f"rel_{n}{r}" for n in ("out", "back") for r in range(4))):
            m.queue(k)

    def load_start(self):
        m, nc = self.m, self.m.nc
        m.S.dma(self.q_w, self.xT[:], self.dram["xT"])
        m.S.dma(self.q_w, self.ident[:], self.dram["c_ident"])
        m.V(nc.vector.memset, self.mean_d[:], 1.0 / D, own=False)
        m.V(nc.vector.memset, self.one[:], 1.0, own=False)
        for v, t in self.eps.items():
            m.V(nc.vector.memset, t[:], v, own=False)
        m.barrier()

    def layernorm(self, x, xn, tmp, bk):
        m, nc = self.m, self.m.nc
        V, A, E = m.V, m.A, m.E
        E(nc.tensor.matmul, bank(self.ps, bk), self.mean_d[:], x, start=True, stop=True, after=(V, A))
        V(nc.vector.tensor_tensor, xn, x, bank(self.ps, bk), ALU.subtract, after=(E, A))
        self.inverse_rms(xn, tmp, bk, LN_EPS)
        V(nc.vector.tensor_tensor, xn, xn, tmp, ALU.mult)

    def inverse_rms(self, x, out, bk, eps):
        m, nc = self.m, self.m.nc
        V, A, E = m.V, m.A, m.E
        A(nc.scalar.activation, out, x, ACT.Square, after=(V, E))
        E(nc.tensor.matmul, bank(self.ps, bk), self.mean_d[:], out, start=True, stop=True, after=(A, V))
        A(nc.scalar.activation, out, bank(self.ps, bk), ACT.Sqrt, bias=self.eps[eps][:], after=(E, V))
        V(nc.vector.reciprocal, out, out, after=(A,))

    def transpose(self, out, in_, after=()):
        k = in_.shape[0]
        return self.m.E(self.m.nc.tensor.transpose, out, in_, self.ident[0:k, 0:k], after=after)

    def update(self, x, s, g_ps, tmp):
        m, nc = self.m, self.m.nc
        m.A(nc.scalar.activation, tmp, g_ps, ACT.Silu, after=(m.E, m.V))
        m.V(nc.vector.tensor_tensor, tmp, tmp, s, ALU.mult, after=(m.A,))
        m.V(nc.vector.tensor_tensor, x, x, tmp, ALU.add)


H0, HP = 4, 64
DI0 = H0 * HP
FF0 = 352
QB = 16


def fp4(c, src, out, w, after):
    m, nc = c.m, c.m.nc
    V, A, G = m.V, m.A, m.G
    n = src.shape[0]
    nb = src.shape[1] // QB
    s3 = src.rearrange("p (b k) -> p b k", k=QB)
    o3 = out.rearrange("p (b k) -> p b k", k=QB)
    scale, inv = w["scale"][0:n, 0:nb], w["inv"][0:n, 0:nb]
    mag, fine, coarse, sign = (w[k][0:n, 0:nb * QB] for k in ("mag", "fine", "coarse", "sign"))
    mag3 = mag.rearrange("p (b k) -> p b k", k=QB)
    A(nc.scalar.activation, sign, src, ACT.Sign, after=(*after, V))
    V(nc.vector.tensor_reduce, scale, s3, AX, ALU.max, apply_absolute_value=True, after=after)
    V(nc.vector.tensor_scalar, scale, scale, 1.0 / 6.0, 1e-12, ALU.mult, ALU.max)
    V(nc.vector.reciprocal, inv, scale)
    V(nc.vector.tensor_tensor, mag3, s3, rep(inv, 2, QB), ALU.mult, after=(G,))
    V(nc.vector.scalar_tensor_tensor, mag, mag, -1.0, mag, ALU.mult, ALU.max)
    V(nc.vector.tensor_scalar, coarse, mag, 5.0, 2.0, ALU.is_gt, ALU.mult)
    V(nc.vector.tensor_scalar, fine, mag, 0.25, None, ALU.is_gt, own=False)
    for mid in (2.5, 3.5):
        V(nc.vector.scalar_tensor_tensor, coarse, mag, mid, coarse, ALU.is_gt, ALU.add)
    for mid in (0.75, 1.25, 1.75):
        V(nc.vector.scalar_tensor_tensor, fine, mag, mid, fine, ALU.is_gt, ALU.add)
    V(nc.vector.scalar_tensor_tensor, fine, coarse, 2.0, fine, ALU.mult, ALU.add)
    V(nc.vector.tensor_scalar, scale, scale, 0.5, None, ALU.mult, own=False)
    V(nc.vector.tensor_tensor, fine, fine, sign, ALU.mult, after=(A,))
    return V(nc.vector.tensor_tensor, o3, fine.rearrange("p (b k) -> p b k", k=QB), rep(scale, 2, QB), ALU.mult)


def layer0(c):
    m, nc, ps, d = c.m, c.m.nc, c.ps, c.dram
    V, A, G, E, S = m.V, m.A, m.G, m.E, m.S
    mm, act, tt, ts, stt = (nc.tensor.matmul, nc.scalar.activation, nc.vector.tensor_tensor,
                            nc.vector.tensor_scalar, nc.vector.scalar_tensor_tensor)
    with m.scope() as sb:
        wq, wqr = sb([P, D]), sb([P, D])
        wz, wxbc = sb([P, DI0]), sb([P, 4, 2 * DI0])
        wdt, wout = sb([P, H0]), sb([P, 2, D])
        cos, sin = sb([P, T]), sb([P, T])
        upper = sb([P, P])
        conv_b, npre, ngat, dcol = sb([P, 4]), sb([P, 1]), sb([P, 2]), sb([P, 2])
        dtb, neg_a = sb([P, H0]), sb([P, H0])
        wg, wu, wd = sb([P, FF0]), sb([P, FF0]), sb([P, 3, D])
        mean_di = sb([P, P])
        with m.scope() as tmp:
            raw, taps = tmp([P, 2 * DI0]), tmp([P, 4, 2 * DI0])
            wrow, wquant, wdrow, wdq = tmp([P, 2, 3, D]), tmp([P, D]), tmp([P, FF0]), tmp([P, FF0])
            w = {k: tmp([P, FF0]) for k in ("mag", "fine", "coarse", "sign")}
            w.update(scale=tmp([P, FF0 // QB]), inv=tmp([P, FF0 // QB]))
            for out, name in ((wq, "wq"), (wqr, "wqr"), (wz, "wz"), (wdt, "wdt"), (cos, "c_cos"), (sin, "c_sin"),
                              (upper, "c_upper"), (raw, "wxbc"), (wdrow, "fd0")):
                S.dma(c.q_w, out[:], d[name])
            S.dma(c.q_w, wout[:], d["wout0"].rearrange("(k p) n -> p k n", p=P))
            S.dma(c.q_w, conv_b[:], d["convb0"])
            S.dma(c.q_w, npre[:], d["npre"])
            S.dma(c.q_w, ngat[:], d["ngat"])
            for k in range(4):
                S.dma(c.q_w, taps[:, k, :], d["convw0"][k:k + 1, :].partition_broadcast(P))
            S.dma(c.q_w, dcol[:], d["D0"])
            S.dma(c.q_w, dtb[:], d["dtb"].unsqueeze(0).partition_broadcast(P))
            S.dma(c.q_w, neg_a[:], d["alog"].unsqueeze(0).partition_broadcast(P))
            for g, name in enumerate(("fg0", "fu0")):
                for k in range(3):
                    n = min(P, FF0 - k * P)
                    S.dma(c.q_w, wrow[0:n, g, k, :], d[name][k * P:k * P + n, :])
            V(nc.vector.memset, mean_di[:], 1.0 / DI0)
            for k in range(4):
                V(tt, wxbc[:, k, :], raw[:], taps[:, k, :], ALU.mult, after=(c.q_w,), own=False)
            A(act, neg_a[:], neg_a[:], ACT.Exp, after=(c.q_w,))
            V(ts, neg_a[:], neg_a[:], -1.0, None, ALU.mult, after=(A,))
            for g, out in enumerate((wg, wu)):
                for k in range(3):
                    n = min(P, FF0 - k * P)
                    fp4(c, wrow[0:n, g, k, :], wquant[0:n, :], w, (c.q_w, E))
                    c.transpose(ps[:, 0, 0:n], wquant[0:n, :], after=(V,))
                    V(nc.vector.tensor_copy, out[:, k * P:k * P + n], ps[:, 0, 0:n], after=(E,))
            fp4(c, wdrow[:], wdq[:], w, (c.q_w,))
            for k in range(3):
                n = min(P, FF0 - k * P)
                c.transpose(ps[0:n, 0, 0:P], wdq[:, k * P:k * P + n], after=(V,))
                V(nc.vector.tensor_copy, wd[0:n, k, :], ps[0:n, 0, 0:P], after=(E,))

        xn, q, hp = sb([P, TB]), sb([P, TB]), sb([P, 3 + TB])
        ta, tb = sb([P, TB]), sb([P, TB])
        zs, xbc, y = sb([P, 2, TB]), sb([P, 4, TB]), sb([P, 2, TB])
        dt, adt, t16 = sb([P, NT, H0]), sb([P, NT, H0]), sb([P, NT, H0])
        xdt, xdd, btok = sb([P, H0, HP]), sb([P, H0, HP]), sb([P, P])
        acs, dd = sb([P, H0]), sb([P, H0])
        ua, low, ce, mt = sb([P, H0, P]), sb([P, H0, P]), sb([P, H0, P]), sb([P, H0, P])
        ec, gm = sb([P, H0, P]), sb([P, P])
        state = sb([P, H0, HP])
        ones = sb([P, P])
        V(nc.vector.memset, ones[:], 1.0)
        w = {k: sb([P, FF0]) for k in ("mag", "fine", "coarse", "sign")}
        w.update(scale=sb([P, FF0 // QB]), inv=sb([P, FF0 // QB]))
        xt, xq, xqT = sb([P, D]), sb([P, D]), sb([P, P])
        hid, hq, hqT = sb([P, FF0]), sb([P, FF0]), sb([P, 3, TB])

        with m.loop("layer0", B) as b:
            for half in range(T // TB):
                xb = c.xT[:, bass.ds(b * T + half * TB, TB)]
                c.layernorm(xb, xn[:], ta[:], 0)
                E(mm, bank(ps, 0), wq[:], xn[:], start=True, stop=True, after=(V, A))
                E(mm, bank(ps, 1), wqr[:], xn[:], start=True, stop=True)
                at = slice(half * TB, half * TB + TB)
                V(tt, q[:], bank(ps, 0), cos[:, at], ALU.mult, after=(E,))
                V(tt, ta[:], bank(ps, 1), sin[:, at], ALU.mult)
                V(tt, q[:], q[:], ta[:], ALU.add)
                if half == 0:
                    V(nc.vector.memset, hp[:, 0:3], 0.0, after=(E,))
                else:
                    V(nc.vector.tensor_copy, hp[:, 0:3], hp[:, TB:TB + 3], after=(E,))
                c.inverse_rms(q[:], ta[:], 0, 1e-5)
                V(stt, hp[:, 3:], q[:], npre[:], ta[:], ALU.mult, ALU.mult)
                for k in range(2):
                    E(mm, bank(ps, k), wz[:, k * P:(k + 1) * P], hp[:, 3:], start=True, stop=True, after=(V, A))
                for k in range(4):
                    for j in range(4):
                        E(mm, bank(ps, 2 + k), wxbc[:, j, k * P:(k + 1) * P], hp[:, j:j + TB],
                          start=(j == 0), stop=(j == 3), own=False)
                for t in range(NT):
                    E(mm, ps[:, 6, H0 * t:H0 * t + H0], hp[:, 3 + t * P:3 + (t + 1) * P], wdt[:],
                      start=True, stop=True, own=False)
                for k in range(2):
                    A(act, zs[:, k, :], bank(ps, k), ACT.Silu, after=(E, V), own=False)
                for k in range(4):
                    A(act, xbc[:, k, :], bank(ps, 2 + k), ACT.Silu, bias=conv_b[:, k:k + 1], own=False)
                V(tt, dt[:], ps[:, 6, 0:NT * H0].rearrange("p (t h) -> p t h", h=H0), rep(dtb[:], 1, NT),
                  ALU.add, after=(E,))
                V(stt, t16[:], dt[:], -1.0, dt[:], ALU.mult, ALU.max)
                A(act, t16[:], t16[:], ACT.Exp, scale=-1.0, after=(V,))
                A(act, t16[:], t16[:], ACT.Ln, bias=c.one[:], own=True)
                V(stt, dt[:], dt[:], 0.0, t16[:], ALU.max, ALU.add, after=(A,))
                V(tt, adt[:], dt[:], rep(neg_a[:], 1, NT), ALU.mult)
                for t in range(NT):
                    ct = slice(t * P, (t + 1) * P)
                    first = half == 0 and t == 0
                    for k in range(3):
                        c.transpose(ps[:, 0, k * P:(k + 1) * P], xbc[:, k, ct], after=(A, V))
                    V(tt, xdt[:], ps[:, 0, 0:DI0].rearrange("p (h q) -> p h q", h=H0), rep(dt[:, t, :], 2, HP),
                      ALU.mult, after=(E,))
                    V(nc.vector.tensor_copy, btok[:], ps[:, 0, DI0:DI0 + P], own=False)
                    V(tt, ua[:], rep(upper[:], 1, H0), rep(adt[:, t, :], 2, P), ALU.mult, own=False)
                    E(mm, ps[:, 1, 0:H0], upper[:], adt[:, t, :], start=True, stop=True, after=(V,))
                    E(mm, bank(ps, 2), ones[:], ua[:].rearrange("p h t -> p (h t)"), start=True, stop=True, own=False)
                    E(mm, ps[:, 3, 0:P], xbc[:, 2, ct], xbc[:, 3, ct], start=True, stop=True, own=False)
                    rows = bank(ps, 2).rearrange("p (h t) -> p h t", h=H0)
                    V(nc.vector.tensor_copy, acs[:], ps[:, 1, 0:H0], after=(E,))
                    V(tt, gm[:], ps[:, 3, 0:P], upper[:], ALU.mult, own=False)
                    for h in range(H0):
                        V(ts, low[:, h, :], rows[:, h, :], acs[:, h:h + 1], 0.0, ALU.subtract, ALU.min, own=(h == 0))
                    V(tt, dd[:], rows[:, :, P - 1], acs[:], ALU.subtract, own=False)
                    A(act, ec[:], rows, ACT.Exp, after=(E, V))
                    A(act, low[:], low[:], ACT.Exp, own=False)
                    A(act, dd[:], dd[:], ACT.Exp, own=False)
                    V(tt, mt[:], low[:], rep(gm[:], 1, H0), ALU.mult, after=(A,))
                    V(tt, ce[:], ec[:], rep(xbc[:, 3, ct], 1, H0), ALU.mult, own=False)
                    V(tt, xdd[:], xdt[:], rep(dd[:], 2, HP), ALU.mult, own=False)
                    for h in range(H0):
                        o = ps[(h % 2) * HP:(h % 2 + 1) * HP, 4, (h // 2) * P:(h // 2 + 1) * P]
                        E(mm, o, xdt[:, h, :], mt[:, h, :], start=True, stop=first, after=(V,))
                        if not first:
                            E(mm, o, state[:, h, :], ce[:, h, :], start=False, stop=True, own=False)
                    E(mm, ps[:, 5, 0:DI0], btok[:], xdd[:].rearrange("p h q -> p (h q)"), start=True, stop=True)
                    for k in range(2):
                        V(stt, y[:, k, ct], xbc[:, k, ct], dcol[:, k:k + 1], ps[:, 4, k * P:(k + 1) * P],
                          ALU.mult, ALU.add, after=(E,), own=False)
                    new = ps[:, 5, 0:DI0].rearrange("p (h q) -> p h q", h=H0)
                    if first:
                        V(nc.vector.tensor_copy, state[:], new)
                    else:
                        V(tt, state[:], state[:], rep(ec[:, :, P - 1], 2, HP), ALU.mult)
                        V(tt, state[:], state[:], new, ALU.add)
                V(tt, y[:], y[:], zs[:], ALU.mult)
                for k in range(2):
                    A(act, zs[:, k, :], y[:, k, :], ACT.Square, after=(V,))
                    E(mm, bank(ps, 0), mean_di[:], zs[:, k, :], start=(k == 0), stop=(k == 1), after=(A,))
                A(act, ta[:], bank(ps, 0), ACT.Sqrt, bias=c.eps[1e-5][:], after=(E,))
                V(nc.vector.reciprocal, ta[:], ta[:], after=(A,))
                for k in range(2):
                    V(stt, y[:, k, :], y[:, k, :], ngat[:, k:k + 1], ta[:], ALU.mult, ALU.mult)
                    E(mm, bank(ps, 1), wout[:, k, :], y[:, k, :], start=(k == 0), stop=(k == 1), after=(V,))
                V(tt, q[:], q[:], bank(ps, 1), ALU.add, after=(E,))
                for t in range(NT):
                    ct = slice(t * P, (t + 1) * P)
                    c.transpose(ps[:, 2, 0:P], xn[:, ct], after=(V,))
                    A(nc.scalar.copy, xt[:], ps[:, 2, 0:P], after=(E, V))
                    fp4(c, xt[:], xq[:], w, (A,))
                    c.transpose(ps[:, 2, 0:P], xq[:], after=(V,))
                    A(nc.scalar.copy, xqT[:], ps[:, 2, 0:P], after=(E,))
                    E(mm, ps[:, 3, 0:FF0], xqT[:], wg[:], start=True, stop=True, after=(A,))
                    E(mm, ps[:, 4, 0:FF0], xqT[:], wu[:], start=True, stop=True)
                    A(act, hid[:], ps[:, 3, 0:FF0], ACT.Silu, after=(E, V))
                    V(tt, hid[:], hid[:], ps[:, 4, 0:FF0], ALU.mult, after=(A,))
                    fp4(c, hid[:], hq[:], w, (A,))
                    for k in range(3):
                        n = min(P, FF0 - k * P)
                        c.transpose(ps[0:n, 5, k * P:(k + 1) * P], hq[:, k * P:k * P + n], after=(V, A))
                    turned = bank(ps, 5, 3 * P).rearrange("p (k t) -> p k t", k=3)
                    A(nc.scalar.copy, hqT[:, 0:2, ct], turned[:, 0:2, :], after=(E,))
                    A(nc.scalar.copy, hqT[0:n, 2, ct], turned[0:n, 2, :])
                for k in range(3):
                    n = min(P, FF0 - k * P)
                    E(mm, bank(ps, 6), wd[0:n, k, :], hqT[0:n, k, :], start=(k == 0), stop=(k == 2), after=(A,))
                c.update(xb, q[:], bank(ps, 6), tb[:])


NH = 16
HD = D // NH
E1, F1 = 8, 256
ATTN_SCALE1 = D ** -0.5 / 2.0


def woven(*parts):
    live = list(parts)
    while live:
        for part in list(live):
            for _ in range(part[1]):
                if next(part[0], True):
                    live.remove(part)
                    break


def route(c, logits, w, keep, softmax):
    m, nc = c.m, c.m.nc
    V, A = m.V, m.A
    tt = nc.vector.tensor_tensor
    n = logits.shape[2]
    lj, le = rep(logits, 2, n), rep(logits, 3, n)
    V(tt, w["beats"], lj, le, ALU.is_equal, own=True)
    V(tt, w["beats"], w["beats"], rep(w["lower"], 1, NT), ALU.mult)
    V(tt, w["more"], lj, le, ALU.is_gt, own=False)
    V(tt, w["beats"], w["beats"], w["more"], ALU.add)
    V(nc.vector.tensor_reduce, w["rank"], w["beats"], AX, ALU.add)
    if softmax:
        V(nc.vector.tensor_reduce, w["top"], logits, AX, ALU.max, own=False)
        V(tt, w["score"], logits, rep(w["top"], 2, n), ALU.subtract)
        e = A(nc.scalar.activation, w["score"], w["score"], ACT.Exp, after=(Mark(V),), own=False)
        V(nc.vector.scalar_tensor_tensor, w["comb"], w["rank"], float(keep), w["score"], ALU.is_lt, ALU.mult, after=(e,))
        V(nc.vector.tensor_reduce, w["top"], w["comb"], AX, ALU.add)
        V(nc.vector.reciprocal, w["top"], w["top"])
        return V(tt, w["comb"], w["comb"], rep(w["top"], 2, n), ALU.mult)
    return V(nc.vector.scalar_tensor_tensor, w["comb"], w["rank"], float(keep), w["score"], ALU.is_lt, ALU.mult)


def route_buffers(sb, n):
    w = {k: sb([P, NT, n])[:] for k in ("rank", "score", "comb")}
    w.update(top=sb([P, NT])[:], beats=sb([P, NT, n, n])[:], more=sb([P, NT, n, n])[:], lower=sb([P, n, n])[:])
    return w


def sort_descending(c, a, b, n):
    V, tt = c.m.V, c.m.nc.vector.tensor_tensor
    size = 2
    while size <= n:
        step = size
        while step >= 2:
            va, vb = (x.rearrange("p (r k) -> p r k", k=step) for x in (a, b))
            h = step // 2
            if step == size:
                hi = slice(step - 1, h - 1 if h > 0 else None, -1)
            else:
                hi = slice(h, step)
            V(tt, vb[:, :, 0:h], va[:, :, 0:h], va[:, :, hi], ALU.max)
            V(tt, vb[:, :, hi], va[:, :, 0:h], va[:, :, hi], ALU.min, own=False)
            a, b = b, a
            step //= 2
        size *= 2
    return a, b


def layer1(c):
    m, nc, ps, d = c.m, c.m.nc, c.ps, c.dram
    V, A, G, E, S = m.V, m.A, m.G, m.E, m.S
    mm, act, tt, ts, stt = (nc.tensor.matmul, nc.scalar.activation, nc.vector.tensor_tensor,
                            nc.vector.tensor_scalar, nc.vector.scalar_tensor_tensor)
    reduce, copy = nc.vector.tensor_reduce, nc.vector.tensor_copy
    with m.scope() as sb:
        wqkv, bias, ones = sb([P, 3 * D]), sb([1, 3 * D]), sb([1, P])
        wr, w1, w3, w2 = sb([P, E1]), sb([P, E1, F1]), sb([P, E1, F1]), sb([P, F1 // P, E1, D])
        blocks, before = sb([P, P]), sb([P, P])
        order, restart, inv_k = sb([P, NH]), sb([P, NT * NH * NH]), sb([P, NH])
        pick = sb([E1, E1, P])
        rb = route_buffers(sb, E1)
        for out, name in ((wqkv, "wqkv1"), (bias, "bqkv1"), (blocks, "c_blocks"), (before, "c_before"),
                          (order, "c_order"), (inv_k, "c_inv_k"), (restart, "c_restart"), (pick, "c_pick"), (wr, "wr1")):
            S.dma(c.q_w, out[:], d[name])
        S.dma(c.q_w, rb["lower"], d["c_lower"])
        S.dma(c.q_w, w1[:], d["w1"].rearrange("e h f -> h e f"))
        S.dma(c.q_w, w3[:], d["w3"].rearrange("e h f -> h e f"))
        for k in range(F1 // P):
            S.dma(c.q_w, w2[:, k], d["w2"][:, k * P:(k + 1) * P, :].rearrange("e f h -> f e h"))
        V(nc.vector.memset, ones[:], 1.0)
        for k in range(3):
            V(tt, wqkv[:, k * D:(k + 1) * D], wqkv[:, k * D:(k + 1) * D], blocks[:], ALU.mult, after=(c.q_w,))

        xn, xm, tmp = sb([P, TB]), sb([P, P]), sb([P, TB])
        qkv = sb([P, NT, 3 * D])
        prod = [sb([P, NH * NH * HD]) for _ in range(2)]
        sc, sa, sbuf2 = (sb([P, NT, NH, NH]) for _ in range(3))
        cum, cumsq, tau = (sb([P, NT, NH, NH]) for _ in range(3))
        one = sb([P, NT * NH])
        s_tok, s_T = sb([P, NT, D]), sb([P, TB])
        lg, combT = sb([P, NT, E1]), sb([E1, TB])
        xs, hid = sb([P, 2, TB]), sb([P, 2, TB])
        rows = NT * NH

        def attention(half):
            ready = []
            for t in range(NT):
                x = xn[:, t * P:(t + 1) * P]
                if half == 0 and t == 0:
                    r = V(tt, xm[:], x, before[:], ALU.mult)
                    x = xm[:]
                else:
                    r = Mark(V)
                E(mm, bank(ps, 0, 3 * D), x, wqkv[:], start=True, stop=False, after=(r, Mark(A)))
                e = E(mm, bank(ps, 0, 3 * D), ones[:], bias[:], start=False, stop=True, own=False)
                A(act, qkv[:, t, 0:D], bank(ps, 0, D), ACT.Copy, scale=ATTN_SCALE1, after=(e, Mark(V), Mark(G)), own=False)
                a = A(nc.scalar.copy, qkv[:, t, D:], ps[:, 0, D:3 * D], own=False)
                q = qkv[:, t, 0:D].rearrange("p (h d) -> p h d", h=NH)
                k = qkv[:, t, D:2 * D].rearrange("p (h d) -> p h d", h=NH)
                pr = prod[t % 2][:].rearrange("p (h g d) -> p h g d", h=NH, g=NH)
                g = G(nc.gpsimd.tensor_tensor, pr, rep(q, 2, NH), rep(k, 1, NH), ALU.mult, after=(a, *ready[-2:-1]), own=False)
                ready.append(V(reduce, sc[:, t], pr, AX, ALU.add, after=(g,), own=False))
                yield
            flat = "p t h g -> p (t h g)"
            V(copy, sa[:], sc[:])
            top, other = sort_descending(c, sa[:].rearrange(flat), sbuf2[:].rearrange(flat), NH)
            yield
            r3 = "p (r k) -> p r k"
            top, other = top.rearrange(r3, k=NH), other.rearrange(r3, k=NH)
            z, cm, cs, tu = (x[:].rearrange("p t h g -> p (t h) g") for x in (sc, cum, cumsq, tau))
            V(copy, one[:], top[:, :, 0])
            V(tt, z, z, rep(one[:], 2, NH), ALU.subtract)
            r = V(tt, top, top, rep(one[:], 2, NH), ALU.subtract, own=False)
            a = A(act, other, top, ACT.Square, after=(r,), own=False)
            yield
            fl = "p r k -> p (r k)"
            V(nc.vector.tensor_tensor_scan, cm.rearrange(fl), restart[:], top.rearrange(fl), 0.0, ALU.mult, ALU.add)
            V(nc.vector.tensor_tensor_scan, cs.rearrange(fl), restart[:], other.rearrange(fl), 0.0, ALU.mult, ALU.add,
              after=(a,), own=False)
            yield
            ik = rep(inv_k[:], 1, rows)
            V(tt, tu, cm, ik, ALU.mult)
            V(tt, cm, cm, tu, ALU.mult)
            V(tt, cs, cs, cm, ALU.subtract)
            yield
            V(ts, cs, cs, -1.0, 1.0, ALU.mult, ALU.add)
            V(tt, cs, cs, ik, ALU.mult)
            r = V(ts, cs, cs, 0.0, None, ALU.max)
            a = A(act, cs, cs, ACT.Sqrt, after=(r,), own=False)
            yield
            V(tt, tu, tu, cs, ALU.subtract, after=(a,))
            V(tt, cm, tu, top, ALU.is_le)
            V(reduce, one[:], cm, AX, ALU.add)
            yield
            V(tt, cm, rep(order[:], 1, rows), rep(one[:], 2, NH), ALU.is_equal)
            V(tt, cm, cm, tu, ALU.mult)
            V(reduce, one[:], cm, AX, ALU.add)
            yield
            V(tt, z, z, rep(one[:], 2, NH), ALU.subtract)
            r = V(ts, z, z, 0.0, None, ALU.max)
            a = A(act, z, z, ACT.Square, after=(r,), own=False)
            yield
            ready = []
            for t in range(NT):
                v = qkv[:, t, 2 * D:].rearrange("p (g d) -> p d g", g=NH)
                pr = prod[t % 2][:].rearrange("p (h d g) -> p h d g", h=NH, d=HD)
                g = G(nc.gpsimd.tensor_tensor, pr, rep(sc[:, t], 2, HD), rep(v, 1, NH), ALU.mult,
                      after=(a, *ready[-2:-1]), own=False)
                ready.append(V(reduce, s_tok[:, t].rearrange("p (h d) -> p h d", h=NH), pr, AX, ALU.add,
                               after=(g,), own=False))
                c.transpose(ps[:, 0, t * P:(t + 1) * P], s_tok[:, t], after=(ready[-1], Mark(A)))
                yield
            A(nc.scalar.copy, s_T[:], bank(ps, 0), after=(Mark(E), Mark(V)), own=False)
            yield

        def moe():
            for t in range(NT):
                e = E(mm, ps[:, 1, t * E1:(t + 1) * E1], xn[:, t * P:(t + 1) * P], wr[:], start=True, stop=True, own=False)
            V(copy, lg[:], ps[:, 1, 0:NT * E1].rearrange("p (t e) -> p t e", t=NT), after=(e,))
            r = route(c, lg[:], rb, 2, True)
            yield
            for t in range(NT):
                e = c.transpose(ps[0:E1, 1, t * P:(t + 1) * P], rb["comb"][:, t], after=(r,))
            spread = A(nc.scalar.copy, combT[:], ps[0:E1, 1, :], after=(e,), own=False)
            yield
            hidden, downs = [], []
            for s in range(2 * E1 + 1):
                if s < 2 * E1:
                    e, k = s // 2, s % 2
                    b1, b3 = 2 + 2 * (s % 2), 3 + 2 * (s % 2)
                    if k == 0:
                        mk = E(mm, bank(ps, 1), pick[:, e, :], combT[:], start=True, stop=True,
                               after=(spread,), own=False)
                        spread = V(tt, xs[:, e % 2], xn[:], bank(ps, 1), ALU.mult, after=(mk,), own=False)
                    free = hidden[s - 2:s - 1]
                    g = E(mm, bank(ps, b1), w1[:, e, k * P:(k + 1) * P], xn[:], start=True, stop=True, after=free, own=False)
                    u = E(mm, bank(ps, b3), w3[:, e, k * P:(k + 1) * P], xs[:, e % 2], start=True, stop=True,
                          after=(spread,), own=False)
                    a = A(act, hid[:, s % 2], bank(ps, b1), ACT.Silu, after=(g, *downs[s - 2:s - 1]), own=False)
                    hidden.append(V(tt, hid[:, s % 2], hid[:, s % 2], bank(ps, b3), ALU.mult, after=(a, u), own=False))
                if s > 0:
                    e, k = (s - 1) // 2, (s - 1) % 2
                    downs.append(E(mm, bank(ps, 6), w2[:, k, e, :], hid[:, (s - 1) % 2], start=(s == 1),
                                   stop=(s == 2 * E1), after=(hidden[s - 1],), own=False))
                yield

        with m.loop("layer1", B) as b:
            for half in range(T // TB):
                xb = c.xT[:, bass.ds(b * T + half * TB, TB)]
                c.layernorm(xb, xn[:], tmp[:], 0)
                E.wait(V, A)
                woven((attention(half), 1), (moe(), 1))
                c.update(xb, s_T[:], bank(ps, 6), tmp[:])


DI2 = 256
DH2 = DI2 // NH
CH = P
E2, F2 = 8, 176
NTT = B * T // P


def delta_inputs(c, sb, keep):
    m, nc, ps, d = c.m, c.m.nc, c.ps, c.dram
    V, A, G, E, S = m.V, m.A, m.G, m.E, m.S
    mm, act, tt, ts, stt = (nc.tensor.matmul, nc.scalar.activation, nc.vector.tensor_tensor,
                            nc.vector.tensor_scalar, nc.vector.scalar_tensor_tensor)
    win, ones = sb([P, 800]), sb([1, P])
    b_z, b_x, b_kv, b_g = sb([P, 2]), sb([P, 2]), sb([1, 288]), sb([1, 7 * NH])
    rms_w, taps, conv_b = sb([P, 1]), sb([P, 2, 4]), sb([P, 2])
    gate_w, q_w = sb([P, 2, 7 * NH]), sb([P, 2, DI2])
    for out, name in ((win, "win2"), (b_z, "bz2"), (b_x, "bx2"), (b_kv, "bkv2"), (b_g, "bg2"), (rms_w, "rms2"),
                      (conv_b, "convb2")):
        S.dma(c.q_w, out[:], d[name])
    for out, name in ((taps, "convw2"), (gate_w, "gatew2"), (q_w, "qw2")):
        S.dma(c.q_w, out[:], d[name].rearrange("(k p) n -> p k n", p=P))
    V(nc.vector.memset, ones[:], 1.0)
    V.wait(c.q_w)
    E.wait(c.q_w, V)
    A.wait(c.q_w)
    h, ta = sb([P, TB]), sb([P, TB])
    xn = sb([P, TB])
    xg, zs, xc = sb([P, 2, 3 + TB]), sb([P, 2, TB]), sb([P, 2, TB])
    kq, sq = sb([P, NT, 2, DI2]), sb([P, NT, 2, DI2])
    norm = sb([P, NT, 2 * NH])
    with m.loop("layer2_inputs", B) as b:
        for half in range(T // TB):
            x0, t0 = b * T + half * TB, b * (T // P) + half * NT
            c.layernorm(c.xT[:, bass.ds(x0, TB)], xn[:], ta[:], 0)
            V(nc.vector.tensor_copy, keep["xn"][:, bass.ds(x0, TB)], xn[:])
            c.inverse_rms(xn[:], ta[:], 0, 1e-6)
            V(stt, h[:], xn[:], rms_w[:], ta[:], ALU.mult, ALU.mult)
            if half == 0:
                V(nc.vector.memset, xg[:, :, 0:3], 0.0)
            else:
                V(nc.vector.tensor_copy, xg[:, :, 0:3], xg[:, :, TB:TB + 3])
            for k in range(4):
                E(mm, bank(ps, k), win[:, k * P:(k + 1) * P], h[:], start=True, stop=True, after=(V, A), own=False)
            for k in range(2):
                A(act, zs[:, k], bank(ps, k), ACT.Silu, bias=b_z[:, k:k + 1], after=(E, m.queues["a"]), own=False)
            for k in range(2):
                A(act, xg[:, k, 3:], bank(ps, 2 + k), ACT.Identity, bias=b_x[:, k:k + 1], after=(V,), own=False)
            S.dma(m.queues["a"], keep["z"][:, :, bass.ds(x0, TB)], zs[:], after=(A,))
            for k in range(2):
                V(ts, xc[:, k], xg[:, k, 0:TB], taps[:, k, 0:1], conv_b[:, k:k + 1], ALU.mult, ALU.add,
                  after=(A, m.queues["b"]))
                for j in range(1, 4):
                    V(stt, xc[:, k], xg[:, k, j:j + TB], taps[:, k, j:j + 1], xc[:, k], ALU.mult, ALU.add)
            A(act, xc[:], xc[:], ACT.Silu, after=(V,))
            S.dma(m.queues["b"], keep["xconv"][:, :, bass.ds(x0, TB)], xc[:], after=(A,))
            for t in range(NT):
                ct = slice(t * P, (t + 1) * P)
                for out, rows, w_row, w_main in ((bank(ps, 4, 288), (h[:, ct],), b_kv, (win[:, 512:800],)),
                                                 (bank(ps, 5, 7 * NH), (xc[:, 0, ct], xc[:, 1, ct]), b_g,
                                                  (gate_w[:, 0], gate_w[:, 1])),
                                                 (bank(ps, 6, DI2), (xc[:, 0, ct], xc[:, 1, ct]), None,
                                                  (q_w[:, 0], q_w[:, 1]))):
                    for k, (r, w) in enumerate(zip(rows, w_main)):
                        E(mm, out, r, w, start=(k == 0), stop=(k == 1 and w_row is None), after=(A, V), own=False)
                    if w_row is not None:
                        E(mm, out, ones[:], w_row[:], start=False, stop=True, own=False)
                A(nc.scalar.copy, kq[:, t, 0], bank(ps, 4, DI2), after=(E, V), own=False)
                A(nc.scalar.copy, keep["v"][:, bass.ds(t0 + t, 1)], ps[:, 4:5, DI2:288], own=False)
                A(nc.scalar.copy, keep["gates"][:, bass.ds(t0 + t, 1)], ps[:, 5:6, 0:7 * NH], own=False)
                A(nc.scalar.copy, kq[:, t, 1], bank(ps, 6, DI2), own=False)
            A(act, sq[:], kq[:], ACT.Square, own=True)
            V(nc.vector.tensor_reduce, norm[:], sq[:].rearrange("p t k (h d) -> p t (k h) d", d=DH2), AX, ALU.add, after=(A,))
            A(act, norm[:], norm[:], ACT.Sqrt, after=(V,))
            V(ts, norm[:], norm[:], 1e-6, None, ALU.add, after=(A,))
            V(nc.vector.reciprocal, norm[:], norm[:])
            for k, name in enumerate(("k", "q")):
                V(tt, keep[name][:, bass.ds(t0, NT)].rearrange("p t (h d) -> p t h d", d=DH2),
                  kq[:, :, k].rearrange("p t (h d) -> p t h d", d=DH2), rep(norm[:, :, k * NH:(k + 1) * NH], 3, DH2),
                  ALU.mult, own=(k == 0))


def delta_gates(c, sb, keep):
    m, nc, d = c.m, c.m.nc, c.dram
    V, A, S = m.V, m.A, m.S
    act, tt, ts, stt = nc.scalar.activation, nc.vector.tensor_tensor, nc.vector.tensor_scalar, nc.vector.scalar_tensor_tensor
    t_scale, freqs = sb([P, NH]), sb([P, NH])
    S.dma(c.q_w, t_scale[:], d["ldt2"].unsqueeze(0).partition_broadcast(P))
    S.dma(c.q_w, freqs[:], d["c_freqs"])
    A(act, t_scale[:], t_scale[:], ACT.Exp, after=(c.q_w,))
    V.wait(c.q_w, A)
    alpha, omega, sel_b, sel_c, sel_dt, beta, r = (keep["gates"][:, :, j * NH:(j + 1) * NH] for j in range(7))
    decay, o_beta, cos, sin, v0, v1 = (keep["g"][:, j] for j in range(6))
    t1, t2, dt, det = (sb([P, NTT, NH])[:] for _ in range(4))

    def softplus(out, x):
        V(stt, t1, x, -1.0, x, ALU.mult, ALU.max)
        A(act, t1, t1, ACT.Exp, scale=-1.0, after=(V,))
        A(act, t1, t1, ACT.Ln, bias=c.one[:], own=True)
        V(stt, out, x, 0.0, t1, ALU.max, ALU.add, after=(A,))

    softplus(dt, sel_dt)
    V(tt, dt, dt, rep(t_scale[:], 1, NTT), ALU.mult)
    V(ts, dt, dt, 1e-4, 0.5, ALU.add, ALU.mult)
    softplus(t2, alpha)
    V(tt, alpha, t2, dt, ALU.mult)
    A(act, omega, omega, ACT.Tanh, after=(V,))
    A(act, sel_b, sel_b, ACT.Sigmoid)
    A(act, keep["sel_c"][:], sel_c, ACT.Sigmoid)
    A(act, o_beta, beta, ACT.Sigmoid)
    A(act, r, r, ACT.Sigmoid)
    V(ts, omega, omega, 1.0, None, ALU.add, after=(A,))
    V(tt, omega, omega, rep(freqs[:], 1, NTT), ALU.mult)
    V(tt, omega, omega, dt, ALU.mult)
    V(tt, t2, omega, omega, ALU.mult)
    V(ts, det, alpha, 1.0, None, ALU.add)
    V(tt, det, det, det, ALU.mult)
    V(tt, det, det, t2, ALU.add)
    V(nc.vector.reciprocal, det, det)
    V(tt, t1, alpha, alpha, ALU.mult)
    V(tt, t1, t1, t2, ALU.add)
    V(ts, t1, t1, -1.0, 1.0, ALU.mult, ALU.add)
    V(tt, cos, t1, det, ALU.mult)
    V(stt, sin, omega, 2.0, det, ALU.mult, ALU.mult)
    V(tt, t1, cos, cos, ALU.mult)
    V(tt, t2, sin, sin, ALU.mult)
    V(tt, t1, t1, t2, ALU.add)
    V(ts, det, t1, 0.0, None, ALU.is_equal)
    V(ts, t1, t1, 1e-32, None, ALU.max)
    A(act, t1, t1, ACT.Sqrt, after=(V,))
    V(nc.vector.reciprocal, t2, t1, after=(A,))
    V(tt, cos, cos, t2, ALU.mult)
    V(tt, cos, cos, det, ALU.add)
    V(tt, sin, sin, t2, ALU.mult)
    V(ts, t1, t1, 1e-8, 1.0, ALU.max, ALU.min)
    A(act, t1, t1, ACT.Ln, after=(V,))
    V(stt, t1, t1, 8.0, r, ALU.mult, ALU.mult, after=(A,))
    A(act, decay, t1, ACT.Exp, after=(V,))
    V(tt, t1, decay, decay, ALU.mult, after=(A,))
    V(ts, t1, t1, -1.0, 1.0, ALU.mult, ALU.add)
    V(ts, t1, t1, 0.0, 1.0, ALU.max, ALU.min)
    V(ts, t1, t1, 1e-6, None, ALU.add)
    A(act, t1, t1, ACT.Sqrt, after=(V,))
    V(tt, t1, t1, sel_b, ALU.mult, after=(A,))
    vv = keep["v"][:].rearrange("p t (h s) -> p t h s", s=2)
    V(tt, v0, vv[:, :, :, 0], t1, ALU.mult)
    V(tt, v1, vv[:, :, :, 1], t1, ALU.mult, own=False)


def delta_recurrence(c, sb, keep):
    m, nc, ps, d = c.m, c.m.nc, c.ps, c.dram
    V, A, G, E, S = m.V, m.A, m.G, m.E, m.S
    act, tt, ts, stt = nc.scalar.activation, nc.vector.tensor_tensor, nc.vector.tensor_scalar, nc.vector.scalar_tensor_tensor
    gtt, gts, gcopy = nc.gpsimd.tensor_tensor, nc.gpsimd.tensor_scalar, nc.gpsimd.tensor_copy
    kst, qst = sb([P, 2, B, NH, DH2]), sb([P, 2, B, NH, DH2])
    gst = sb([P, 6, 2, B, NH])
    kc, qc, nb = (sb([P, CH, DH2]) for _ in range(3))
    yc = sb([P, 1 + CH, DH2])
    g = sb([P, 6, CH])
    turn, turn2, ta, tb = (sb([P, 2, CH]) for _ in range(4))
    carry = sb([P, 2])
    w, wt, nbm, u, scaled = sb([P, CH]), sb([P, 2, CH]), sb([P, CH]), sb([P, CH]), sb([P, DH2])
    product = sb([P, DH2])
    ret = sb([P, CH])
    tok, cs_tok, rt, ro = sb([P, 2, B, NH]), sb([P, 2, B, NH]), sb([P, 2, B, NH]), sb([P, B, NH, 2])
    sel = sb([P, B, NH])
    V(nc.vector.memset, yc[:, 0, :], 0.0)
    V(nc.vector.memset, carry[:, 0:1], 1.0)
    V(nc.vector.memset, carry[:, 1:2], 0.0)
    H = P // 2
    nt = T // P
    m.barrier()
    with m.loop("layer2_recurrence", nt) as i:
        def tile_of(x):
            return x.rearrange("p (b t) n -> p b t n", b=B)[:, :, bass.ds(i, 1), :].squeeze(2)

        for s in range(2):
            for st, name in ((kst, "k"), (qst, "q")):
                G(gcopy, st[:, s].rearrange("p b h d -> p b (h d)"), tile_of(keep[name][:]), after=(E,), own=False)
            for j in range(6):
                A(nc.scalar.copy, gst[:, j, s], tile_of(keep["g"][:, j]), after=(E, V), own=False)
        V(nc.vector.tensor_copy, sel[:], tile_of(keep["sel_c"][:]))
        for j in range(6):
            c.transpose(ps[:, j // 4, (j % 4) * P:(j % 4 + 1) * P], gst[:, j].rearrange("p s b h -> p (s b h)"), after=(A, V, G))
        A(nc.scalar.copy, g[:, 0:4].rearrange("p j t -> p (j t)"), bank(ps, 0), after=(E, V, G))
        A(nc.scalar.copy, g[:, 4:6].rearrange("p j t -> p (j t)"), bank(ps, 1, 2 * P), own=False)
        for q, (st, out) in enumerate(((kst, kc), (qst, qc))):
            for d0 in range(0, DH2, 4):
                bk = 2 + (d0 // 4) % 4
                for dd in range(4):
                    c.transpose(ps[:, bk, dd * P:(dd + 1) * P], st[:, :, :, :, d0 + dd].rearrange("p s b h -> p (s b h)"),
                                after=(G, A))
                A(nc.scalar.copy, out[:, :, d0:d0 + 4].rearrange("p t d -> p d t"),
                  bank(ps, bk).rearrange("p (d t) -> p d t", d=4), after=(E, V), own=False)
        G(gcopy, turn[:], g[:, 2:4], after=(A,))
        a, b2 = turn, turn2
        sh = 1
        while sh < CH:
            G(gcopy, b2[:, :, 0:sh], a[:, :, 0:sh])
            G(gtt, ta[:, :, sh:], a[:, :, sh:], rep(a[:, 0, 0:CH - sh], 1, 2), ALU.mult, own=False)
            G(gtt, tb[:, :, sh:], a[:, ::-1, sh:], rep(a[:, 1, 0:CH - sh], 1, 2), ALU.mult, own=False)
            G(gtt, b2[:, 0, sh:], ta[:, 0, sh:], tb[:, 0, sh:], ALU.subtract)
            G(gtt, b2[:, 1, sh:], ta[:, 1, sh:], tb[:, 1, sh:], ALU.add, own=False)
            a, b2 = b2, a
            sh *= 2
        G(gts, ta[:], a[:], carry[:, 0:1], None, ALU.mult)
        G(gts, tb[:], a[:, ::-1], carry[:, 1:2], None, ALU.mult, own=False)
        G(gtt, a[:, 0], ta[:, 0], tb[:, 0], ALU.subtract)
        G(gtt, a[:, 1], ta[:, 1], tb[:, 1], ALU.add)
        G(gcopy, carry[:], a[:, :, CH - 1])
        cum = a
        for lo, ci, si in ((0, 0, 1), (H, 1, 0)):
            hp = slice(lo, lo + H)
            V(tt, wt[hp, 0], g[hp, 4], cum[hp, ci], ALU.mult, after=(G, A), own=False)
            V(tt, wt[hp, 1], g[hp, 5], cum[hp, si], ALU.mult, own=False)
            V(tt, w[hp], wt[hp, 0], wt[hp, 1], ALU.subtract if lo == 0 else ALU.add)
        V(tt, w[:], w[:], g[:, 1], ALU.mult)
        V(stt, nbm[:], g[:, 0], -1.0, g[:, 1], ALU.mult, ALU.mult)
        V(tt, nb[:], kc[:], rep(nbm[:], 2, DH2), ALU.mult)
        for t in range(CH):
            V(nc.vector.tensor_tensor_reduce, product[:], yc[:, t], nb[:, t], 1.0, w[:, t:t + 1],
              ALU.mult, ALU.add, u[:, t:t + 1])
            V(ts, scaled[:], yc[:, t], g[:, 0, t:t + 1], None, ALU.mult, own=False)
            V(stt, yc[:, t + 1], kc[:, t], u[:, t:t + 1], scaled[:], ALU.mult, ALU.add)
        V(nc.vector.tensor_copy, yc[:, 0], yc[:, CH])
        V(tt, nb[:], yc[:, 1:], qc[:], ALU.mult, own=False)
        V(nc.vector.tensor_reduce, ret[:], nb[:], AX, ALU.add)
        c.transpose(ps[:, 6, 0:P], ret[:], after=(V, A))
        for k in range(2):
            c.transpose(ps[:, 6, (1 + k) * P:(2 + k) * P], cum[:, k], after=(G,))
        A(nc.scalar.copy, tok[:].rearrange("p s b h -> p (s b h)"), ps[:, 6, 0:P], after=(E, V))
        for k in range(2):
            A(nc.scalar.copy, cs_tok[:, k].rearrange("p b h -> p (b h)"), ps[:, 6, (1 + k) * P:(1 + k) * P + H], own=False)
        re, im, co, si = tok[:, 0], tok[:, 1], cs_tok[:, 0], cs_tok[:, 1]
        for s, (x, y, op) in enumerate((((re, co), (im, si), ALU.add), ((im, co), (re, si), ALU.subtract))):
            V(tt, rt[:, 0], x[0], x[1], ALU.mult, after=(A,))
            V(tt, rt[:, 1], y[0], y[1], ALU.mult, own=False)
            V(tt, rt[:, 0], rt[:, 0], rt[:, 1], op)
            V(tt, ro[:, :, :, s], rt[:, 0], sel[:], ALU.mult, after=(E,))
        for b in range(B):
            c.transpose(ps[0:2 * NH, 7, b * P:(b + 1) * P], ro[:, b].rearrange("p h s -> p (h s)"), after=(V, A))
        A(nc.scalar.copy, keep["ret"][:].rearrange("p b t -> p b t")[:, :, bass.ds(i * P, P)],
          ps[0:2 * NH, 7].rearrange("p (b t) -> p b t", b=B), after=(E,), own=False)


def delta_outputs(c, sb, keep):
    m, nc, ps, d = c.m, c.m.nc, c.ps, c.dram
    V, A, G, E, S = m.V, m.A, m.G, m.E, m.S
    mm, act, tt, ts, stt = (nc.tensor.matmul, nc.scalar.activation, nc.vector.tensor_tensor,
                            nc.vector.tensor_scalar, nc.vector.scalar_tensor_tensor)
    copy = nc.vector.tensor_copy
    F = (P, F2 - P)
    read_w, group, out_w = sb([2 * NH, DI2]), sb([P, P]), sb([P, 2, D])
    gn_w, gn_b, dp = sb([P, 2]), sb([P, 2]), sb([P, 2])
    wr, ebias, pick = sb([P, E2]), sb([P, E2]), sb([E2, E2, P])
    up, down = sb([P, E2, F2], BF16), sb([P, 2, E2, D], BF16)
    sup, sdown = sb([P, F2]), sb([P, 2, D])
    rb = route_buffers(sb, E2)
    for out, name in ((read_w, "readw2"), (group, "c_group"), (gn_w, "gnw2"), (gn_b, "gnb2"), (dp, "dp2"), (wr, "wr2"),
                      (pick, "c_pick"), (sup, "sup2")):
        S.dma(c.q_w, out[:], d[name])
    S.dma(c.q_w, rb["lower"], d["c_lower"])
    S.dma(c.q_w, out_w[:], d["outw2"].rearrange("(k p) n -> p k n", p=P))
    S.dma(c.q_w, ebias[:], d["eb2"].unsqueeze(0).partition_broadcast(P))
    S.dma(c.q_w, sdown[0:F[0], 0], d["sdown2"][0:P, :])
    S.dma(c.q_w, sdown[0:F[1], 1], d["sdown2"][P:F2, :])
    with m.scope() as tmp:
        f_up, f_down = tmp([P, E2, F2]), tmp([P, 2, E2, D])
        S.dma(c.q_w, f_up[:], d["up2"])
        S.dma(c.q_w, f_down[0:F[0], 0], d["down2"][0:P])
        S.dma(c.q_w, f_down[0:F[1], 1], d["down2"][P:F2])
        V(copy, up[:], f_up[:], after=(c.q_w,))
        V(copy, down[0:F[0], 0], f_down[0:F[0], 0])
        V(copy, down[0:F[1], 1], f_down[0:F[1], 1])
    zx = sb([P, 2, 2, T])
    y = sb([P, 2, T])
    sq = sb([P, TB])
    sums, stat, ab = sb([P, 2, 2]), sb([P, 2, 2]), sb([P, 2, 2])
    xn, s_T, tmp_ = sb([P, TB]), sb([P, TB]), sb([P, TB])
    lg, combT = sb([P, NT, E2]), sb([E2, TB])
    xs, hid, rounded = sb([P, 2, TB], BF16), sb([P, 2, 2, TB], BF16), sb([P, TB], BF16)
    hs, acc = sb([P, 2, TB]), sb([P, TB])
    m.barrier()
    with m.loop("layer2_outputs", B) as b:
        S.dma(m.queues["a"], zx[:, 0], keep["z"][:, :, bass.ds(b * T, T)], after=(V,))
        S.dma(m.queues["b"], zx[:, 1], keep["xconv"][:, :, bass.ds(b * T, T)])
        for k in range(2):
            for half in range(2):
                bk = 2 * k + half
                E(mm, bank(ps, bk), read_w[:, k * P:(k + 1) * P],
                  keep["ret"][:, bass.ds(b, 1), half * TB:half * TB + TB].squeeze(1),
                  start=True, stop=True, after=(A, V), own=False, apart=True)
                A(act, y[:, k, half * TB:half * TB + TB], bank(ps, bk), ACT.Copy, accum_out=sums[:, k, half:half + 1],
                  after=(E, V), own=False)
        V(tt, stat[:, 0], sums[:, :, 0], sums[:, :, 1], ALU.add, after=(A,))
        E(mm, ps[:, 4, 0:2], group[:], stat[:, 0], start=True, stop=True, after=(V,))
        V(ts, ab[:, 1], ps[:, 4, 0:2], -1.0, None, ALU.mult, after=(E,))
        for k in range(2):
            for half in range(2):
                A(act, sq[:], y[:, k, half * TB:half * TB + TB], ACT.Square, bias=ab[:, 1, k:k + 1],
                  accum_out=sums[:, k, half:half + 1], after=(V,), own=True)
        V(tt, stat[:, 1], sums[:, :, 0], sums[:, :, 1], ALU.add, after=(A,))
        E(mm, ps[:, 4, 0:2], group[:], stat[:, 1], start=True, stop=True, after=(V,))
        A(act, stat[:, 0], ps[:, 4, 0:2], ACT.Sqrt, bias=c.eps[1e-5][:], after=(E,))
        V(nc.vector.reciprocal, stat[:, 0], stat[:, 0], after=(A,))
        V(tt, ab[:, 0], stat[:, 0], gn_w[:], ALU.mult)
        V(tt, stat[:, 1], ab[:, 1], ab[:, 0], ALU.mult)
        V(tt, stat[:, 1], stat[:, 1], gn_b[:], ALU.add)
        for k in range(2):
            V(ts, y[:, k], y[:, k], ab[:, 0, k:k + 1], stat[:, 1, k:k + 1], ALU.mult, ALU.add)
            V(tt, y[:, k], y[:, k], zx[:, 0, k], ALU.mult, after=(m.queues["a"],))
            V(stt, y[:, k], zx[:, 1, k], dp[:, k:k + 1], y[:, k], ALU.mult, ALU.add, after=(m.queues["b"],))
        for half in range(T // TB):
            hs_ = slice(half * TB, half * TB + TB)
            xb = c.xT[:, bass.ds(b * T + half * TB, TB)]
            V(copy, xn[:], keep["xn"][:, bass.ds(b * T + half * TB, TB)], after=(E,))
            for k in range(2):
                E(mm, bank(ps, 0), out_w[:, k], y[:, k, hs_], start=(k == 0), stop=(k == 1), after=(V, A), own=False)
            V(tt, s_T[:], xn[:], bank(ps, 0), ALU.add, after=(E,))
            for t in range(NT):
                E(mm, ps[:, 1, t * E2:(t + 1) * E2], xn[:, t * P:(t + 1) * P], wr[:], start=True, stop=True, own=False)
            A(act, rb["score"], ps[:, 1, 0:NT * E2].rearrange("p (t e) -> p t e", t=NT), ACT.Sigmoid, after=(E, V))
            V(tt, lg[:], rb["score"], rep(ebias[:], 1, NT), ALU.add, after=(A,))
            route(c, lg[:], rb, 2, False)
            for t in range(NT):
                c.transpose(ps[0:E2, 1, t * P:(t + 1) * P], rb["comb"][:, t], after=(V,))
            A(nc.scalar.copy, combT[:], ps[0:E2, 1, :], after=(E,))
            for k in range(2):
                E(mm, ps[0:F[k], 2 + k, :], sup[:, k * P:k * P + F[k]], xn[:], start=True, stop=True, after=(V, A), own=False)
                A(act, hs[0:F[k], k], ps[0:F[k], 2 + k, :], ACT.Relu, after=(E, V), own=False)
                V(tt, hs[0:F[k], k], hs[0:F[k], k], hs[0:F[k], k], ALU.mult, after=(A,), own=False)
                E(mm, bank(ps, 6), sdown[0:F[k], k], hs[0:F[k], k], start=(k == 0), stop=(k == 1), after=(V,), own=False)
            V(copy, acc[:], bank(ps, 6), after=(E,))
            for e in range(E2):
                E(mm, bank(ps, 1), pick[:, e, :], combT[:], start=True, stop=True, after=(A, V), own=False)
                V(tt, xs[:, e % 2], xn[:], bank(ps, 1), ALU.mult, after=(E,), own=False)
                for k in range(2):
                    E(mm, ps[0:F[k], 2 + k, :], up[:, e, k * P:k * P + F[k]], xs[:, e % 2], start=True, stop=True,
                      after=(V, A), own=False)
                    A(act, hid[0:F[k], e % 2, k], ps[0:F[k], 2 + k, :], ACT.Relu, after=(E, V), own=False)
                    V(tt, hid[0:F[k], e % 2, k], hid[0:F[k], e % 2, k], hid[0:F[k], e % 2, k], ALU.mult, after=(A,), own=False)
                for k in range(2):
                    E(mm, bank(ps, 4), down[0:F[k], k, e], hid[0:F[k], e % 2, k], start=(k == 0), stop=(k == 1), after=(V,), own=False)
                A(nc.scalar.copy, rounded[:], bank(ps, 4), after=(E, V), own=False)
                V(tt, acc[:], acc[:], rounded[:], ALU.add, after=(A,))
            c.update(xb, s_T[:], acc[:], tmp_[:])


def layer2(c):
    m, nc = c.m, c.m.nc
    with m.scope() as sb:
        keep = {"xn": sb([P, B * T]), "ret": sb([2 * NH, B, T]), 
                "z": nc.dram_tensor("z_scratch", (P, 2, B * T), F32, kind="Internal").ap(),
                "xconv": nc.dram_tensor("xconv_scratch", (P, 2, B * T), F32, kind="Internal").ap()}
        with m.scope() as tmp:
            keep.update(k=tmp([P, NTT, DI2]), q=tmp([P, NTT, DI2]), g=tmp([P, 6, NTT, NH]), sel_c=tmp([P, NTT, NH]))
            with m.scope() as tmp2:
                keep.update(v=tmp2([P, NTT, 2 * NH]), gates=tmp2([P, NTT, 7 * NH]))
                with m.scope() as inner:
                    delta_inputs(c, inner, keep)
                with m.scope() as inner:
                    delta_gates(c, inner, keep)
            with m.scope() as inner:
                delta_recurrence(c, inner, keep)
        with m.scope() as inner:
            delta_outputs(c, inner, keep)


PAD = 32
JG = P // PAD
NG = NH // JG
REL = 256
QW = REL + P
NI = T // P
F3 = 384
PARTS = ((1, 1), (1, 2), (2, 1), (2, 2), (1, 3), (3, 1))
KP = P // 2
KR = len(PARTS) * HD


def relative_attention(c, sb, keep):
    m, nc, ps, d = c.m, c.m.nc, c.ps, c.dram
    V, A, G, E, S = m.V, m.A, m.G, m.E, m.S
    mm, act, tt, ts, stt = (nc.tensor.matmul, nc.scalar.activation, nc.vector.tensor_tensor,
                            nc.vector.tensor_scalar, nc.vector.scalar_tensor_tensor)
    gtt = nc.gpsimd.tensor_tensor
    scale = HD ** -0.5
    R = 4
    scratch = nc.dram_tensor("relative_scratch", (R, JG, P, QW), F32, kind="Internal").ap()

    def shifted(r):
        return bass.AP(tensor=scratch.tensor, offset=r * JG * P * QW + P, ap=[[QW - 1, P], [P * QW, JG], [1, REL]])

    wq, wk, wv, rel = sb([P, 2, P]), sb([P, 2, P]), sb([P, JG * HD]), sb([P, 2, REL])
    row0 = sb([P, 2])
    within, other, neg, ident_b, less, head = (sb([P, P]), sb([P, P]), sb([P, P], BF16), sb([P, P], BF16),
                                                  sb([P, 4]), sb([P, 2]))
    x = sb([P, T])
    q, k, rel_b, v = ([sb(*shape) for _ in range(2)] for shape in (
        ([P, JG, 1 + T], BF16), ([P, 2, T], BF16), ([P, 2, REL], BF16), ([P, NI, JG, PAD],)))
    q2, part, rest = sb([P, TB], BF16), sb([P, TB], BF16), sb([P, TB])
    rows = [sb([P, JG, QW]) for _ in range(R)]
    cs = [sb([P, JG, REL]) for _ in range(R)]
    far, two = ([sb([P, JG, P]) for _ in range(R)] for _ in range(2))
    NS = 6
    s = [sb([P, T]) for _ in range(NS)]
    pt = [sb([P, NI, P]) for _ in range(JG)]
    mx, nmax = sb([P, NS, 6]), sb([P, NS, 1])
    out_T, inv = sb([P, P]), sb([P, JG])
    q_in = m.queues["a"]
    q_out, q_back = ([m.queues[f"{n}{r}"] for r in range(R)] for n in ("rel_out", "rel_back"))
    S.dma(c.q_w, within[:], d["c_within"])
    S.dma(c.q_w, less[:], d["c_less"])
    S.dma(c.q_w, head[:], d["c_head"])
    V(ts, neg[:], within[:], -1e9, None, ALU.mult, after=(c.q_w,))
    V(ts, other[:], c.ident[:], -1.0, 1.0, ALU.mult, ALU.add)
    for n in range(2):
        V(nc.vector.memset, q[n][:, :, 0:1], 0.0)
        V(nc.vector.memset, v[n][:], 0.0)
        V(nc.vector.memset, v[n][:, :, :, HD:HD + 1], 1.0)
    V(nc.vector.tensor_copy, ident_b[:], c.ident[:])
    m.barrier()

    def stack(out, src, which, made):
        n = src.shape[1]
        p, r = part[:, 0:n], rest[:, 0:n]
        a = A(nc.scalar.copy, p, src, after=(made, Mark(V)))
        yield
        e = V(stt, r, p, less[:, 2 * which:2 * which + 1], src, ALU.mult, ALU.add, after=(a,))
        yield
        a = A(nc.scalar.copy, p, r, after=(e,))
        yield
        V(stt, out, p, less[:, 2 * which + 1:2 * which + 2], r, ALU.mult, ALU.add, after=(a, Mark(E)))

    def prepare(n, b, g):
        for out, name in ((wq, "wq3"), (wk, "wk3"), (wv, "wv3"), (rel, "rel3")):
            S.dma(q_in, out[:], d[name][bass.ds(g, 1)].squeeze(0), after=(Mark(E), Mark(V), Mark(A)))
        for half in range(2):
            a = A(nc.scalar.copy, x[:, half * TB:(half + 1) * TB], keep["xn"][:, bass.ds(b * T + half * TB, TB)],
                  after=(Mark(E),))
            yield
        V.wait(a)
        V(ts, wq[:], wq[:], scale, None, ALU.mult, after=(q_in,))
        V(nc.vector.tensor_copy, row0[:], rel[:, :, 0])
        V(tt, rel[:], rel[:], rep(row0[:], 2, REL), ALU.subtract)
        V(ts, rel[:, :, 0], row0[:], -1.0, None, ALU.mult)
        yield
        loaded, freed = Mark(V), [Mark(V)]
        for p in range(2):
            yield from stack(rel_b[n][:, p], rel[:, p], 1, Mark(V))
            yield
        for p in range(2):
            for half in range(2):
                h = slice(half * TB, half * TB + TB)
                for which, w, out in ((0, wq, q2[:]), (1, wk, k[n][:, p, h])):
                    e = E(mm, bank(ps, 6), w[:, p], x[:, h], start=True, stop=True, after=(loaded, *freed[-1:]))
                    yield
                    yield from stack(out, bank(ps, 6), which, e)
                    freed.append(Mark(V))
                    if which == 0:
                        for jj in range(2):
                            V(ts, q[n][:, 2 * p + jj, 1 + half * TB:1 + half * TB + TB], q2[:], head[:, jj:jj + 1], None,
                              ALU.mult, own=(jj == 0))
                    yield
        for t in range(NI):
            e = E(mm, ps[:, 6, t * JG * HD:(t + 1) * JG * HD], x[:, t * P:(t + 1) * P], wv[:], start=True, stop=True,
                  after=(freed[-1],) if t == 0 else ())
            if t == NI // 2:
                yield
        yield
        A(nc.scalar.copy, v[n][:, :, :, 0:HD], bank(ps, 6, NI * JG * HD).rearrange("p (t j d) -> p t j d", t=NI, j=JG),
          after=(e,))
        yield

    def relative(quad, made, gone, evac):
        r, i, n = quad % R, quad % NI, quad // NI % 2
        for p in range(2):
            for jj in range(2):
                e = E(mm, ps[:, 7, jj * REL:(jj + 1) * REL], q[n][:, 2 * p + jj, i * P:(i + 1) * P], rel_b[n][:, p],
                      start=True, stop=True, after=(made, evac[-1]) if jj == 0 else ())
            a = A(nc.scalar.copy, rows[r][:, 2 * p:2 * p + 2, 0:REL], ps[:, 7].rearrange("p (j z) -> p j z", j=2),
                  after=(e, q_out[r]))
            evac.append(a)
        e = G(nc.gpsimd.tensor_copy, rows[r][:, :, REL:QW], rows[r][:, :, 0:P], after=(a,), own=False)
        S.dma(q_out[r], scratch[r].rearrange("j p z -> p j z"), rows[r][:], after=(e, a, q_back[r]))
        z = S.dma(q_back[r], cs[r][:], shifted(r), after=(q_out[r], gone, Mark(G)))
        if i >= 2:
            z = G(gtt, two[r][:], cs[r][:, :, P:], rep(other[:], 1, JG), ALU.mult, after=(z, gone), own=False)
        if i >= 4:
            z = G(gtt, far[r][:], cs[r][:, :, P:], rep(within[:], 1, JG), ALU.mult, own=False)
        return z

    for _ in prepare(0, 0, 0):
        pass
    for quad in range(2):
        relative(quad, Mark(V), Mark(V), [Mark(A)])
    m.barrier()
    with m.loop("layer3_attention", B, NG // 2) as (b, gg):
        start = tuple(Mark(x) for x in (E, V, A, G))
        V.wait(*q_back[0:2], G)
        biased = {0: start[1], 1: start[1]}
        quad_done = {}
        scored, done, expd, turned, moved = [], [], [], [], []
        evac = [start[2]]

        def scores(u):
            quad, j = divmod(u, JG)
            i, set_ = quad % NI, quad // NI
            n = (i + 1) * P
            b0 = 2 * (u % 2)
            free = (*expd[u - 2:u - 1], *done[u - 2:u - 1]) if u >= 2 else start
            for lo in range(0, n, TB):
                hi = min(n, lo + TB)
                E(mm, ps[:, b0 + lo // TB, 0:hi - lo], q[set_][:, j, 1 + i * P:1 + (i + 1) * P], k[set_][:, j // 2, lo:hi],
                  start=True, stop=hi < n, after=free)
            scored.append(E(mm, ps[:, b0 + i // 4, (i % 4) * P:(i % 4 + 1) * P], ident_b[:], neg[:], start=False, stop=True))

        def weights(u):
            quad, j = divmod(u, JG)
            i, r, n, b0 = quad % NI, quad % R, u % NS, 2 * (u % 2)
            out, sc = s[n], ps[:, b0:b0 + 2, :].rearrange("p b n -> p (b n)")
            V.wait(scored[u], biased[quad], *(turned[u - NS:u - NS + 1] if u >= NS else start))
            parts = [(i - 1, i + 1, cs[r][:, j, :]) if i else (0, 1, cs[r][:, j, P:])]
            if i >= 2:
                parts.append((i - 2, i - 1, two[r][:, j]))
            if i >= 3:
                parts.append((i - 3, i - 2, cs[r][:, j, 0:P]))
            if i >= 4:
                parts.append((i - 4, i - 3, far[r][:, j]))
            for lo, hi, bias in parts:
                V(tt, out[:, lo * P:hi * P], sc[:, lo * P:hi * P], bias, ALU.add, own=False)
            first = max(0, i - 4) * P
            if first:
                V(nc.vector.tensor_reduce, mx[:, n, 1:2], sc[:, 0:first], AX, ALU.max, own=False)
            V(nc.vector.tensor_reduce, mx[:, n, 0:1], out[:, first:(i + 1) * P], AX, ALU.max)
            done.append(V(nc.vector.tensor_reduce, nmax[:, n], mx[:, n, 0:2 if first else 1], AX, ALU.max, negate=True))
            if j == JG - 1:
                quad_done[quad] = done[-1]
            if first:
                A(act, out[:, 0:first], sc[:, 0:first], ACT.Exp, bias=nmax[:, n], after=(done[u],))
            expd.append(A(act, out[:, first:(i + 1) * P], out[:, first:(i + 1) * P], ACT.Exp, bias=nmax[:, n],
                          after=(done[u],)))

        chunks = [start[2], start[2]]

        def turn(u):
            quad, j = divmod(u, JG)
            i = quad % NI
            src, dst = s[u % NS], pt[j]
            for lo in range(0, i + 1, 4):
                hi = min(i + 1, lo + 4)
                bk = 4 + len(chunks) % 2
                for t in range(lo, hi):
                    e = c.transpose(ps[:, bk, (t - lo) * P:(t - lo + 1) * P], src[:, t * P:(t + 1) * P],
                                    after=(expd[u], chunks[-2]) if t == lo else ())
                chunks.append(A(nc.scalar.copy, dst[:, lo:hi].rearrange("p t n -> p (t n)"), bank(ps, bk, (hi - lo) * P),
                                after=(e, *moved[-1:])))
            turned.append(e)

        def values(quad):
            i, set_ = quad % NI, quad // NI
            last = chunks[-1]
            for t in range(i + 1):
                for j in range(JG):
                    e = E(mm, ps[j * PAD:(j + 1) * PAD, 7, 0:P], v[set_][:, t, j], pt[j][:, t, :], start=(t == 0),
                          stop=(t == i), after=(last, evac[-1]) if t == j == 0 else ())
            moved.append(e)
            yield
            a = A(nc.scalar.copy, out_T[:], ps[:, 7, 0:P], after=(e,))
            e = c.transpose(ps[:, 7, P:2 * P], out_T[:], after=(a,))
            yield
            got = ps[:, 7, P:2 * P].rearrange("p (j n) -> p j n", j=JG)
            V(nc.vector.reciprocal, inv[:], got[:, :, HD], after=(e,))
            to = keep["att"][:, bass.ds(b * NI + i, 1), bass.ds((gg * 2 + set_) * JG * HD, JG * HD)].squeeze(1)
            evac.append(V(tt, to.rearrange("p (j d) -> p j d", j=JG), got[:, :, 0:HD], rep(inv[:], 2, HD), ALU.mult))
            yield

        n_units, quads = 2 * JG * NI, 2 * NI
        nexts = {1: prepare(1, b, gg * 2 + 1), JG * NI + 5: prepare(0, (b + gg) % B, 2 - gg * 2)}
        making, valued = None, None
        operands = [start[1], None]
        for u in range(n_units + 7):
            making = nexts.get(u, making)
            if u % JG == 2 and u // JG + 2 < quads:
                quad = u // JG + 2
                if quad == NI:
                    for _ in making:
                        pass
                    operands[1] = Mark(V)
                biased[quad] = relative(quad, operands[quad // NI], quad_done.get(quad - R, start[1]), evac)
            if u < n_units:
                scores(u)
            if u % JG == 3 and 7 <= u:
                valued = values(u // JG - 1)
                next(valued)
            elif u % JG == 0 and valued:
                next(valued)
            elif u % JG == 1 and valued:
                next(valued)
            if 1 <= u <= n_units:
                weights(u - 1)
            for _ in range(2):
                next(making, None) if making else None
            if 3 <= u < n_units + 3:
                turn(u - 3)
        for _ in making:
            pass
        for quad in range(2):
            relative(2 * NI + quad, Mark(V), quad_done[2 * NI + quad - R], evac)


def layer3(c):
    m, nc, ps, d = c.m, c.m.nc, c.ps, c.dram
    V, A, G, E, S = m.V, m.A, m.G, m.E, m.S
    mm, act, tt, ts = nc.tensor.matmul, nc.scalar.activation, nc.vector.tensor_tensor, nc.vector.tensor_scalar
    with m.scope() as sb:
        keep = {"xn": sb([P, B * T]), "att": sb([P, NTT, D])}
        with m.scope() as tmp:
            xn, ta = tmp([P, TB]), tmp([P, TB])
            with m.loop("layer3_norm", B * T // TB) as n:
                c.layernorm(c.xT[:, bass.ds(n * TB, TB)], xn[:], ta[:], 0)
                V(nc.vector.tensor_copy, keep["xn"][:, bass.ds(n * TB, TB)], xn[:])
        with m.scope() as tmp:
            relative_attention(c, tmp, keep)
        wp, bp = sb([P, D]), sb([P, 1])
        wg, wu, wd = sb([P, F3]), sb([P, F3]), sb([P, F3 // P, D])
        with m.scope() as tmp:
            ints = tmp([P, 3, F3], I32)
            S.dma(c.q_w, wp[:], d["wp3"])
            S.dma(c.q_w, bp[:], d["bp3"])
            S.dma(c.q_w, ints[:, 0], d["gate3"])
            S.dma(c.q_w, ints[:, 1], d["up3"])
            S.dma(c.q_w, ints[:, 2].rearrange("p (k n) -> p k n", k=3), d["down3"].rearrange("(k p) n -> p k n", p=P))
            for k, w in enumerate((wg[:], wu[:], wd[:].rearrange("p k n -> p (k n)"))):
                V(ts, w, ints[:, k], 1.0 / 127.0, None, ALU.mult, after=(c.q_w,))
        att, aT, sT, xn, hid, tmp_ = sb([P, NT, D]), sb([P, TB]), sb([P, TB]), sb([P, TB]), sb([P, 3, TB]), sb([P, TB])
        with m.loop("layer3_ffn", B * T // TB) as n:
            V(nc.vector.tensor_copy, att[:], keep["att"][:, bass.ds(n * NT, NT)], after=(E,))
            V(nc.vector.tensor_copy, xn[:], keep["xn"][:, bass.ds(n * TB, TB)])
            for t in range(NT):
                c.transpose(ps[:, 0, t * P:(t + 1) * P], att[:, t], after=(V, A))
            A(nc.scalar.copy, aT[:], bank(ps, 0), after=(E,))
            E(mm, bank(ps, 1), wp[:], aT[:], start=True, stop=True, after=(A,))
            A(act, sT[:], bank(ps, 1), ACT.Identity, bias=bp[:], after=(E, V))
            for k in range(3):
                b1, b2 = 2 + 2 * (k % 2), 3 + 2 * (k % 2)
                E(mm, bank(ps, b1), wg[:, k * P:(k + 1) * P], xn[:], start=True, stop=True, after=(V, A), own=False)
                E(mm, bank(ps, b2), wu[:, k * P:(k + 1) * P], xn[:], start=True, stop=True, own=False)
                A(act, hid[:, k], bank(ps, b1), ACT.Silu, after=(E, V), own=False)
                V(tt, hid[:, k], hid[:, k], bank(ps, b2), ALU.mult, after=(A,), own=False)
            for k in range(3):
                E(mm, bank(ps, 6), wd[:, k], hid[:, k], start=(k == 0), stop=(k == 2), after=(V,), own=False)
            c.update(c.xT[:, bass.ds(n * TB, TB)], sT[:], bank(ps, 6), tmp_[:])


LAYERS = (0, 1, 2, 3)


def program(nc, dram, out, per_iteration):
    m = Machine(nc, per_iteration)
    c = Common(m, dram)
    c.load_start()
    for k in LAYERS:
        (layer0, layer1, layer2, layer3)[k](c)
    m.barrier()
    m.S.dma(m.queues["out"], out, c.xT[:], after=(m.V,))
    m.S.wait(m.queues["out"])
    m.barrier()
    return m.learned


def constants():
    inv = (1.0 / 10000.0 ** (np.arange(0, 8, 2, dtype=np.float32) / 8)).astype(np.float32)
    f = np.arange(T, dtype=np.float32)[:, None] * inv[None, :]
    cos, sin = np.cos(f).T, np.sin(f).T
    i = np.arange(P)
    out = {
        "c_ident": np.eye(P),
        "c_upper": i[:, None] <= i[None, :],
        "c_cos": np.tile(cos, (32, 1)),
        "c_sin": np.tile(np.concatenate([-sin, sin]), (16, 1)),
        "c_blocks": i[:, None] // HD == i[None, :] // HD,
        "c_before": i[:, None] < i[None, :],
        "c_order": np.tile(np.arange(1, NH + 1), (P, 1)),
        "c_inv_k": np.tile(1.0 / np.arange(1, NH + 1), (P, 1)),
        "c_restart": np.tile(np.arange(NT * NH * NH) % NH != 0, (P, 1)),
        "c_pick": np.repeat(np.eye(E1)[:, :, None], P, 2),
        "c_freqs": np.tile(1.0 / 10000.0 ** (np.arange(NH, dtype=np.float32) / NH), (P, 1)),
        "c_group": (i[:, None] // DH2 == i[None, :] // DH2) / (DH2 * T),
        "c_within": i[None, :] > i[:, None],
        "c_head": i[:, None] // KP == np.arange(2)[None, :],
        "c_lower": np.tile(np.arange(E1)[None, :] < np.arange(E1)[:, None], (P, 1, 1)),
    }
    less = np.zeros((2, KP, 4))
    for n, (pq, pk) in enumerate(PARTS):
        less[:, n * HD:(n + 1) * HD] = [-(pq > 1), -(pq > 2), -(pk > 1), -(pk > 2)]
    out["c_less"] = less.reshape(P, 4)
    return {k: np.ascontiguousarray(v, dtype=np.float32) for k, v in out.items()}


def laid_out(i):
    def columns(v):
        return v.reshape(-1, P).T

    def stacked(w, axis):
        w = np.moveaxis(w, axis, 0).reshape(NG, 2, 2, HD, -1)
        out = np.zeros((NG, 2, 2, KP, w.shape[-1]), w.dtype)
        out[:, :, :, :KR] = np.tile(w, (1, 1, 1, len(PARTS), 1))
        return out.reshape(NG, 2, P, -1)

    partner = np.arange(D).reshape(16, 2, 4)[:, ::-1].reshape(-1)
    wq, zx = i["L0_attn_W_in"][:D], i["L0_attn_W_zxbcdt"]
    a = {
        "xT": i["L0_attn_x"].reshape(B * T, D).T,
        "wq": wq.T, "wqr": wq[partner].T,
        "wz": zx[:DI0].T, "wxbc": zx[DI0:DI0 + 2 * DI0].T, "wdt": zx[3 * DI0:].T,
        "convw0": i["L0_attn_conv_w"].T, "convb0": columns(i["L0_attn_conv_b"]), "dtb": i["L0_attn_dt_bias"],
        "alog": i["L0_attn_A_log"], "D0": columns(np.repeat(i["L0_attn_D_param"], HP)), "npre": columns(i["L0_attn_norm_pre_w"]),
        "ngat": columns(i["L0_attn_norm_gated_w"]), "wout0": i["L0_attn_W_out"].T,
        "fg0": i["L0_ffn_w_gate"], "fu0": i["L0_ffn_w_up"], "fd0": i["L0_ffn_w_down"],
    }
    a.update({
        "wqkv1": np.concatenate([np.tile(i["L1_attn_W" + k].T, (NH, NH)) for k in "qkv"], 1),
        "bqkv1": np.concatenate([np.tile(i["L1_attn_b" + k], NH) for k in "qkv"])[None, :],
        "wr1": i["L1_ffn_router_w"], "w1": i["L1_ffn_w1"], "w3": i["L1_ffn_w3"], "w2": i["L1_ffn_w2"],
    })
    a.update({
        "win2": i["L2_attn_in_proj_w"], "bz2": columns(i["L2_attn_in_proj_b"][:DI2]),
        "bx2": columns(i["L2_attn_in_proj_b"][DI2:2 * DI2]), "bkv2": i["L2_attn_in_proj_b"][None, 2 * DI2:],
        "bg2": i["L2_attn_gate_b"][None, :], "rms2": columns(i["L2_attn_rms_w"]), "convw2": i["L2_attn_conv_w"],
        "convb2": columns(i["L2_attn_conv_b"]), "gatew2": i["L2_attn_gate_w"], "qw2": i["L2_attn_Q_w"],
        "ldt2": i["L2_attn_log_dt_scale"], "readw2": i["L2_attn_readout_w"], "gnw2": columns(i["L2_attn_gn_w"]),
        "gnb2": columns(i["L2_attn_gn_b"]), "dp2": columns(i["L2_attn_D_param"]), "outw2": i["L2_attn_out_w"],
        "wr2": i["L2_ffn_gate_w"].T, "eb2": i["L2_ffn_expert_bias"],
        "up2": i["L2_ffn_w_up"].transpose(2, 0, 1), "down2": i["L2_ffn_w_down"].transpose(2, 0, 1),
        "sup2": i["L2_ffn_shared_w_up"].T, "sdown2": i["L2_ffn_shared_w_down"].T,
    })
    a.update({
        "wq3": stacked(i["L3_attn_Wq"], 0).transpose(0, 3, 1, 2), "wk3": stacked(i["L3_attn_Wk"], 0).transpose(0, 3, 1, 2),
        "wv3": i["L3_attn_Wv"].reshape(NG, JG * HD, D).transpose(0, 2, 1), "rel3": stacked(i["L3_attn_rel_embed"], 1).transpose(0, 2, 1, 3),
        "wp3": i["L3_attn_Wp"].T, "bp3": columns(i["L3_attn_bp"]),
        "gate3": i["L3_ffn_w_gate"].T, "up3": i["L3_ffn_w_up"].T, "down3": i["L3_ffn_w_down"].T,
    })
    return {k: np.ascontiguousarray(v) for k, v in a.items()}


def kernel(**inputs):
    import concourse.bacc as bacc
    from concourse.bass_utils import run_bass_kernel_spmd as run

    arrays = {**laid_out({k: np.asarray(v) for k, v in inputs.items()}), **constants()}

    def build(per_iteration):
        nc = bacc.Bacc("TRN2", target_bir_lowering=False, num_devices=1)
        dram = {k: nc.dram_tensor("in_" + k, v.shape, mybir.dt.from_np(v.dtype), kind="ExternalInput").ap()
                for k, v in arrays.items()}
        out = nc.dram_tensor("out", (D, B * T), F32, kind="ExternalOutput").ap()
        return nc, program(nc, dram, out, per_iteration)

    _, per_iteration = build({})
    nc, _ = build(per_iteration)
    r = run(nc, [{"in_" + k: v for k, v in arrays.items()}], core_ids=[0])
    return np.ascontiguousarray(r.results[0]["out"].T).reshape(B, T, D)
```

```python
from contextlib import ExitStack, contextmanager

import concourse.bass as bass
import numpy as np
from concourse import mybir

F32 = mybir.dt.float32
BF16 = mybir.dt.bfloat16
I32 = mybir.dt.int32
ALU = mybir.AluOpType
ACT = mybir.ActivationFunctionType
AX = mybir.AxisListType.X
P = 128
D = 128
B, T = 4, 1024
TB = 512
NT = TB // P
LN_EPS = 1e-5


class Part:
    now = None

    def __init__(self, m, steps, per_turn):
        self.steps, self.per_turn = steps, per_turn
        self.issued = {x.name: x.n for x in (*m.engines, *m.queues.values())}

    def turn(self):
        Part.now = self
        more = all(next(self.steps, "end") != "end" for _ in range(self.per_turn))
        Part.now = None
        return more


def woven(m, *parts):
    live = [Part(m, *part) for part in parts]
    while live:
        live = [part for part in live if part.turn()]


class Mark:

    def __init__(self, src):
        self.src, self.loop = src, src.loop
        self.n = Part.now.issued[src.name] if Part.now else src.n


class Counted:

    def __init__(self, nc, name, step=1):
        self.sem = nc.alloc_semaphore(name)
        nc.sync.sem_inc(self.sem, step)
        self.name, self.step, self.n, self.loop, self.per, self.base = name, step, step, None, 0, 0

    def value(self, n, loop):
        if loop is None:
            return n
        assert loop is self.loop, "a mark from a loop's body is used outside of it"
        return loop * self.per + n

    def raise_by(self, ins):
        ins.then_inc(self.sem, self.step)
        self.n += self.step
        if Part.now:
            Part.now.issued[self.name] = self.n


class Engine(Counted):

    def __init__(self, nc, eng, name):
        super().__init__(nc, name)
        self.eng, self.seen, self.apart, self.spare = eng, {}, False, None
        self.each_apart, self.in_chain = False, True

    def wait(self, *sources):
        for s in sources:
            m = s if isinstance(s, Mark) else Mark(s)
            key = (m.src.name, m.loop is None)
            if self.seen.get(key, -1) >= m.n:
                continue
            self.seen[key] = m.n
            self.eng.wait_ge(m.src.sem, m.src.value(m.n, m.loop))
            if self.each_apart and self.loop is not None:
                self.eng.sem_inc(self.spare.sem, 1)

    def __call__(self, op, *args, after=(), own=None, apart=False, **kw):
        self.wait(*after)
        if own or (own is None and self.in_chain):
            self.wait(self)
        if self.loop is not None and (apart or self.apart):
            self.eng.sem_inc(self.spare.sem, 1)
        self.raise_by(op(*args, **kw))
        return Mark(self)

    def dma(self, queue, out, in_, after=()):
        self.wait(*after)
        queue.raise_by(self.eng.dma_start(out, in_))
        return Mark(queue)


class Machine:

    def __init__(self, nc, per_iteration):
        self.nc, self.per_iteration, self.learned = nc, per_iteration, {}
        self.V = Engine(nc, nc.vector, "vector_done")
        self.A = Engine(nc, nc.scalar, "scalar_done")
        self.G = Engine(nc, nc.gpsimd, "gpsimd_done")
        self.E = Engine(nc, nc.tensor, "tensor_done")
        self.S = Engine(nc, nc.sync, "sync_done")
        self.engines = (self.V, self.A, self.G, self.E, self.S)
        self.queues = {}
        spare = Counted(nc, "spare")
        for e in self.engines:
            e.spare = spare
        self.G.apart = self.S.each_apart = True
        self.E.in_chain = self.A.in_chain = False
        self.n_names = 0

    def queue(self, name):
        if name not in self.queues:
            self.queues[name] = Counted(self.nc, "dma_" + name, 16)
        return self.queues[name]

    @contextmanager
    def loop(self, name, n, inner=None):
        every = list(self.engines) + list(self.queues.values())
        per = self.per_iteration.get(name, {})
        with ExitStack() as st:
            i = at = st.enter_context(self.nc.Fori(0, n))
            if inner:
                j = st.enter_context(self.nc.Fori(0, inner))
                i, at, n = i * inner + j, (i, j), n * inner
            for c in every:
                assert c.loop is None
                c.loop, c.per, c.base = i, per.get(c.name, 0), c.n
            for e in self.engines:
                e.seen = {}
            yield at
            assert all(q in every for q in self.queues.values()), "make queues ahead of a loop"
            self.learned[name] = {c.name: c.n - c.base for c in every}
        for c in every:
            c.n, c.loop = c.base + n * (c.n - c.base), None
        for e in self.engines:
            e.seen = {}

    def barrier(self):
        for e in self.engines:
            e.wait(*self.engines, *self.queues.values())

    @contextmanager
    def scope(self):
        with ExitStack() as st:
            def sb(shape, dt=F32):
                self.n_names += 1
                return st.enter_context(self.nc.sbuf_tensor(f"t{self.n_names}", list(shape), dt))
            yield sb
            self.barrier()


def rep(ap, axis, n):
    v = ap.unsqueeze(axis)
    shape = list(v.shape)
    shape[axis] = n
    return v.broadcast_to(shape)


def bank(ps, k, n=TB):
    return ps[:, k, 0:n]


class Common:

    def __init__(self, m, dram):
        nc = m.nc
        self.m, self.dram = m, dram
        self.ps = nc.alloc_psum_tensor("banks", [P, 8, TB], F32)
        self.xT = nc.alloc_sbuf_tensor("xT", [P, B * T], F32)
        self.ident = nc.alloc_sbuf_tensor("ident", [P, P], F32)
        self.mean_d = nc.alloc_sbuf_tensor("mean_d", [P, P], F32)
        self.eps = {v: nc.alloc_sbuf_tensor(f"eps{k}", [P, 1], F32) for k, v in enumerate((1e-5, 1e-6))}
        self.one = nc.alloc_sbuf_tensor("one", [P, 1], F32)
        self.q_w = m.queue("weights")
        m.queue("out")
        for k in ("a", "b", "c", "d", *(f"rel_{n}{r}" for n in ("out", "back") for r in range(4))):
            m.queue(k)

    def load_start(self):
        m, nc = self.m, self.m.nc
        m.S.dma(self.q_w, self.xT[:], self.dram["xT"])
        m.S.dma(self.q_w, self.ident[:], self.dram["c_ident"])
        m.V(nc.vector.memset, self.mean_d[:], 1.0 / D, own=False)
        m.V(nc.vector.memset, self.one[:], 1.0, own=False)
        for v, t in self.eps.items():
            m.V(nc.vector.memset, t[:], v, own=False)
        m.barrier()

    def layernorm(self, x, xn, tmp, bk):
        for _ in self.layernorm_steps(x, xn, tmp, bk):
            pass

    def layernorm_steps(self, x, xn, tmp, bk):
        m, nc = self.m, self.m.nc
        V, A, E = m.V, m.A, m.E
        E(nc.tensor.matmul, bank(self.ps, bk), self.mean_d[:], x, start=True, stop=True, after=(V, A))
        yield
        V(nc.vector.tensor_tensor, xn, x, bank(self.ps, bk), ALU.subtract, after=(E, A))
        yield
        yield from self.inverse_rms_steps(xn, tmp, bk, LN_EPS)
        V(nc.vector.tensor_tensor, xn, xn, tmp, ALU.mult)

    def inverse_rms(self, x, out, bk, eps):
        for _ in self.inverse_rms_steps(x, out, bk, eps):
            pass

    def inverse_rms_steps(self, x, out, bk, eps):
        m, nc = self.m, self.m.nc
        V, A, E = m.V, m.A, m.E
        A(nc.scalar.activation, out, x, ACT.Square, after=(V, E))
        yield
        E(nc.tensor.matmul, bank(self.ps, bk), self.mean_d[:], out, start=True, stop=True, after=(A, V))
        yield
        A(nc.scalar.activation, out, bank(self.ps, bk), ACT.Sqrt, bias=self.eps[eps][:], after=(E, V))
        yield
        V(nc.vector.reciprocal, out, out, after=(A,))
        yield

    def transpose(self, out, in_, after=()):
        k = in_.shape[0]
        return self.m.E(self.m.nc.tensor.transpose, out, in_, self.ident[0:k, 0:k], after=after)

    def update(self, x, s, g_ps, tmp):
        m, nc = self.m, self.m.nc
        m.A(nc.scalar.activation, tmp, g_ps, ACT.Silu, after=(m.E, m.V))
        m.V(nc.vector.tensor_tensor, tmp, tmp, s, ALU.mult, after=(m.A,))
        m.V(nc.vector.tensor_tensor, x, x, tmp, ALU.add)


H0, HP = 4, 64
DI0 = H0 * HP
FF0 = 352
QB = 16


def fp4(c, src, out, w, after):
    m, nc = c.m, c.m.nc
    V, A, G = m.V, m.A, m.G
    n = src.shape[0]
    nb = src.shape[1] // QB
    s3 = src.rearrange("p (b k) -> p b k", k=QB)
    o3 = out.rearrange("p (b k) -> p b k", k=QB)
    scale, inv = w["scale"][0:n, 0:nb], w["inv"][0:n, 0:nb]
    mag, fine, coarse, sign = (w[k][0:n, 0:nb * QB] for k in ("mag", "fine", "coarse", "sign"))
    mag3 = mag.rearrange("p (b k) -> p b k", k=QB)
    A(nc.scalar.activation, sign, src, ACT.Sign, after=(*after, V))
    A(nc.scalar.activation, mag, src, ACT.Abs, after=(G,))
    V(nc.vector.tensor_reduce, scale, s3, AX, ALU.max, apply_absolute_value=True, after=after)
    V(nc.vector.tensor_scalar, scale, scale, 1.0 / 6.0, 1e-12, ALU.mult, ALU.max)
    V(nc.vector.reciprocal, inv, scale)
    V(nc.vector.tensor_tensor, mag3, mag3, rep(inv, 2, QB), ALU.mult, after=(A,))
    yield
    V(nc.vector.tensor_scalar, coarse, mag, 5.0, 2.0, ALU.is_gt, ALU.mult)
    V(nc.vector.tensor_scalar, fine, mag, 0.25, None, ALU.is_gt, own=False)
    for mid in (2.5, 3.5):
        V(nc.vector.scalar_tensor_tensor, coarse, mag, mid, coarse, ALU.is_gt, ALU.add)
    yield
    for mid in (0.75, 1.25, 1.75):
        V(nc.vector.scalar_tensor_tensor, fine, mag, mid, fine, ALU.is_gt, ALU.add)
    yield
    V(nc.vector.scalar_tensor_tensor, fine, coarse, 2.0, fine, ALU.mult, ALU.add)
    V(nc.vector.tensor_scalar, scale, scale, 0.5, None, ALU.mult, own=False)
    V(nc.vector.tensor_tensor, fine, fine, sign, ALU.mult, after=(A,))
    V(nc.vector.tensor_tensor, o3, fine.rearrange("p (b k) -> p b k", k=QB), rep(scale, 2, QB), ALU.mult)


def layer0(c):
    m, nc, ps, d = c.m, c.m.nc, c.ps, c.dram
    V, A, G, E, S = m.V, m.A, m.G, m.E, m.S
    mm, act, tt, ts, stt = (nc.tensor.matmul, nc.scalar.activation, nc.vector.tensor_tensor,
                            nc.vector.tensor_scalar, nc.vector.scalar_tensor_tensor)
    with m.scope() as sb:
        wq, wqr = sb([P, D]), sb([P, D])
        wz, wxbc = sb([P, DI0]), sb([P, 4, 2 * DI0])
        wdt, wout = sb([P, H0]), sb([P, 2, D])
        cos, sin = sb([P, T]), sb([P, T])
        upper = sb([P, P])
        conv_b, npre, ngat, dcol = sb([P, 4]), sb([P, 1]), sb([P, 2]), sb([P, 2])
        dtb, neg_a = sb([P, H0]), sb([P, H0])
        wg, wu, wd = sb([P, FF0]), sb([P, FF0]), sb([P, 3, D])
        mean_di = sb([P, P])
        with m.scope() as tmp:
            raw, taps = tmp([P, 2 * DI0]), tmp([P, 4, 2 * DI0])
            wrow, wquant, wdrow, wdq = tmp([P, 2, 3, D]), tmp([P, D]), tmp([P, FF0]), tmp([P, FF0])
            w = {k: tmp([P, FF0]) for k in ("mag", "fine", "coarse", "sign")}
            w.update(scale=tmp([P, FF0 // QB]), inv=tmp([P, FF0 // QB]))
            for out, name in ((wq, "wq"), (wqr, "wqr"), (wz, "wz"), (wdt, "wdt"), (cos, "c_cos"), (sin, "c_sin"),
                              (upper, "c_upper"), (raw, "wxbc"), (wdrow, "fd0")):
                S.dma(c.q_w, out[:], d[name])
            S.dma(c.q_w, wout[:], d["wout0"].rearrange("(k p) n -> p k n", p=P))
            S.dma(c.q_w, conv_b[:], d["convb0"])
            S.dma(c.q_w, npre[:], d["npre"])
            S.dma(c.q_w, ngat[:], d["ngat"])
            for k in range(4):
                S.dma(c.q_w, taps[:, k, :], d["convw0"][k:k + 1, :].partition_broadcast(P))
            S.dma(c.q_w, dcol[:], d["D0"])
            S.dma(c.q_w, dtb[:], d["dtb"].unsqueeze(0).partition_broadcast(P))
            S.dma(c.q_w, neg_a[:], d["alog"].unsqueeze(0).partition_broadcast(P))
            for g, name in enumerate(("fg0", "fu0")):
                for k in range(3):
                    n = min(P, FF0 - k * P)
                    S.dma(c.q_w, wrow[0:n, g, k, :], d[name][k * P:k * P + n, :])
            V(nc.vector.memset, mean_di[:], 1.0 / DI0)
            for k in range(4):
                V(tt, wxbc[:, k, :], raw[:], taps[:, k, :], ALU.mult, after=(c.q_w,), own=False)
            A(act, neg_a[:], neg_a[:], ACT.Exp, after=(c.q_w,))
            V(ts, neg_a[:], neg_a[:], -1.0, None, ALU.mult, after=(A,))
            for g, out in enumerate((wg, wu)):
                for k in range(3):
                    n = min(P, FF0 - k * P)
                    for _ in fp4(c, wrow[0:n, g, k, :], wquant[0:n, :], w, (c.q_w, E)):
                        pass
                    c.transpose(ps[:, 0, 0:n], wquant[0:n, :], after=(V,))
                    V(nc.vector.tensor_copy, out[:, k * P:k * P + n], ps[:, 0, 0:n], after=(E,))
            for _ in fp4(c, wdrow[:], wdq[:], w, (c.q_w,)):
                pass
            for k in range(3):
                n = min(P, FF0 - k * P)
                c.transpose(ps[0:n, 0, 0:P], wdq[:, k * P:k * P + n], after=(V,))
                V(nc.vector.tensor_copy, wd[0:n, k, :], ps[0:n, 0, 0:P], after=(E,))

        xn, q, gate = (sb([P, 2, TB]) for _ in range(3))
        hp, ta = sb([P, 3 + TB]), sb([P, TB])
        zs, xbc, y = sb([P, 2, TB]), sb([P, 4, TB]), sb([P, 2, TB])
        dt, adt, t16 = sb([P, NT, H0]), sb([P, NT, H0]), sb([P, NT, H0])
        xdt, xdd, btok = sb([P, H0, HP]), sb([P, H0, HP]), sb([P, P])
        acs, dd = sb([P, H0]), sb([P, H0])
        ua, low, ce, mt = sb([P, H0, P]), sb([P, H0, P]), sb([P, H0, P]), sb([P, H0, P])
        ec, gm = sb([P, H0, P]), sb([P, P])
        state = sb([P, H0, HP])
        ones = sb([P, P])
        V(nc.vector.memset, ones[:], 1.0)
        ws = [{k: sb([P, FF0]) for k in ("mag", "fine", "coarse", "sign")} for _ in range(2)]
        for w in ws:
            w.update(scale=sb([P, FF0 // QB]), inv=sb([P, FF0 // QB]))
        bufs = [[sb(shape) for shape in ([P, D], [P, D], [P, P], [P, FF0], [P, FF0], [P, 3, TB])] for _ in range(2)]

        def mixer(half):
            x = xn[:, half]
            E(mm, bank(ps, 0), wq[:], x, start=True, stop=True, after=(V, A))
            E(mm, bank(ps, 1), wqr[:], x, start=True, stop=True)
            yield
            at = slice(half * TB, half * TB + TB)
            V(tt, q[:, half], bank(ps, 0), cos[:, at], ALU.mult, after=(E,))
            V(tt, ta[:], bank(ps, 1), sin[:, at], ALU.mult, own=False)
            V(tt, q[:, half], q[:, half], ta[:], ALU.add)
            yield
            if half == 0:
                V(nc.vector.memset, hp[:, 0:3], 0.0, after=(E,))
            else:
                V(nc.vector.tensor_copy, hp[:, 0:3], hp[:, TB:TB + 3], after=(E,))
            yield from c.inverse_rms_steps(q[:, half], ta[:], 0, 1e-5)
            V(stt, hp[:, 3:], q[:, half], npre[:], ta[:], ALU.mult, ALU.mult)
            yield
            for k in range(2):
                e = E(mm, bank(ps, k), wz[:, k * P:(k + 1) * P], hp[:, 3:], start=True, stop=True, after=(V, A))
            yield
            for k in range(2):
                A(act, zs[:, k, :], bank(ps, k), ACT.Silu, after=(e, V), own=False)
            for k in range(4):
                bk = (2, 3, 0, 1)[k]
                for j in range(4):
                    e = E(mm, bank(ps, bk), wxbc[:, j, k * P:(k + 1) * P], hp[:, j:j + TB],
                          start=(j == 0), stop=(j == 3), after=(A,) if j == 0 and k >= 2 else ())
                A(act, xbc[:, k, :], bank(ps, bk), ACT.Silu, bias=conv_b[:, k:k + 1], after=(e, V), own=False)
                yield
            for t in range(NT):
                E(mm, ps[:, 2, H0 * t:H0 * t + H0], hp[:, 3 + t * P:3 + (t + 1) * P], wdt[:],
                  start=True, stop=True, after=(A,) if t == 0 else ())
            yield
            V(tt, dt[:], ps[:, 2, 0:NT * H0].rearrange("p (t h) -> p t h", h=H0), rep(dtb[:], 1, NT),
              ALU.add, after=(E,))
            V(stt, t16[:], dt[:], -1.0, dt[:], ALU.mult, ALU.max)
            yield
            A(act, t16[:], t16[:], ACT.Exp, scale=-1.0, after=(V,))
            A(act, t16[:], t16[:], ACT.Ln, bias=c.one[:], own=True)
            yield
            V(stt, dt[:], dt[:], 0.0, t16[:], ALU.max, ALU.add, after=(A,))
            V(tt, adt[:], dt[:], rep(neg_a[:], 1, NT), ALU.mult)
            for t in range(NT):
                ct = slice(t * P, (t + 1) * P)
                first = half == 0 and t == 0
                for k in range(3):
                    c.transpose(ps[:, 0, k * P:(k + 1) * P], xbc[:, k, ct], after=(A, V))
                V(tt, xdt[:], ps[:, 0, 0:DI0].rearrange("p (h q) -> p h q", h=H0), rep(dt[:, t, :], 2, HP),
                  ALU.mult, after=(E,))
                V(nc.vector.tensor_copy, btok[:], ps[:, 0, DI0:DI0 + P], own=False)
                yield
                G(nc.gpsimd.tensor_tensor, ua[:], rep(upper[:], 1, H0), rep(adt[:, t, :], 2, P), ALU.mult, after=(E, V))
                E(mm, ps[:, 1, P:P + H0], upper[:], adt[:, t, :], start=True, stop=True, after=(V,))
                E(mm, bank(ps, 2), ones[:], ua[:].rearrange("p h t -> p (h t)"), start=True, stop=True, after=(G,))
                E(mm, ps[:, 1, 0:P], xbc[:, 2, ct], xbc[:, 3, ct], start=True, stop=True, own=False)
                yield
                rows = bank(ps, 2).rearrange("p (h t) -> p h t", h=H0)
                V(nc.vector.tensor_copy, acs[:], ps[:, 1, P:P + H0], after=(E,))
                V(tt, gm[:], ps[:, 1, 0:P], upper[:], ALU.mult, own=False)
                for h in range(H0):
                    V(ts, low[:, h, :], rows[:, h, :], acs[:, h:h + 1], 0.0, ALU.subtract, ALU.min, own=(h == 0))
                V(tt, dd[:], rows[:, :, P - 1], acs[:], ALU.subtract, own=False)
                yield
                A(act, ec[:], rows, ACT.Exp, after=(E, V))
                A(act, low[:], low[:], ACT.Exp, own=False)
                A(act, dd[:], dd[:], ACT.Exp, own=False)
                yield
                V(tt, mt[:], low[:], rep(gm[:], 1, H0), ALU.mult, after=(A,))
                G(nc.gpsimd.tensor_tensor, ce[:], ec[:], rep(xbc[:, 3, ct], 1, H0), ALU.mult, after=(A, E), own=False)
                V(tt, xdd[:], xdt[:], rep(dd[:], 2, HP), ALU.mult, own=False)
                yield
                for h in range(H0):
                    o = ps[(h % 2) * HP:(h % 2 + 1) * HP, 3, (h // 2) * P:(h // 2 + 1) * P]
                    E(mm, o, xdt[:, h, :], mt[:, h, :], start=True, stop=first, after=(V,))
                    if not first:
                        E(mm, o, state[:, h, :], ce[:, h, :], start=False, stop=True, after=(G,))
                E(mm, ps[:, 1, DI0:2 * DI0], btok[:], xdd[:].rearrange("p h q -> p (h q)"), start=True, stop=True)
                yield
                for k in range(2):
                    V(stt, y[:, k, ct], xbc[:, k, ct], dcol[:, k:k + 1], ps[:, 3, k * P:(k + 1) * P],
                      ALU.mult, ALU.add, after=(E,), own=False)
                new = ps[:, 1, DI0:2 * DI0].rearrange("p (h q) -> p h q", h=H0)
                if first:
                    V(nc.vector.tensor_copy, state[:], new)
                else:
                    V(tt, state[:], state[:], rep(ec[:, :, P - 1], 2, HP), ALU.mult)
                    V(tt, state[:], state[:], new, ALU.add)
                yield
            V(tt, y[:], y[:], zs[:], ALU.mult)
            for k in range(2):
                A(act, zs[:, k, :], y[:, k, :], ACT.Square, after=(V,))
                E(mm, bank(ps, 0), mean_di[:], zs[:, k, :], start=(k == 0), stop=(k == 1), after=(A,))
            A(act, ta[:], bank(ps, 0), ACT.Sqrt, bias=c.eps[1e-5][:], after=(E,))
            yield
            V(nc.vector.reciprocal, ta[:], ta[:], after=(A,))
            for k in range(2):
                V(stt, y[:, k, :], y[:, k, :], ngat[:, k:k + 1], ta[:], ALU.mult, ALU.mult)
                E(mm, bank(ps, 1), wout[:, k, :], y[:, k, :], start=(k == 0), stop=(k == 1), after=(V,))
            V(tt, q[:, half], q[:, half], bank(ps, 1), ALU.add, after=(E,))
            yield

        def ffn(half):
            w, b0, b1 = ws[half], 4 + 2 * half, 5 + 2 * half
            xt, xq, xqT, hid, hq, hqT = bufs[half]
            for t in range(NT):
                ct = slice(t * P, (t + 1) * P)
                c.transpose(ps[:, b0, 0:P], xn[:, half, ct], after=(V, A))
                A(nc.scalar.copy, xt[:], ps[:, b0, 0:P], after=(E, V))
                yield
                yield from fp4(c, xt[:], xq[:], w, (A,))
                yield
                c.transpose(ps[:, b0, 0:P], xq[:], after=(V,))
                A(nc.scalar.copy, xqT[:], ps[:, b0, 0:P], after=(E,))
                yield
                E(mm, ps[:, b0, 0:FF0], xqT[:], wg[:], start=True, stop=True, after=(A,))
                E(mm, ps[:, b1, 0:FF0], xqT[:], wu[:], start=True, stop=True)
                yield
                A(act, hid[:], ps[:, b0, 0:FF0], ACT.Silu, after=(E, V))
                V(tt, hid[:], hid[:], ps[:, b1, 0:FF0], ALU.mult, after=(A,))
                yield
                yield from fp4(c, hid[:], hq[:], w, (A,))
                yield
                for k in range(3):
                    n = min(P, FF0 - k * P)
                    c.transpose(ps[0:n, b0, k * P:(k + 1) * P], hq[:, k * P:k * P + n], after=(V, A))
                yield
                turned = bank(ps, b0, 3 * P).rearrange("p (k t) -> p k t", k=3)
                A(nc.scalar.copy, hqT[:, 0:2, ct], turned[:, 0:2, :], after=(E,))
                A(nc.scalar.copy, hqT[0:n, 2, ct], turned[0:n, 2, :])
                yield
            for k in range(3):
                n = min(P, FF0 - k * P)
                E(mm, bank(ps, b1), wd[0:n, k, :], hqT[0:n, k, :], start=(k == 0), stop=(k == 2), after=(A, V))
            yield
            A(act, gate[:, half], bank(ps, b1), ACT.Silu, after=(E, V))

        def both_mixers():
            for half in range(2):
                yield from mixer(half)

        with m.loop("layer0", B) as b:
            xb = c.xT[:, bass.ds(b * T, T)].rearrange("p (h n) -> p h n", h=2)
            woven(m, *((c.layernorm_steps(xb[:, half], xn[:, half], gate[:, half], half), 1) for half in range(2)))
            woven(m, (both_mixers(), 1), (ffn(0), 1), (ffn(1), 1))
            V(tt, gate[:], gate[:], q[:], ALU.mult, after=(A,))
            V(tt, xb, xb, gate[:], ALU.add)


NH = 16
HD = D // NH
E1, F1 = 8, 256
ATTN_SCALE1 = D ** -0.5 / 2.0


def route(c, logits, w, keep, softmax):
    m, nc = c.m, c.m.nc
    V, A = m.V, m.A
    tt = nc.vector.tensor_tensor
    n = logits.shape[2]
    lj, le = rep(logits, 2, n), rep(logits, 3, n)
    V(tt, w["beats"], lj, le, ALU.is_equal, own=True)
    V(tt, w["beats"], w["beats"], rep(w["lower"], 1, NT), ALU.mult)
    V(tt, w["more"], lj, le, ALU.is_gt, own=False)
    V(tt, w["beats"], w["beats"], w["more"], ALU.add)
    V(nc.vector.tensor_reduce, w["rank"], w["beats"], AX, ALU.add)
    if softmax:
        V(nc.vector.tensor_reduce, w["top"], logits, AX, ALU.max, own=False)
        V(tt, w["score"], logits, rep(w["top"], 2, n), ALU.subtract)
        e = A(nc.scalar.activation, w["score"], w["score"], ACT.Exp, after=(Mark(V),), own=False)
        V(nc.vector.scalar_tensor_tensor, w["comb"], w["rank"], float(keep), w["score"], ALU.is_lt, ALU.mult, after=(e,))
        V(nc.vector.tensor_reduce, w["top"], w["comb"], AX, ALU.add)
        V(nc.vector.reciprocal, w["top"], w["top"])
        return V(tt, w["comb"], w["comb"], rep(w["top"], 2, n), ALU.mult)
    return V(nc.vector.scalar_tensor_tensor, w["comb"], w["rank"], float(keep), w["score"], ALU.is_lt, ALU.mult)


def route_buffers(sb, n):
    w = {k: sb([P, NT, n])[:] for k in ("rank", "score", "comb")}
    w.update(top=sb([P, NT])[:], beats=sb([P, NT, n, n])[:], more=sb([P, NT, n, n])[:], lower=sb([P, n, n])[:])
    return w


def sort_descending(c, a, b, n):
    V, tt = c.m.V, c.m.nc.vector.tensor_tensor
    size = 2
    while size <= n:
        step = size
        while step >= 2:
            va, vb = (x.rearrange("p (r k) -> p r k", k=step) for x in (a, b))
            h = step // 2
            if step == size:
                hi = slice(step - 1, h - 1 if h > 0 else None, -1)
            else:
                hi = slice(h, step)
            V(tt, vb[:, :, 0:h], va[:, :, 0:h], va[:, :, hi], ALU.max)
            V(tt, vb[:, :, hi], va[:, :, 0:h], va[:, :, hi], ALU.min, own=False)
            a, b = b, a
            step //= 2
        size *= 2
    return a, b


def layer1(c):
    m, nc, ps, d = c.m, c.m.nc, c.ps, c.dram
    V, A, G, E, S = m.V, m.A, m.G, m.E, m.S
    mm, act, tt, ts, stt = (nc.tensor.matmul, nc.scalar.activation, nc.vector.tensor_tensor,
                            nc.vector.tensor_scalar, nc.vector.scalar_tensor_tensor)
    reduce, copy = nc.vector.tensor_reduce, nc.vector.tensor_copy
    with m.scope() as sb:
        wqkv, bias, ones = sb([P, 3 * D]), sb([1, 3 * D]), sb([1, P])
        wr, w1, w3, w2 = sb([P, E1]), sb([P, E1, F1]), sb([P, E1, F1]), sb([P, F1 // P, E1, D])
        blocks, before = sb([P, P]), sb([P, P])
        order, restart, inv_k = sb([P, NH]), sb([P, NT * NH * NH]), sb([P, NH])
        pick = sb([P, E1, P])
        rb = route_buffers(sb, E1)
        for out, name in ((wqkv, "wqkv1"), (bias, "bqkv1"), (blocks, "c_blocks"), (before, "c_before"),
                          (order, "c_order"), (inv_k, "c_inv_k"), (restart, "c_restart"), (wr, "wr1")):
            S.dma(c.q_w, out[:], d[name])
        S.dma(c.q_w, rb["lower"], d["c_lower"])
        V(nc.vector.memset, pick[:], 0.0)
        S.dma(c.q_w, pick[0:E1], d["c_pick"], after=(V,))
        S.dma(c.q_w, w1[:], d["w1"].rearrange("e h f -> h e f"))
        S.dma(c.q_w, w3[:], d["w3"].rearrange("e h f -> h e f"))
        for k in range(F1 // P):
            S.dma(c.q_w, w2[:, k], d["w2"][:, k * P:(k + 1) * P, :].rearrange("e f h -> f e h"))
        V(nc.vector.memset, ones[:], 1.0)
        for k in range(3):
            V(tt, wqkv[:, k * D:(k + 1) * D], wqkv[:, k * D:(k + 1) * D], blocks[:], ALU.mult, after=(c.q_w,))

        xn, tmp, s_T, out = (sb([P, 2, TB]) for _ in range(4))
        xm = sb([P, P])
        of_half = [dict(qkv=sb([P, NT, 3 * D]), prod=[sb([P, NH * NH * HD]) for _ in range(2)],
                        grids=[sb([P, NT, NH, NH]) for _ in range(6)], one=sb([P, NT * NH]), s_tok=sb([P, NT, D]))
                   for _ in range(2)]
        lg, combT = sb([P, NT, E1]), sb([P, TB])
        xs, hid = sb([P, 2, TB]), sb([P, 2, TB])
        V(nc.vector.memset, combT[:], 0.0)
        rows = NT * NH

        def attention(half):
            ready, late, bk, w = [], (), 7 * half, of_half[half]
            qkv, prod, one, s_tok = w["qkv"], w["prod"], w["one"], w["s_tok"]
            sc, sa, sbuf2, cum, cumsq, tau = w["grids"]
            for t in range(NT):
                x = xn[:, half, t * P:(t + 1) * P]
                if half == 0 and t == 0:
                    r = V(tt, xm[:], x, before[:], ALU.mult)
                    x = xm[:]
                else:
                    r = Mark(V)
                E(mm, bank(ps, bk, 3 * D), x, wqkv[:], start=True, stop=False, after=(r, Mark(A)))
                e = E(mm, bank(ps, bk, 3 * D), ones[:], bias[:], start=False, stop=True, own=False)
                A(act, qkv[:, t, 0:D], bank(ps, bk, D), ACT.Copy, scale=ATTN_SCALE1, after=(e, Mark(V), Mark(G)), own=False)
                a = A(nc.scalar.copy, qkv[:, t, D:], ps[:, bk, D:3 * D], own=False)
                q = qkv[:, t, 0:D].rearrange("p (h d) -> p h d", h=NH)
                k = qkv[:, t, D:2 * D].rearrange("p (h d) -> p h d", h=NH)
                pr = prod[t % 2][:].rearrange("p (h g d) -> p h g d", h=NH, g=NH)
                g = G(nc.gpsimd.tensor_tensor, pr, rep(q, 2, NH), rep(k, 1, NH), ALU.mult, after=(a, *ready[-1:]), own=False)
                yield
                if late:
                    ready.append(V(reduce, *late[0], AX, ALU.add, after=late[1:], own=False))
                late = ((sc[:, t], pr), g)
                yield
            yield
            V(reduce, *late[0], AX, ALU.add, after=late[1:], own=False)
            flat = "p t h g -> p (t h g)"
            V(copy, sa[:], sc[:])
            top, other = sort_descending(c, sa[:].rearrange(flat), sbuf2[:].rearrange(flat), NH)
            yield
            r3 = "p (r k) -> p r k"
            top, other = top.rearrange(r3, k=NH), other.rearrange(r3, k=NH)
            z, cm, cs, tu = (x[:].rearrange("p t h g -> p (t h) g") for x in (sc, cum, cumsq, tau))
            V(copy, one[:], top[:, :, 0])
            V(tt, z, z, rep(one[:], 2, NH), ALU.subtract)
            r = V(tt, top, top, rep(one[:], 2, NH), ALU.subtract, own=False)
            a = A(act, other, top, ACT.Square, after=(r,), own=False)
            yield
            fl = "p r k -> p (r k)"
            V(nc.vector.tensor_tensor_scan, cm.rearrange(fl), restart[:], top.rearrange(fl), 0.0, ALU.mult, ALU.add)
            V(nc.vector.tensor_tensor_scan, cs.rearrange(fl), restart[:], other.rearrange(fl), 0.0, ALU.mult, ALU.add,
              after=(a,), own=False)
            yield
            ik = rep(inv_k[:], 1, rows)
            V(tt, tu, cm, ik, ALU.mult)
            V(tt, cm, cm, tu, ALU.mult)
            V(tt, cs, cs, cm, ALU.subtract)
            yield
            V(ts, cs, cs, -1.0, 1.0, ALU.mult, ALU.add)
            V(tt, cs, cs, ik, ALU.mult)
            r = V(ts, cs, cs, 0.0, None, ALU.max)
            a = A(act, cs, cs, ACT.Sqrt, after=(r,), own=False)
            yield
            V(tt, tu, tu, cs, ALU.subtract, after=(a,))
            V(tt, cm, tu, top, ALU.is_le)
            V(reduce, one[:], cm, AX, ALU.add)
            yield
            V(tt, cm, rep(order[:], 1, rows), rep(one[:], 2, NH), ALU.is_equal)
            V(tt, cm, cm, tu, ALU.mult)
            V(reduce, one[:], cm, AX, ALU.add)
            yield
            V(tt, z, z, rep(one[:], 2, NH), ALU.subtract)
            r = V(ts, z, z, 0.0, None, ALU.max)
            a = A(act, z, z, ACT.Square, after=(r,), own=False)
            yield
            ready, late = [], ()

            def gather(t):
                ready.append(V(reduce, s_tok[:, t].rearrange("p (h d) -> p h d", h=NH), late[0], AX, ALU.add,
                               after=late[1:], own=False))
                c.transpose(ps[:, bk, t * P:(t + 1) * P], s_tok[:, t], after=(ready[-1], Mark(A)))

            for t in range(NT):
                v = qkv[:, t, 2 * D:].rearrange("p (g d) -> p d g", g=NH)
                pr = prod[t % 2][:].rearrange("p (h d g) -> p h d g", h=NH, d=HD)
                g = G(nc.gpsimd.tensor_tensor, pr, rep(sc[:, t], 2, HD), rep(v, 1, NH), ALU.mult,
                      after=(a, *ready[-1:]), own=False)
                yield
                if late:
                    gather(t - 1)
                late = (pr, g)
                yield
            yield
            gather(NT - 1)
            A(nc.scalar.copy, s_T[:, half], bank(ps, bk), after=(Mark(E), Mark(V)), own=False)
            yield

        def moe(half):
            x = xn[:, half]
            for t in range(NT):
                e = E(mm, ps[:, 1, t * E1:(t + 1) * E1], x[:, t * P:(t + 1) * P], wr[:], start=True, stop=True, after=(A, V))
            V(copy, lg[:], ps[:, 1, 0:NT * E1].rearrange("p (t e) -> p t e", t=NT), after=(e,))
            r = route(c, lg[:], rb, 2, True)
            yield
            for t in range(NT):
                e = c.transpose(ps[0:E1, 1, t * P:(t + 1) * P], rb["comb"][:, t], after=(r,))
            spread = A(nc.scalar.copy, combT[0:E1, :], ps[0:E1, 1, :], after=(e,), own=False)
            yield
            hidden, downs = [], []
            for s in range(2 * E1 + 1):
                if s < 2 * E1:
                    e, k = s // 2, s % 2
                    b1, b3 = 2 + 2 * (s % 2), 3 + 2 * (s % 2)
                    if k == 0:
                        mk = E(mm, bank(ps, 1), pick[:, e, :], combT[:], start=True, stop=True,
                               after=(spread,), own=False)
                        spread = V(tt, xs[:, e % 2], x, bank(ps, 1), ALU.mult, after=(mk,), own=False)
                    free = hidden[s - 2:s - 1]
                    g = E(mm, bank(ps, b1), w1[:, e, k * P:(k + 1) * P], x, start=True, stop=True, after=free, own=False)
                    u = E(mm, bank(ps, b3), w3[:, e, k * P:(k + 1) * P], xs[:, e % 2], start=True, stop=True,
                          after=(spread,), own=False)
                    a = A(act, hid[:, s % 2], bank(ps, b1), ACT.Silu, after=(g, *downs[s - 2:s - 1]), own=False)
                    hidden.append(V(tt, hid[:, s % 2], hid[:, s % 2], bank(ps, b3), ALU.mult, after=(a, u), own=False))
                if s > 0:
                    e, k = (s - 1) // 2, (s - 1) % 2
                    downs.append(E(mm, bank(ps, 6), w2[:, k, e, :], hid[:, (s - 1) % 2], start=(s == 1),
                                   stop=(s == 2 * E1), after=(hidden[s - 1],), own=False))
                yield
            A(act, out[:, half], bank(ps, 6), ACT.Silu, after=(E,))

        def both_moes():
            for half in range(2):
                yield from moe(half)

        with m.loop("layer1", B) as b:
            xb = c.xT[:, bass.ds(b * T, T)].rearrange("p (h n) -> p h n", h=2)
            woven(m, *((c.layernorm_steps(xb[:, half], xn[:, half], tmp[:, half], 7 * half), 1) for half in range(2)))
            woven(m, (both_moes(), 1), (attention(0), 1), (attention(1), 1))
            V(tt, out[:], out[:], s_T[:], ALU.mult, after=(A,))
            V(tt, xb, xb, out[:], ALU.add)


DI2 = 256
DH2 = DI2 // NH
CH = P
BS = 4
NBL = CH // BS
E2, F2 = 8, 176
NTT = B * T // P


def delta_inputs(c, sb, keep):
    m, nc, ps, d = c.m, c.m.nc, c.ps, c.dram
    V, A, G, E, S = m.V, m.A, m.G, m.E, m.S
    mm, act, tt, ts, stt = (nc.tensor.matmul, nc.scalar.activation, nc.vector.tensor_tensor,
                            nc.vector.tensor_scalar, nc.vector.scalar_tensor_tensor)
    win, ones = sb([P, 800]), sb([1, P])
    b_z, b_x, b_kv, b_g = sb([P, 2]), sb([P, 2]), sb([1, 288]), sb([1, 7 * NH])
    rms_w, taps, conv_b = sb([P, 1]), sb([P, 2, 4]), sb([P, 2])
    gate_w, q_w = sb([P, 2, 7 * NH]), sb([P, 2, DI2])
    for out, name in ((win, "win2"), (b_z, "bz2"), (b_x, "bx2"), (b_kv, "bkv2"), (b_g, "bg2"), (rms_w, "rms2"),
                      (conv_b, "convb2")):
        S.dma(c.q_w, out[:], d[name])
    for out, name in ((taps, "convw2"), (gate_w, "gatew2"), (q_w, "qw2")):
        S.dma(c.q_w, out[:], d[name].rearrange("(k p) n -> p k n", p=P))
    V(nc.vector.memset, ones[:], 1.0)
    V.wait(c.q_w)
    E.wait(c.q_w, V)
    A.wait(c.q_w)
    h, ta = sb([P, TB]), sb([P, TB])
    xn = sb([P, TB])
    xg, zs, xc = sb([P, 2, 3 + TB]), sb([P, 2, TB]), sb([P, 2, TB])
    kq, sq = sb([P, NT, 2, DI2]), sb([P, NT, 2, DI2])
    norm = sb([P, NT, 2 * NH])
    with m.loop("layer2_inputs", B) as b:
        for half in range(T // TB):
            x0, t0 = b * T + half * TB, b * (T // P) + half * NT
            V.wait(m.queues["c"])
            c.layernorm(c.xT[:, bass.ds(x0, TB)], xn[:], ta[:], 0)
            S.dma(m.queues["c"], keep["xn"][:, bass.ds(x0, TB)], xn[:], after=(V,))
            c.inverse_rms(xn[:], ta[:], 0, 1e-6)
            V(stt, h[:], xn[:], rms_w[:], ta[:], ALU.mult, ALU.mult)
            if half == 0:
                V(nc.vector.memset, xg[:, :, 0:3], 0.0)
            else:
                V(nc.vector.tensor_copy, xg[:, :, 0:3], xg[:, :, TB:TB + 3])
            for k in range(4):
                E(mm, bank(ps, k), win[:, k * P:(k + 1) * P], h[:], start=True, stop=True, after=(V, A), own=False)
            for k in range(2):
                A(act, zs[:, k], bank(ps, k), ACT.Silu, bias=b_z[:, k:k + 1], after=(E, m.queues["a"]), own=False)
            for k in range(2):
                A(act, xg[:, k, 3:], bank(ps, 2 + k), ACT.Identity, bias=b_x[:, k:k + 1], after=(V,), own=False)
            S.dma(m.queues["a"], keep["z"][:, :, bass.ds(x0, TB)], zs[:], after=(A,))
            for k in range(2):
                V(ts, xc[:, k], xg[:, k, 0:TB], taps[:, k, 0:1], conv_b[:, k:k + 1], ALU.mult, ALU.add,
                  after=(A, m.queues["b"]))
                for j in range(1, 4):
                    V(stt, xc[:, k], xg[:, k, j:j + TB], taps[:, k, j:j + 1], xc[:, k], ALU.mult, ALU.add)
            A(act, xc[:], xc[:], ACT.Silu, after=(V,))
            S.dma(m.queues["b"], keep["xconv"][:, :, bass.ds(x0, TB)], xc[:], after=(A,))
            copied = [Mark(A), Mark(A)]
            for t in range(NT):
                ct = slice(t * P, (t + 1) * P)
                b0 = (4, 1)[t % 2]
                for out, rows, w_row, w_main in ((bank(ps, b0, 288), (h[:, ct],), b_kv, (win[:, 512:800],)),
                                                 (bank(ps, b0 + 1, 7 * NH), (xc[:, 0, ct], xc[:, 1, ct]), b_g,
                                                  (gate_w[:, 0], gate_w[:, 1])),
                                                 (bank(ps, b0 + 2, DI2), (xc[:, 0, ct], xc[:, 1, ct]), None,
                                                  (q_w[:, 0], q_w[:, 1]))):
                    for k, (r, w) in enumerate(zip(rows, w_main)):
                        E(mm, out, r, w, start=(k == 0), stop=(k == 1 and w_row is None), after=(copied[t],), own=False)
                    if w_row is not None:
                        E(mm, out, ones[:], w_row[:], start=False, stop=True, own=False)
                A(nc.scalar.copy, kq[:, t, 0], bank(ps, b0, DI2), after=(E, V), own=False)
                A(nc.scalar.copy, keep["v"][:, bass.ds(t0 + t, 1)], ps[:, b0:b0 + 1, DI2:288], own=False)
                A(nc.scalar.copy, keep["gates"][:, bass.ds(t0 + t, 1)], ps[:, b0 + 1:b0 + 2, 0:7 * NH], own=False)
                copied.append(A(nc.scalar.copy, kq[:, t, 1], bank(ps, b0 + 2, DI2), own=False))
            A(act, sq[:], kq[:], ACT.Square, own=True)
            V(nc.vector.tensor_reduce, norm[:], sq[:].rearrange("p t k (h d) -> p t (k h) d", d=DH2), AX, ALU.add, after=(A,))
            A(act, norm[:], norm[:], ACT.Sqrt, after=(V,))
            V(ts, norm[:], norm[:], 1e-6, None, ALU.add, after=(A,))
            V(nc.vector.reciprocal, norm[:], norm[:])
            for k, name in enumerate(("k", "q")):
                V(tt, keep[name][:, bass.ds(t0, NT)].rearrange("p t (h d) -> p t h d", d=DH2),
                  kq[:, :, k].rearrange("p t (h d) -> p t h d", d=DH2), rep(norm[:, :, k * NH:(k + 1) * NH], 3, DH2),
                  ALU.mult, own=(k == 0))


def delta_gates(c, sb, keep):
    m, nc, d = c.m, c.m.nc, c.dram
    V, A, S = m.V, m.A, m.S
    act, tt, ts, stt = nc.scalar.activation, nc.vector.tensor_tensor, nc.vector.tensor_scalar, nc.vector.scalar_tensor_tensor
    t_scale, freqs = sb([P, NH]), sb([P, NH])
    S.dma(c.q_w, t_scale[:], d["ldt2"].unsqueeze(0).partition_broadcast(P))
    S.dma(c.q_w, freqs[:], d["c_freqs"])
    A(act, t_scale[:], t_scale[:], ACT.Exp, after=(c.q_w,))
    V.wait(c.q_w, A)
    alpha, omega, sel_b, sel_c, sel_dt, beta, r = (keep["gates"][:, :, j * NH:(j + 1) * NH] for j in range(7))
    decay, o_beta, cos, sin, v0, v1 = (keep["g"][:, j] for j in range(6))
    t1, t2, dt, det = (sb([P, NTT, NH])[:] for _ in range(4))

    def softplus(out, x):
        V(stt, t1, x, -1.0, x, ALU.mult, ALU.max)
        A(act, t1, t1, ACT.Exp, scale=-1.0, after=(V,))
        A(act, t1, t1, ACT.Ln, bias=c.one[:], own=True)
        V(stt, out, x, 0.0, t1, ALU.max, ALU.add, after=(A,))

    softplus(dt, sel_dt)
    V(tt, dt, dt, rep(t_scale[:], 1, NTT), ALU.mult)
    V(ts, dt, dt, 1e-4, 0.5, ALU.add, ALU.mult)
    softplus(t2, alpha)
    V(tt, alpha, t2, dt, ALU.mult)
    A(act, omega, omega, ACT.Tanh, after=(V,))
    A(act, sel_b, sel_b, ACT.Sigmoid)
    A(act, keep["sel_c"][:], sel_c, ACT.Sigmoid)
    A(act, o_beta, beta, ACT.Sigmoid)
    A(act, r, r, ACT.Sigmoid)
    V(ts, omega, omega, 1.0, None, ALU.add, after=(A,))
    V(tt, omega, omega, rep(freqs[:], 1, NTT), ALU.mult)
    V(tt, omega, omega, dt, ALU.mult)
    V(tt, t2, omega, omega, ALU.mult)
    V(ts, det, alpha, 1.0, None, ALU.add)
    V(tt, det, det, det, ALU.mult)
    V(tt, det, det, t2, ALU.add)
    V(nc.vector.reciprocal, det, det)
    V(tt, t1, alpha, alpha, ALU.mult)
    V(tt, t1, t1, t2, ALU.add)
    V(ts, t1, t1, -1.0, 1.0, ALU.mult, ALU.add)
    V(tt, cos, t1, det, ALU.mult)
    V(stt, sin, omega, 2.0, det, ALU.mult, ALU.mult)
    V(tt, t1, cos, cos, ALU.mult)
    V(tt, t2, sin, sin, ALU.mult)
    V(tt, t1, t1, t2, ALU.add)
    V(ts, det, t1, 0.0, None, ALU.is_equal)
    V(ts, t1, t1, 1e-32, None, ALU.max)
    A(act, t1, t1, ACT.Sqrt, after=(V,))
    V(nc.vector.reciprocal, t2, t1, after=(A,))
    V(tt, cos, cos, t2, ALU.mult)
    V(tt, cos, cos, det, ALU.add)
    V(tt, sin, sin, t2, ALU.mult)
    V(ts, t1, t1, 1e-8, 1.0, ALU.max, ALU.min)
    A(act, t1, t1, ACT.Ln, after=(V,))
    V(stt, t1, t1, 8.0, r, ALU.mult, ALU.mult, after=(A,))
    A(act, decay, t1, ACT.Exp, after=(V,))
    V(tt, t1, decay, decay, ALU.mult, after=(A,))
    V(ts, t1, t1, -1.0, 1.0, ALU.mult, ALU.add)
    V(ts, t1, t1, 0.0, 1.0, ALU.max, ALU.min)
    V(ts, t1, t1, 1e-6, None, ALU.add)
    A(act, t1, t1, ACT.Sqrt, after=(V,))
    V(tt, t1, t1, sel_b, ALU.mult, after=(A,))
    vv = keep["v"][:].rearrange("p t (h s) -> p t h s", s=2)
    V(tt, v0, vv[:, :, :, 0], t1, ALU.mult)
    V(tt, v1, vv[:, :, :, 1], t1, ALU.mult, own=False)


def delta_recurrence(c, sb, keep):
    m, nc, ps, d = c.m, c.m.nc, c.ps, c.dram
    V, A, G, E, S = m.V, m.A, m.G, m.E, m.S
    act, tt, ts, stt = nc.scalar.activation, nc.vector.tensor_tensor, nc.vector.tensor_scalar, nc.vector.scalar_tensor_tensor
    gtt, gts, gcopy = nc.gpsimd.tensor_tensor, nc.gpsimd.tensor_scalar, nc.gpsimd.tensor_copy
    kst, qst = sb([P, B, NH, DH2]), sb([P, B, NH, DH2])
    gst = sb([P, 6, 2, B, NH])
    kc, g, turn, turn2 = ([sb(shape) for _ in range(2)] for shape in (
        [P, CH, DH2], [P, 6, CH], [P, 2, CH], [P, 2, CH]))
    qc, tmp = sb([P, CH, DH2]), sb([P, CH, DH2])
    ta, tb, carry = sb([P, 2, CH]), sb([P, 2, CH]), sb([P, 2])
    w, wt, nbm, u, ret = sb([P, CH]), sb([P, 2, CH]), sb([P, CH]), sb([P, CH]), sb([P, CH])
    first, at = sb([P, 1 + NBL, DH2 + 1]), sb([P, NBL, DH2])
    coef, later = sb([P, NBL, BS, BS]), sb([P, NBL, 1 + BS])
    rows, kk, kd = sb([P, NBL, BS, DH2 + 1]), sb([P, NBL, BS]), sb([P, NBL, BS, DH2])
    product, terms = sb([P, BS, DH2 + 1]), sb([P, DH2, 1 + BS])
    H = P // 2
    nt = T // P
    V(nc.vector.memset, first[:, 0, 0:DH2], 0.0)
    V(nc.vector.memset, first[:, :, DH2:], 1.0)
    V(nc.vector.memset, carry[:, 0:1], 1.0)
    V(nc.vector.memset, carry[:, 1:2], 0.0)
    V(nc.vector.memset, later[:, :, BS:], 1.0)
    m.barrier()

    def blocks(x):
        return x.rearrange("p (n l) -> p n l", l=BS)

    def transposed(out, stage, bank0, ready, free):
        freed = [ready, ready]
        for d0 in range(0, DH2, 4):
            bk = bank0 + (d0 // 4) % 2
            for dd in range(4):
                e = E(nc.tensor.transpose, ps[0:H, bk, dd * P:(dd + 1) * P],
                      stage[:, :, :, d0 + dd].rearrange("p b h -> p (b h)"), c.ident[:],
                      after=(ready, freed[-2]) if dd == 0 else (), apart=(dd == 0))
            for half in (slice(0, H), slice(H, P)):
                a = A(nc.scalar.copy, out[half, :, d0:d0 + 4].rearrange("p t d -> p d t"),
                      ps[0:H, bk].rearrange("p (d t) -> p d t", d=4), after=(e, free))
            freed.append(a)
        return freed[-1]

    def prologue(i, n, used, last):
        def tile_of(x):
            return x.rearrange("p (b t) n -> p b t n", b=B)[:, :, bass.ds(i, 1), :].squeeze(2)

        for s in range(2):
            for j in range(6):
                a = A(nc.scalar.copy, gst[:, j, s], tile_of(keep["g"][:, j]), after=last)
        for j in range(6):
            e = c.transpose(ps[:, j // 4, (j % 4) * P:(j % 4 + 1) * P], gst[:, j].rearrange("p s b h -> p (s b h)"),
                            after=(a,))
        a = A(nc.scalar.copy, g[n][:, 0:4].rearrange("p j t -> p (j t)"), bank(ps, 0), after=(e, used))
        a = A(nc.scalar.copy, g[n][:, 4:6].rearrange("p j t -> p (j t)"), bank(ps, 1, 2 * P))
        z = G(gcopy, kst[:].rearrange("p b h d -> p b (h d)"), tile_of(keep["k"][:]), after=last, own=False)
        transposed(kc[n][:], kst, 2, z, used)
        G(gcopy, turn[n][:], g[n][:, 2:4], after=(a, used), own=False)
        x, y = turn[n], turn2[n]
        sh = 1
        while sh < CH:
            G(gcopy, y[:, :, 0:sh], x[:, :, 0:sh])
            G(gtt, ta[:, :, sh:], x[:, :, sh:], rep(x[:, 0, 0:CH - sh], 1, 2), ALU.mult, own=False)
            G(gtt, tb[:, :, sh:], x[:, ::-1, sh:], rep(x[:, 1, 0:CH - sh], 1, 2), ALU.mult, own=False)
            G(gtt, y[:, 0, sh:], ta[:, 0, sh:], tb[:, 0, sh:], ALU.subtract)
            G(gtt, y[:, 1, sh:], ta[:, 1, sh:], tb[:, 1, sh:], ALU.add, own=False)
            x, y = y, x
            sh *= 2
        G(gts, ta[:], x[:], carry[:, 0:1], None, ALU.mult)
        G(gts, tb[:], x[:, ::-1], carry[:, 1:2], None, ALU.mult, own=False)
        G(gtt, x[:, 0], ta[:, 0], tb[:, 0], ALU.subtract)
        G(gtt, x[:, 1], ta[:, 1], tb[:, 1], ALU.add)
        G(gcopy, carry[:], x[:, :, CH - 1])

    def coefficients(n):
        decay, beta = g[n][:, 0], g[n][:, 1]
        dl, kb = blocks(decay), kc[n][:].rearrange("p (n l) d -> p n l d", l=BS)
        for lo, ci, si in ((0, 0, 1), (H, 1, 0)):
            hp = slice(lo, lo + H)
            V(tt, wt[hp, 0], g[n][hp, 4], turn2[n][hp, ci], ALU.mult, own=False)
            V(tt, wt[hp, 1], g[n][hp, 5], turn2[n][hp, si], ALU.mult, own=False)
            V(tt, w[hp], wt[hp, 0], wt[hp, 1], ALU.subtract if lo == 0 else ALU.add)
        V(stt, nbm[:], decay, -1.0, beta, ALU.mult, ALU.mult, own=False)
        V(tt, rows[:, :, :, DH2], blocks(w[:]), blocks(beta), ALU.mult)
        V(nc.vector.tensor_copy, coef[:].rearrange("p n a j -> p n (a j)")[:, :, ::BS + 1], blocks(nbm[:]), own=False)
        V(nc.vector.tensor_copy, later[:, :, BS - 1], dl[:, :, BS - 1], own=False)
        for a in range(BS - 2, -1, -1):
            V(tt, coef[:, :, a, a + 1:], coef[:, :, a + 1, a + 1:], rep(dl[:, :, a], 2, BS - 1 - a), ALU.mult)
            V(tt, later[:, :, a], later[:, :, a + 1], dl[:, :, a], ALU.mult, own=False)
        V(tt, rows[:, :, :, 0:DH2], kb, rep(coef[:, :, 0], 3, DH2), ALU.mult)
        V(tt, kd[:], kb, rep(later[:, :, 1:], 3, DH2), ALU.mult, own=False)
        for l in range(BS - 1):
            k = BS - 1 - l
            pairs = tmp[:, 0:NBL * k].rearrange("p (n l) d -> p n l d", l=k)
            V(tt, pairs, kb[:, :, l + 1:], rep(kb[:, :, l], 2, k), ALU.mult, own=(l > 0))
            V(nc.vector.tensor_reduce, kk[:, :, l + 1:], pairs, AX, ALU.add)
            V(tt, kk[:, :, l + 1:], kk[:, :, l + 1:], coef[:, :, l + 1, l + 1:], ALU.mult)
            for r in (slice(0, DH2), slice(DH2, DH2 + 1)):
                w_ = r.stop - r.start
                p = tmp[:, 0:NBL * k].rearrange("p (n l) d -> p n l d", l=k)[:, :, :, 0:w_]
                V(tt, p, rep(rows[:, :, l, r], 2, k), rep(kk[:, :, l + 1:], 3, w_), ALU.mult)
                V(tt, rows[:, :, l + 1:, r], rows[:, :, l + 1:, r], p, ALU.add)

    def steps(n):
        for b in range(NBL):
            y, uj = first[:, b, 0:DH2], u[:, b * BS:(b + 1) * BS]
            V(tt, product[:], rows[:, b], rep(first[:, b], 1, BS), ALU.mult)
            V(ts, terms[:, :, BS], y, later[:, b, 0:1], None, ALU.mult, own=False)
            V(nc.vector.tensor_reduce, uj, product[:], AX, ALU.add)
            V(tt, terms[:, :, 0:BS], kd[:, b].rearrange("p l d -> p d l"), rep(uj, 1, DH2), ALU.mult)
            V(nc.vector.tensor_reduce, first[:, b + 1, 0:DH2], terms[:], AX, ALU.add)

    def reads(n):
        kb, qb, y = (x.rearrange("p (n l) d -> p n l d", l=BS) for x in (kc[n][:], qc[:], tmp[:]))
        dl, before = blocks(g[n][:, 0]), first[:, 0:NBL, 0:DH2]
        V(tt, y[:, :, 0:BS - 1], kb[:, :, 0:BS - 1], rep(blocks(u[:])[:, :, 0:BS - 1], 3, DH2), ALU.mult)
        for j in range(BS - 1):
            V(tt, at[:], before, rep(dl[:, :, j], 2, DH2), ALU.mult)
            V(tt, y[:, :, j], y[:, :, j], at[:], ALU.add)
            before = y[:, :, j]
        V(tt, y[:, :, 0:BS - 1], y[:, :, 0:BS - 1], qb[:, :, 0:BS - 1], ALU.mult)
        V(tt, y[:, :, BS - 1], first[:, 1:, 0:DH2], qb[:, :, BS - 1], ALU.mult, own=False)
        V(nc.vector.tensor_reduce, ret[:], tmp[:], AX, ALU.add)
        return V(nc.vector.tensor_copy, first[:, 0], first[:, NBL], own=False)

    prologue(0, 0, Mark(V), (Mark(V),))
    m.barrier()
    with m.loop("layer2_recurrence", nt // 2) as i:
        ready = [(Mark(A), Mark(G)), None]
        used = [Mark(V), Mark(V)]
        for n in range(2):
            behind = (Mark(E), Mark(A))
            z = G(gcopy, qst[:].rearrange("p b h d -> p b (h d)"),
                  keep["q"][:].rearrange("p (b t) n -> p b t n", b=B)[:, :, bass.ds(i * 2 + n, 1), :].squeeze(2),
                  after=behind, own=False)
            queries = transposed(qc[:], qst, 4, z, used[1 - n])
            prologue((i * 2 + n + 1) % nt, 1 - n, used[1 - n], (Mark(E), Mark(A)))
            ready[1 - n] = (Mark(A), Mark(G))
            V.wait(*ready[n])
            coefficients(n)
            steps(n)
            V.wait(queries)
            read = used[n] = reads(n)
            c.transpose(ps[:, 6, 0:P], ret[:], after=(read, Mark(A)))
            for k in range(2):
                e = c.transpose(ps[:, 6, (1 + k) * P:(2 + k) * P], turn2[n][:, k])
            out = bass.ds(i * 2 + n, 1)
            A(nc.scalar.copy, keep["tok"][:, out].rearrange("p o x -> p (o x)"), ps[:, 6, 0:P], after=(e,))
            for k in range(2):
                a = A(nc.scalar.copy, keep["cs"][:, k, out].rearrange("p o x -> p (o x)"), ps[:, 6, (1 + k) * P:(1 + k) * P + H])
            used[n] = Mark(V)
            turned = a
            V.wait(turned)


def delta_reads(c, sb, keep):
    m, nc, ps = c.m, c.m.nc, c.ps
    V, A, G, E = m.V, m.A, m.G, m.E
    tt = nc.vector.tensor_tensor
    nt = T // P
    rt, ro = sb([P, 2, nt, B, NH]), sb([P, nt, B, NH, 2])
    stage = sb([P, B, NH, 2])
    tok = keep["tok"][:].rearrange("p i (s b h) -> p s i b h", s=2, b=B)
    co, si = (keep["cs"][:, k].rearrange("p i (b h) -> p i b h", b=B) for k in range(2))
    sel = keep["sel_c"][:].rearrange("p (b i) h -> p i b h", b=B)
    re, im = tok[:, 0], tok[:, 1]
    for s, (x, y, op) in enumerate((((re, co), (im, si), ALU.add), ((im, co), (re, si), ALU.subtract))):
        for b in range(B):
            V(tt, rt[:, 0, :, b], x[0][:, :, b], x[1][:, :, b], ALU.mult, own=(b == 0))
            V(tt, rt[:, 1, :, b], y[0][:, :, b], y[1][:, :, b], ALU.mult, own=False)
        V(tt, rt[:, 0], rt[:, 0], rt[:, 1], op)
        for b in range(B):
            V(tt, ro[:, :, b, :, s], rt[:, 0, :, b], sel[:, :, b], ALU.mult, own=(b == 0))
    m.barrier()
    for i in range(nt):
        for b in range(B):
            e = c.transpose(ps[0:2 * NH, i % 2, b * P:(b + 1) * P], ro[:, i, b].rearrange("p h s -> p (h s)"),
                            after=(A,) if b == 0 else ())
        A(nc.scalar.copy, keep["ret"][:, :, i * P:(i + 1) * P], ps[0:2 * NH, i % 2].rearrange("p (b t) -> p b t", b=B), after=(e,))


def delta_outputs(c, sb, keep):
    m, nc, ps, d = c.m, c.m.nc, c.ps, c.dram
    V, A, G, E, S = m.V, m.A, m.G, m.E, m.S
    mm, act, tt, ts, stt = (nc.tensor.matmul, nc.scalar.activation, nc.vector.tensor_tensor,
                            nc.vector.tensor_scalar, nc.vector.scalar_tensor_tensor)
    copy = nc.vector.tensor_copy
    F = (P, F2 - P)
    read_w, group, out_w = sb([2 * NH, DI2]), sb([P, P]), sb([P, 2, D])
    gn_w, gn_b, dp = sb([P, 2]), sb([P, 2]), sb([P, 2])
    wr, ebias, pick = sb([P, E2]), sb([P, E2]), sb([P, E2, P])
    up, down = sb([P, E2, F2], BF16), sb([P, 2, E2, D], BF16)
    sup, sdown = sb([P, F2]), sb([P, 2, D])
    of_half = [(route_buffers(sb, E2), sb([P, NT, E2]), sb([P, TB]), sb([P, TB], BF16), sb([P, 2, TB], BF16),
                sb([P, TB], BF16), sb([P, 2, TB]), sb([P, TB]), sb([P, TB]), sb([P, TB])) for _ in range(2)]
    for out, name in ((read_w, "readw2"), (group, "c_group"), (gn_w, "gnw2"), (gn_b, "gnb2"), (dp, "dp2"), (wr, "wr2"),
                      (sup, "sup2")):
        S.dma(c.q_w, out[:], d[name])
    for w in of_half:
        S.dma(c.q_w, w[0]["lower"], d["c_lower"])
    V(nc.vector.memset, pick[:], 0.0)
    S.dma(c.q_w, pick[0:E2], d["c_pick"], after=(V,))
    S.dma(c.q_w, out_w[:], d["outw2"].rearrange("(k p) n -> p k n", p=P))
    S.dma(c.q_w, ebias[:], d["eb2"].unsqueeze(0).partition_broadcast(P))
    S.dma(c.q_w, sdown[0:F[0], 0], d["sdown2"][0:P, :])
    S.dma(c.q_w, sdown[0:F[1], 1], d["sdown2"][P:F2, :])
    with m.scope() as tmp:
        f_up, f_down = tmp([P, E2, F2]), tmp([P, 2, E2, D])
        S.dma(c.q_w, f_up[:], d["up2"])
        S.dma(c.q_w, f_down[0:F[0], 0], d["down2"][0:P])
        S.dma(c.q_w, f_down[0:F[1], 1], d["down2"][P:F2])
        V(copy, up[:], f_up[:], after=(c.q_w,))
        V(copy, down[0:F[0], 0], f_down[0:F[0], 0])
        V(copy, down[0:F[1], 1], f_down[0:F[1], 1])
    zx = sb([P, 2, 2, T])
    y = sb([P, 2, T])
    sq = sb([P, TB])
    sums, stat, ab = sb([P, 2, 2]), sb([P, 2, 2]), sb([P, 2, 2])
    xn_all = sb([P, T])
    for w in of_half:
        V(nc.vector.memset, w[2][:], 0.0)
    m.barrier()

    def experts(half, b):
        xn, w, b0 = xn_all[:, half * TB:(half + 1) * TB], of_half[half], 4 * half
        rb, lg, combT, xs, hid, rounded, hs, acc, s_T, tmp_ = w
        hs_ = slice(half * TB, half * TB + TB)
        for k in range(2):
            E(mm, bank(ps, b0), out_w[:, k], y[:, k, hs_], start=(k == 0), stop=(k == 1), after=(V, A))
        for t in range(NT):
            E(mm, ps[:, b0 + 1, t * E2:(t + 1) * E2], xn[:, t * P:(t + 1) * P], wr[:], start=True, stop=True,
              after=(m.queues["c"], A))
        yield
        V(tt, s_T[:], xn, bank(ps, b0), ALU.add, after=(E, m.queues["c"]))
        A(act, rb["score"], ps[:, b0 + 1, 0:NT * E2].rearrange("p (t e) -> p t e", t=NT), ACT.Sigmoid, after=(E, V))
        yield
        V(tt, lg[:], rb["score"], rep(ebias[:], 1, NT), ALU.add, after=(A,))
        route(c, lg[:], rb, 2, False)
        yield
        for t in range(NT):
            c.transpose(ps[0:E2, b0 + 1, t * P:(t + 1) * P], rb["comb"][:, t], after=(V,))
        A(nc.scalar.copy, combT[0:E2], ps[0:E2, b0 + 1, :], after=(E,))
        for k in range(2):
            e = E(mm, ps[0:F[k], b0 + 2 + k, :], sup[:, k * P:k * P + F[k]], xn, start=True, stop=True)
            A(act, hs[0:F[k], k], ps[0:F[k], b0 + 2 + k, :], ACT.Relu, after=(e, V))
        yield
        for k in range(2):
            V(tt, hs[0:F[k], k], hs[0:F[k], k], hs[0:F[k], k], ALU.mult, after=(A,), own=False)
        up_next = E(mm, bank(ps, b0 + 1), pick[:, 0, :], combT[:], start=True, stop=True, after=(A,))
        yield
        for k in range(2):
            e = E(mm, bank(ps, b0), sdown[0:F[k], k], hs[0:F[k], k], start=(k == 0), stop=(k == 1), after=(V,))
        V(tt, xs[:], xn, bank(ps, b0 + 1), ALU.mult, after=(up_next,), own=False)
        scaled = Mark(V)
        taken = V(copy, acc[:], bank(ps, b0), after=(e,))
        yield
        free = [Mark(A)]
        for x in range(E2):
            for k in range(2):
                e = E(mm, ps[0:F[k], b0 + 2 + k, :], up[:, x, k * P:k * P + F[k]], xs[:], start=True, stop=True,
                      after=(scaled, free[-1]))
                A(act, hid[0:F[k], k], ps[0:F[k], b0 + 2 + k, :], ACT.Relu, after=(e,))
            free.append(Mark(A))
            yield
            if x + 1 < E2:
                up_next = E(mm, bank(ps, b0 + 1), pick[:, x + 1, :], combT[:], start=True, stop=True, after=(scaled,))
            for k in range(2):
                V(tt, hid[0:F[k], k], hid[0:F[k], k], hid[0:F[k], k], ALU.mult, after=(free[-1],), own=False)
            squared = Mark(V)
            if x + 1 < E2:
                scaled = V(tt, xs[:], xn, bank(ps, b0 + 1), ALU.mult, after=(up_next,), own=False)
            yield
            for k in range(2):
                e = E(mm, bank(ps, b0), down[0:F[k], k, x], hid[0:F[k], k], start=(k == 0), stop=(k == 1),
                      after=(squared, taken))
            taken = A(nc.scalar.copy, rounded[:], bank(ps, b0), after=(e, V))
            yield
            V(tt, acc[:], acc[:], rounded[:], ALU.add, after=(taken,))
        c.update(c.xT[:, bass.ds(b * T + half * TB, TB)], s_T[:], acc[:], tmp_[:])

    with m.loop("layer2_outputs", B) as b:
        S.dma(m.queues["a"], zx[:, 0], keep["z"][:, :, bass.ds(b * T, T)], after=(V,))
        S.dma(m.queues["b"], zx[:, 1], keep["xconv"][:, :, bass.ds(b * T, T)])
        S.dma(m.queues["c"], xn_all[:], keep["xn"][:, bass.ds(b * T, T)], after=(E,))
        for k in range(2):
            for half in range(2):
                bk = 2 * k + half
                E(mm, bank(ps, bk), read_w[:, k * P:(k + 1) * P],
                  keep["ret"][:, bass.ds(b, 1), half * TB:half * TB + TB].squeeze(1),
                  start=True, stop=True, after=(A, V), own=False, apart=True)
                A(act, y[:, k, half * TB:half * TB + TB], bank(ps, bk), ACT.Copy, accum_out=sums[:, k, half:half + 1],
                  after=(E, V), own=False)
        V(tt, stat[:, 0], sums[:, :, 0], sums[:, :, 1], ALU.add, after=(A,))
        E(mm, ps[:, 4, 0:2], group[:], stat[:, 0], start=True, stop=True, after=(V,))
        V(ts, ab[:, 1], ps[:, 4, 0:2], -1.0, None, ALU.mult, after=(E,))
        for k in range(2):
            for half in range(2):
                A(act, sq[:], y[:, k, half * TB:half * TB + TB], ACT.Square, bias=ab[:, 1, k:k + 1],
                  accum_out=sums[:, k, half:half + 1], after=(V,), own=True)
        V(tt, stat[:, 1], sums[:, :, 0], sums[:, :, 1], ALU.add, after=(A,))
        E(mm, ps[:, 4, 0:2], group[:], stat[:, 1], start=True, stop=True, after=(V,))
        A(act, stat[:, 0], ps[:, 4, 0:2], ACT.Sqrt, bias=c.eps[1e-5][:], after=(E,))
        V(nc.vector.reciprocal, stat[:, 0], stat[:, 0], after=(A,))
        V(tt, ab[:, 0], stat[:, 0], gn_w[:], ALU.mult)
        V(tt, stat[:, 1], ab[:, 1], ab[:, 0], ALU.mult)
        V(tt, stat[:, 1], stat[:, 1], gn_b[:], ALU.add)
        for k in range(2):
            V(ts, y[:, k], y[:, k], ab[:, 0, k:k + 1], stat[:, 1, k:k + 1], ALU.mult, ALU.add)
            V(tt, y[:, k], y[:, k], zx[:, 0, k], ALU.mult, after=(m.queues["a"],))
            V(stt, y[:, k], zx[:, 1, k], dp[:, k:k + 1], y[:, k], ALU.mult, ALU.add, after=(m.queues["b"],))
        woven(m, (experts(0, b), 1), (experts(1, b), 1))


def layer2(c):
    m, nc = c.m, c.m.nc
    with m.scope() as sb:
        keep = {"ret": sb([2 * NH, B, T]),
                "xn": nc.dram_tensor("xn_scratch", (P, B * T), F32, kind="Internal").ap(),
                "z": nc.dram_tensor("z_scratch", (P, 2, B * T), F32, kind="Internal").ap(),
                "xconv": nc.dram_tensor("xconv_scratch", (P, 2, B * T), F32, kind="Internal").ap()}
        with m.scope() as tmp:
            keep.update(k=tmp([P, NTT, DI2]), q=tmp([P, NTT, DI2]), g=tmp([P, 6, NTT, NH]), sel_c=tmp([P, NTT, NH]))
            with m.scope() as tmp2:
                keep.update(v=tmp2([P, NTT, 2 * NH]), gates=tmp2([P, NTT, 7 * NH]))
                with m.scope() as inner:
                    delta_inputs(c, inner, keep)
                with m.scope() as inner:
                    delta_gates(c, inner, keep)
            keep.update(tok=tmp([P, T // P, P]), cs=tmp([P, 2, T // P, P // 2]))
            with m.scope() as inner:
                delta_recurrence(c, inner, keep)
            with m.scope() as inner:
                delta_reads(c, inner, keep)
        with m.scope() as inner:
            delta_outputs(c, inner, keep)


PAD = 32
JG = P // PAD
NG = NH // JG
REL = 256
QW = REL + P
NI = T // P
F3 = 384
PARTS = ((1, 1), (1, 2), (2, 1), (2, 2), (1, 3), (3, 1))
KP = P // 2
KR = len(PARTS) * HD


def relative_attention(c, sb, keep):
    m, nc, ps, d = c.m, c.m.nc, c.ps, c.dram
    V, A, G, E, S = m.V, m.A, m.G, m.E, m.S
    mm, act, tt, ts, stt = (nc.tensor.matmul, nc.scalar.activation, nc.vector.tensor_tensor,
                            nc.vector.tensor_scalar, nc.vector.scalar_tensor_tensor)
    gtt = nc.gpsimd.tensor_tensor
    scale = HD ** -0.5
    R = 4
    scratch = nc.dram_tensor("relative_scratch", (R, JG, P, QW), F32, kind="Internal").ap()

    def shifted(r):
        return bass.AP(tensor=scratch.tensor, offset=r * JG * P * QW + P, ap=[[QW - 1, P], [P * QW, JG], [1, REL]])

    wq, wk, wv, rel = sb([P, 2, P]), sb([P, 2, P]), sb([P, JG * HD]), sb([P, 2, REL])
    row0 = sb([P, 2])
    within, other, neg, ident_b, less, head = (sb([P, P]), sb([P, P]), sb([P, P], BF16), sb([P, P], BF16),
                                                  sb([P, 4]), sb([P, 2]))
    x = sb([P, T])
    q, k, rel_b, v = ([sb(*shape) for _ in range(2)] for shape in (
        ([P, JG, 1 + T], BF16), ([P, 2, T], BF16), ([P, 2, REL], BF16), ([P, NI, JG, PAD],)))
    q2, part, rest = sb([P, TB], BF16), sb([P, TB], BF16), sb([P, TB])
    rows = [sb([P, JG, QW]) for _ in range(R)]
    cs = [sb([P, JG, REL]) for _ in range(R)]
    far, two = ([sb([P, JG, P]) for _ in range(R)] for _ in range(2))
    NS = 6
    s = [sb([P, T]) for _ in range(NS)]
    pt = [sb([P, NI, P]) for _ in range(JG)]
    mx, nmax = sb([P, NS, 6]), sb([P, NS, 1])
    out_T, inv = sb([P, P]), sb([P, JG])
    q_in = m.queues["a"]
    q_out, q_back = ([m.queues[f"{n}{r}"] for r in range(R)] for n in ("rel_out", "rel_back"))
    S.dma(c.q_w, within[:], d["c_within"])
    S.dma(c.q_w, less[:], d["c_less"])
    S.dma(c.q_w, head[:], d["c_head"])
    V(ts, neg[:], within[:], -1e9, None, ALU.mult, after=(c.q_w,))
    V(ts, other[:], c.ident[:], -1.0, 1.0, ALU.mult, ALU.add)
    for n in range(2):
        V(nc.vector.memset, q[n][:, :, 0:1], 0.0)
        V(nc.vector.memset, v[n][:], 0.0)
        V(nc.vector.memset, v[n][:, :, :, HD:HD + 1], 1.0)
    V(nc.vector.tensor_copy, ident_b[:], c.ident[:])
    m.barrier()

    def stack(out, src, which, made):
        n = src.shape[1]
        p, r = part[:, 0:n], rest[:, 0:n]
        a = A(nc.scalar.copy, p, src, after=(made, Mark(V)))
        yield
        e = V(stt, r, p, less[:, 2 * which:2 * which + 1], src, ALU.mult, ALU.add, after=(a,))
        yield
        a = A(nc.scalar.copy, p, r, after=(e,))
        yield
        V(stt, out, p, less[:, 2 * which + 1:2 * which + 2], r, ALU.mult, ALU.add, after=(a, Mark(E)))

    def prepare(n, b, g):
        for out, name in ((wq, "wq3"), (wk, "wk3"), (wv, "wv3"), (rel, "rel3")):
            S.dma(q_in, out[:], d[name][bass.ds(g, 1)].squeeze(0), after=(Mark(E), Mark(V), Mark(A)))
        for half in range(2):
            a = A(nc.scalar.copy, x[:, half * TB:(half + 1) * TB], keep["xn"][:, bass.ds(b * T + half * TB, TB)],
                  after=(Mark(E),))
            yield
        V.wait(a)
        V(ts, wq[:], wq[:], scale, None, ALU.mult, after=(q_in,))
        V(nc.vector.tensor_copy, row0[:], rel[:, :, 0])
        V(tt, rel[:], rel[:], rep(row0[:], 2, REL), ALU.subtract)
        V(ts, rel[:, :, 0], row0[:], -1.0, None, ALU.mult)
        yield
        loaded, freed = Mark(V), [Mark(V)]
        for p in range(2):
            yield from stack(rel_b[n][:, p], rel[:, p], 1, Mark(V))
            yield
        for p in range(2):
            for half in range(2):
                h = slice(half * TB, half * TB + TB)
                for which, w, out in ((0, wq, q2[:]), (1, wk, k[n][:, p, h])):
                    e = E(mm, bank(ps, 6), w[:, p], x[:, h], start=True, stop=True, after=(loaded, *freed[-1:]))
                    yield
                    yield from stack(out, bank(ps, 6), which, e)
                    freed.append(Mark(V))
                    if which == 0:
                        for jj in range(2):
                            V(ts, q[n][:, 2 * p + jj, 1 + half * TB:1 + half * TB + TB], q2[:], head[:, jj:jj + 1], None,
                              ALU.mult, own=(jj == 0))
                    yield
        for t in range(NI):
            e = E(mm, ps[:, 6, t * JG * HD:(t + 1) * JG * HD], x[:, t * P:(t + 1) * P], wv[:], start=True, stop=True,
                  after=(freed[-1],) if t == 0 else ())
            if t == NI // 2:
                yield
        yield
        A(nc.scalar.copy, v[n][:, :, :, 0:HD], bank(ps, 6, NI * JG * HD).rearrange("p (t j d) -> p t j d", t=NI, j=JG),
          after=(e,))
        yield

    def relative(quad, made, gone, evac):
        r, i, n = quad % R, quad % NI, quad // NI % 2
        for p in range(2):
            for jj in range(2):
                e = E(mm, ps[:, 7, jj * REL:(jj + 1) * REL], q[n][:, 2 * p + jj, i * P:(i + 1) * P], rel_b[n][:, p],
                      start=True, stop=True, after=(made, evac[-1]) if jj == 0 else ())
            a = A(nc.scalar.copy, rows[r][:, 2 * p:2 * p + 2, 0:REL], ps[:, 7].rearrange("p (j z) -> p j z", j=2),
                  after=(e, q_out[r]))
            evac.append(a)
        e = G(nc.gpsimd.tensor_copy, rows[r][:, :, REL:QW], rows[r][:, :, 0:P], after=(a,), own=False)
        S.dma(q_out[r], scratch[r].rearrange("j p z -> p j z"), rows[r][:], after=(e, a, q_back[r]))
        z = S.dma(q_back[r], cs[r][:], shifted(r), after=(q_out[r], gone, Mark(G)))
        if i >= 2:
            z = G(gtt, two[r][:], cs[r][:, :, P:], rep(other[:], 1, JG), ALU.mult, after=(z, gone), own=False)
        if i >= 4:
            z = G(gtt, far[r][:], cs[r][:, :, P:], rep(within[:], 1, JG), ALU.mult, own=False)
        return z

    for _ in prepare(0, 0, 0):
        pass
    for quad in range(2):
        relative(quad, Mark(V), Mark(V), [Mark(A)])
    m.barrier()
    with m.loop("layer3_attention", B, NG // 2) as (b, gg):
        start = tuple(Mark(x) for x in (E, V, A, G))
        V.wait(*q_back[0:2], G)
        biased = {0: start[1], 1: start[1]}
        quad_done = {}
        scored, done, expd, turned, moved = [], [], [], [], []
        evac = [start[2]]

        def scores(u):
            quad, j = divmod(u, JG)
            i, set_ = quad % NI, quad // NI
            n = (i + 1) * P
            b0 = 2 * (u % 2)
            free = (*expd[u - 2:u - 1], *done[u - 2:u - 1]) if u >= 2 else start
            for lo in range(0, n, TB):
                hi = min(n, lo + TB)
                E(mm, ps[:, b0 + lo // TB, 0:hi - lo], q[set_][:, j, 1 + i * P:1 + (i + 1) * P], k[set_][:, j // 2, lo:hi],
                  start=True, stop=hi < n, after=free)
            scored.append(E(mm, ps[:, b0 + i // 4, (i % 4) * P:(i % 4 + 1) * P], ident_b[:], neg[:], start=False, stop=True))

        def weights(u):
            quad, j = divmod(u, JG)
            i, r, n, b0 = quad % NI, quad % R, u % NS, 2 * (u % 2)
            out, sc = s[n], ps[:, b0:b0 + 2, :].rearrange("p b n -> p (b n)")
            V.wait(scored[u], biased[quad], *(turned[u - NS:u - NS + 1] if u >= NS else start))
            parts = [(i - 1, i + 1, cs[r][:, j, :]) if i else (0, 1, cs[r][:, j, P:])]
            if i >= 2:
                parts.append((i - 2, i - 1, two[r][:, j]))
            if i >= 3:
                parts.append((i - 3, i - 2, cs[r][:, j, 0:P]))
            if i >= 4:
                parts.append((i - 4, i - 3, far[r][:, j]))
            for lo, hi, bias in parts:
                V(tt, out[:, lo * P:hi * P], sc[:, lo * P:hi * P], bias, ALU.add, own=False)
            first = max(0, i - 4) * P
            if first:
                V(nc.vector.tensor_reduce, mx[:, n, 1:2], sc[:, 0:first], AX, ALU.max, own=False)
            V(nc.vector.tensor_reduce, mx[:, n, 0:1], out[:, first:(i + 1) * P], AX, ALU.max)
            done.append(V(nc.vector.tensor_reduce, nmax[:, n], mx[:, n, 0:2 if first else 1], AX, ALU.max, negate=True))
            if j == JG - 1:
                quad_done[quad] = done[-1]
            if first:
                A(act, out[:, 0:first], sc[:, 0:first], ACT.Exp, bias=nmax[:, n], after=(done[u],))
            expd.append(A(act, out[:, first:(i + 1) * P], out[:, first:(i + 1) * P], ACT.Exp, bias=nmax[:, n],
                          after=(done[u],)))

        chunks = [start[2], start[2]]

        def turn(u):
            quad, j = divmod(u, JG)
            i = quad % NI
            src, dst = s[u % NS], pt[j]
            for lo in range(0, i + 1, 4):
                hi = min(i + 1, lo + 4)
                bk = 4 + len(chunks) % 2
                for t in range(lo, hi):
                    e = c.transpose(ps[:, bk, (t - lo) * P:(t - lo + 1) * P], src[:, t * P:(t + 1) * P],
                                    after=(expd[u], chunks[-2]) if t == lo else ())
                chunks.append(A(nc.scalar.copy, dst[:, lo:hi].rearrange("p t n -> p (t n)"), bank(ps, bk, (hi - lo) * P),
                                after=(e, *moved[-1:])))
            turned.append(e)

        def values(quad):
            i, set_ = quad % NI, quad // NI
            last = chunks[-1]
            for t in range(i + 1):
                for j in range(JG):
                    e = E(mm, ps[j * PAD:(j + 1) * PAD, 7, 0:P], v[set_][:, t, j], pt[j][:, t, :], start=(t == 0),
                          stop=(t == i), after=(last, evac[-1]) if t == j == 0 else ())
            moved.append(e)
            yield
            a = A(nc.scalar.copy, out_T[:], ps[:, 7, 0:P], after=(e,))
            e = c.transpose(ps[:, 7, P:2 * P], out_T[:], after=(a,))
            yield
            got = ps[:, 7, P:2 * P].rearrange("p (j n) -> p j n", j=JG)
            V(nc.vector.reciprocal, inv[:], got[:, :, HD], after=(e,))
            to = keep["att"][:, bass.ds(b * NI + i, 1), bass.ds((gg * 2 + set_) * JG * HD, JG * HD)].squeeze(1)
            evac.append(V(tt, to.rearrange("p (j d) -> p j d", j=JG), got[:, :, 0:HD], rep(inv[:], 2, HD), ALU.mult))
            yield

        n_units, quads = 2 * JG * NI, 2 * NI
        nexts = {1: prepare(1, b, gg * 2 + 1), JG * NI + 5: prepare(0, (b + gg) % B, 2 - gg * 2)}
        making, valued = None, None
        operands = [start[1], None]
        for u in range(n_units + 7):
            making = nexts.get(u, making)
            if u % JG == 2 and u // JG + 2 < quads:
                quad = u // JG + 2
                if quad == NI:
                    for _ in making:
                        pass
                    operands[1] = Mark(V)
                biased[quad] = relative(quad, operands[quad // NI], quad_done.get(quad - R, start[1]), evac)
            if u < n_units:
                scores(u)
            if u % JG == 3 and 7 <= u:
                valued = values(u // JG - 1)
                next(valued)
            elif u % JG == 0 and valued:
                next(valued)
            elif u % JG == 1 and valued:
                next(valued)
            if 1 <= u <= n_units:
                weights(u - 1)
            for _ in range(2):
                next(making, None) if making else None
            if 3 <= u < n_units + 3:
                turn(u - 3)
        for _ in making:
            pass
        for quad in range(2):
            relative(2 * NI + quad, Mark(V), quad_done[2 * NI + quad - R], evac)


def layer3(c):
    m, nc, ps, d = c.m, c.m.nc, c.ps, c.dram
    V, A, G, E, S = m.V, m.A, m.G, m.E, m.S
    mm, act, tt, ts = nc.tensor.matmul, nc.scalar.activation, nc.vector.tensor_tensor, nc.vector.tensor_scalar
    with m.scope() as sb:
        keep = {"xn": sb([P, B * T]), "att": sb([P, NTT, D])}
        with m.scope() as tmp:
            xn, ta = tmp([P, 2, TB]), tmp([P, 2, TB])
            with m.loop("layer3_norm", B) as b:
                x, out = (a[:, bass.ds(b * T, T)].rearrange("p (h n) -> p h n", h=2) for a in (c.xT, keep["xn"]))
                woven(m, *((c.layernorm_steps(x[:, half], xn[:, half], ta[:, half], half), 1) for half in range(2)))
                V(nc.vector.tensor_copy, out, xn[:])
        with m.scope() as tmp:
            relative_attention(c, tmp, keep)
        wp, bp = sb([P, D]), sb([P, 1])
        wg, wu, wd = sb([P, F3]), sb([P, F3]), sb([P, F3 // P, D])
        with m.scope() as tmp:
            ints = tmp([P, 3, F3], I32)
            S.dma(c.q_w, wp[:], d["wp3"])
            S.dma(c.q_w, bp[:], d["bp3"])
            S.dma(c.q_w, ints[:, 0], d["gate3"])
            S.dma(c.q_w, ints[:, 1], d["up3"])
            S.dma(c.q_w, ints[:, 2].rearrange("p (k n) -> p k n", k=3), d["down3"].rearrange("(k p) n -> p k n", p=P))
            for k, w in enumerate((wg[:], wu[:], wd[:].rearrange("p k n -> p (k n)"))):
                V(ts, w, ints[:, k], 1.0 / 127.0, None, ALU.mult, after=(c.q_w,))
        of_half = [(sb([P, NT, D]), sb([P, TB]), sb([P, TB]), sb([P, TB]), sb([P, 3, TB]), sb([P, TB])) for _ in range(2)]

        def block(half, b):
            att, aT, sT, xn, hid, tmp_ = of_half[half]
            b0, n = 4 * half, b * 2 + half
            V(nc.vector.tensor_copy, att[:], keep["att"][:, bass.ds(n * NT, NT)], after=(E,))
            A(nc.scalar.copy, xn[:], keep["xn"][:, bass.ds(n * TB, TB)], after=(E,))
            yield
            for t in range(NT):
                e = c.transpose(ps[:, b0, t * P:(t + 1) * P], att[:, t], after=(V, A))
            A(nc.scalar.copy, aT[:], bank(ps, b0), after=(e,))
            yield
            for k in range(3):
                g = E(mm, bank(ps, b0 + 2), wg[:, k * P:(k + 1) * P], xn[:], start=True, stop=True, after=(V, A))
                u = E(mm, bank(ps, b0 + 3), wu[:, k * P:(k + 1) * P], xn[:], start=True, stop=True)
                A(act, hid[:, k], bank(ps, b0 + 2), ACT.Silu, after=(g, V))
                yield
                if k == 0:
                    e = E(mm, bank(ps, b0 + 1), wp[:], aT[:], start=True, stop=True, after=(A,))
                V(tt, hid[:, k], hid[:, k], bank(ps, b0 + 3), ALU.mult, after=(A, u), own=False)
                if k == 0:
                    V(ts, sT[:], bank(ps, b0 + 1), bp[:], None, ALU.add, after=(e,), own=False)
                yield
            for k in range(3):
                E(mm, bank(ps, b0), wd[:, k], hid[:, k], start=(k == 0), stop=(k == 2), after=(V, A))
            yield
            c.update(c.xT[:, bass.ds(n * TB, TB)], sT[:], bank(ps, b0), tmp_[:])

        with m.loop("layer3_ffn", B) as b:
            woven(m, (block(0, b), 1), (block(1, b), 1))


LAYERS = (0, 1, 2, 3)


def program(nc, dram, out, per_iteration):
    m = Machine(nc, per_iteration)
    c = Common(m, dram)
    c.load_start()
    for k in LAYERS:
        (layer0, layer1, layer2, layer3)[k](c)
    m.barrier()
    m.S.dma(m.queues["out"], out, c.xT[:], after=(m.V,))
    m.S.wait(m.queues["out"])
    m.barrier()
    return m.learned


def constants():
    inv = (1.0 / 10000.0 ** (np.arange(0, 8, 2, dtype=np.float32) / 8)).astype(np.float32)
    f = np.arange(T, dtype=np.float32)[:, None] * inv[None, :]
    cos, sin = np.cos(f).T, np.sin(f).T
    i = np.arange(P)
    out = {
        "c_ident": np.eye(P),
        "c_upper": i[:, None] <= i[None, :],
        "c_cos": np.tile(cos, (32, 1)),
        "c_sin": np.tile(np.concatenate([-sin, sin]), (16, 1)),
        "c_blocks": i[:, None] // HD == i[None, :] // HD,
        "c_before": i[:, None] < i[None, :],
        "c_order": np.tile(np.arange(1, NH + 1), (P, 1)),
        "c_inv_k": np.tile(1.0 / np.arange(1, NH + 1), (P, 1)),
        "c_restart": np.tile(np.arange(NT * NH * NH) % NH != 0, (P, 1)),
        "c_pick": np.repeat(np.eye(E1)[:, :, None], P, 2),
        "c_freqs": np.tile(1.0 / 10000.0 ** (np.arange(NH, dtype=np.float32) / NH), (P, 1)),
        "c_group": (i[:, None] // DH2 == i[None, :] // DH2) / (DH2 * T),
        "c_within": i[None, :] > i[:, None],
        "c_head": i[:, None] // KP == np.arange(2)[None, :],
        "c_lower": np.tile(np.arange(E1)[None, :] < np.arange(E1)[:, None], (P, 1, 1)),
    }
    less = np.zeros((2, KP, 4))
    for n, (pq, pk) in enumerate(PARTS):
        less[:, n * HD:(n + 1) * HD] = [-(pq > 1), -(pq > 2), -(pk > 1), -(pk > 2)]
    out["c_less"] = less.reshape(P, 4)
    return {k: np.ascontiguousarray(v, dtype=np.float32) for k, v in out.items()}


def laid_out(i):
    def columns(v):
        return v.reshape(-1, P).T

    def stacked(w, axis):
        w = np.moveaxis(w, axis, 0).reshape(NG, 2, 2, HD, -1)
        out = np.zeros((NG, 2, 2, KP, w.shape[-1]), w.dtype)
        out[:, :, :, :KR] = np.tile(w, (1, 1, 1, len(PARTS), 1))
        return out.reshape(NG, 2, P, -1)

    partner = np.arange(D).reshape(16, 2, 4)[:, ::-1].reshape(-1)
    wq, zx = i["L0_attn_W_in"][:D], i["L0_attn_W_zxbcdt"]
    a = {
        "xT": i["L0_attn_x"].reshape(B * T, D).T,
        "wq": wq.T, "wqr": wq[partner].T,
        "wz": zx[:DI0].T, "wxbc": zx[DI0:DI0 + 2 * DI0].T, "wdt": zx[3 * DI0:].T,
        "convw0": i["L0_attn_conv_w"].T, "convb0": columns(i["L0_attn_conv_b"]), "dtb": i["L0_attn_dt_bias"],
        "alog": i["L0_attn_A_log"], "D0": columns(np.repeat(i["L0_attn_D_param"], HP)), "npre": columns(i["L0_attn_norm_pre_w"]),
        "ngat": columns(i["L0_attn_norm_gated_w"]), "wout0": i["L0_attn_W_out"].T,
        "fg0": i["L0_ffn_w_gate"], "fu0": i["L0_ffn_w_up"], "fd0": i["L0_ffn_w_down"],
    }
    a.update({
        "wqkv1": np.concatenate([np.tile(i["L1_attn_W" + k].T, (NH, NH)) for k in "qkv"], 1),
        "bqkv1": np.concatenate([np.tile(i["L1_attn_b" + k], NH) for k in "qkv"])[None, :],
        "wr1": i["L1_ffn_router_w"], "w1": i["L1_ffn_w1"], "w3": i["L1_ffn_w3"], "w2": i["L1_ffn_w2"],
    })
    a.update({
        "win2": i["L2_attn_in_proj_w"], "bz2": columns(i["L2_attn_in_proj_b"][:DI2]),
        "bx2": columns(i["L2_attn_in_proj_b"][DI2:2 * DI2]), "bkv2": i["L2_attn_in_proj_b"][None, 2 * DI2:],
        "bg2": i["L2_attn_gate_b"][None, :], "rms2": columns(i["L2_attn_rms_w"]), "convw2": i["L2_attn_conv_w"],
        "convb2": columns(i["L2_attn_conv_b"]), "gatew2": i["L2_attn_gate_w"], "qw2": i["L2_attn_Q_w"],
        "ldt2": i["L2_attn_log_dt_scale"], "readw2": i["L2_attn_readout_w"], "gnw2": columns(i["L2_attn_gn_w"]),
        "gnb2": columns(i["L2_attn_gn_b"]), "dp2": columns(i["L2_attn_D_param"]), "outw2": i["L2_attn_out_w"],
        "wr2": i["L2_ffn_gate_w"].T, "eb2": i["L2_ffn_expert_bias"],
        "up2": i["L2_ffn_w_up"].transpose(2, 0, 1), "down2": i["L2_ffn_w_down"].transpose(2, 0, 1),
        "sup2": i["L2_ffn_shared_w_up"].T, "sdown2": i["L2_ffn_shared_w_down"].T,
    })
    a.update({
        "wq3": stacked(i["L3_attn_Wq"], 0).transpose(0, 3, 1, 2), "wk3": stacked(i["L3_attn_Wk"], 0).transpose(0, 3, 1, 2),
        "wv3": i["L3_attn_Wv"].reshape(NG, JG * HD, D).transpose(0, 2, 1), "rel3": stacked(i["L3_attn_rel_embed"], 1).transpose(0, 2, 1, 3),
        "wp3": i["L3_attn_Wp"].T, "bp3": columns(i["L3_attn_bp"]),
        "gate3": i["L3_ffn_w_gate"].T, "up3": i["L3_ffn_w_up"].T, "down3": i["L3_ffn_w_down"].T,
    })
    return {k: np.ascontiguousarray(v) for k, v in a.items()}


def kernel(**inputs):
    import concourse.bacc as bacc
    from concourse.bass_utils import run_bass_kernel_spmd as run

    arrays = {**laid_out({k: np.asarray(v) for k, v in inputs.items()}), **constants()}

    def build(per_iteration):
        nc = bacc.Bacc("TRN2", target_bir_lowering=False, num_devices=1)
        dram = {k: nc.dram_tensor("in_" + k, v.shape, mybir.dt.from_np(v.dtype), kind="ExternalInput").ap()
                for k, v in arrays.items()}
        out = nc.dram_tensor("out", (D, B * T), F32, kind="ExternalOutput").ap()
        return nc, program(nc, dram, out, per_iteration)

    _, per_iteration = build({})
    nc, _ = build(per_iteration)
    r = run(nc, [{"in_" + k: v for k, v in arrays.items()}], core_ids=[0])
    return np.ascontiguousarray(r.results[0]["out"].T).reshape(B, T, D)
```
